# Optimizing a Trainium2 kernel written in Bass

```python
import numpy as np
import jax
import jax.numpy as jnp

def _softmax(x, axis=-1):
    return jax.nn.softmax(x, axis=axis)

def _gelu(x):
    return jax.nn.gelu(x, approximate=True)

def _silu(x):
    return jax.nn.silu(x)

def _sigmoid(x):
    return jax.nn.sigmoid(x)

def _layernorm(x, axis=-1, eps=1e-05):
    m = jnp.mean(x, axis=axis, keepdims=True)
    v = jnp.var(x, axis=axis, keepdims=True)
    return (x - m) / jnp.sqrt(v + eps)

def _scatter_add(tgt, idx, src, axis=0):
    return tgt.at[idx].add(src)

def _segment_sum(src, seg, n):
    return jax.ops.segment_sum(src, seg, n)
kernel_name = 'mk_macaron_d2_jaxref_r8_ff987a'

def setup_inputs(seed: int=0):
    np.random.seed(seed)
    _w = jnp.asarray

    def _L0_attn_setup():
        import jax, jax.numpy as jnp
        import numpy as np
        DIM = 128
        B, S = (4, 512)
        key = jax.random.key(seed)
        ks = jax.random.split(key, 7)
        s = 1.0 / np.sqrt(DIM)
        return {'x': jax.random.normal(ks[0], (B, S, DIM), dtype=jnp.float32), 'wq': jax.random.uniform(ks[1], (DIM, DIM), minval=-s, maxval=s, dtype=jnp.float32), 'bq': jax.random.uniform(ks[2], (DIM,), minval=-s, maxval=s, dtype=jnp.float32), 'wk': jax.random.uniform(ks[3], (DIM, DIM), minval=-s, maxval=s, dtype=jnp.float32), 'bk': jax.random.uniform(ks[4], (DIM,), minval=-s, maxval=s, dtype=jnp.float32), 'wv': jax.random.uniform(ks[5], (DIM, DIM), minval=-s, maxval=s, dtype=jnp.float32), 'bv': jax.random.uniform(ks[6], (DIM,), minval=-s, maxval=s, dtype=jnp.float32)}
    _L0_attn_in = _L0_attn_setup()

    def _L0_ffn_setup():
        import jax, jax.numpy as jnp
        import numpy as np
        B, S, H, E = (4, 256, 128, 8)
        key = jax.random.key(seed)
        k1, k2, k3 = jax.random.split(key, 3)
        scale_w = 1.0 / np.sqrt(H)
        return {'x': jax.random.normal(k1, (B, S, H), dtype=jnp.float32), 'router_w': jax.random.normal(k2, (H, E), dtype=jnp.float32) * scale_w, 'router_b': jnp.zeros((E,), dtype=jnp.float32), 'expert_w': jax.random.normal(k3, (E, H, H), dtype=jnp.float32) * scale_w, 'expert_b': jnp.zeros((E, H), dtype=jnp.float32)}
    _L0_ffn_in = _L0_ffn_setup()

    def _L1_attn_setup():
        import jax, jax.numpy as jnp
        import numpy as np
        B, T, D = (4, 256, 128)
        H, Kd = (4, 32)
        Vd = 64
        KEY_DIM, VAL_DIM = (H * Kd, H * Vd)
        CONV = 4
        EPS = 1e-06
        LN_EPS = 1e-05

        def _layernorm(x, g, b):
            m = jnp.mean(x, -1, keepdims=True)
            v = jnp.mean((x - m) ** 2, -1, keepdims=True)
            return (x - m) * jax.lax.rsqrt(v + LN_EPS) * g + b

        def _rmsnorm(x, w):
            return x * jax.lax.rsqrt(jnp.mean(x * x, -1, keepdims=True) + EPS) * w

        def _l2norm(x):
            return x * jax.lax.rsqrt(jnp.sum(x * x, -1, keepdims=True) + EPS)

        def _causal_conv_silu(x, w):
            t = x.shape[1]
            xp = jnp.pad(x, ((0, 0), (CONV - 1, 0), (0, 0)))
            y = xp[:, 0:t, :] * w[:, 0]
            for i in range(1, CONV):
                y = y + xp[:, i:i + t, :] * w[:, i]
            return jax.nn.silu(y)

        def _gated_delta_rule(q, k, v, g, beta):
            qT = jnp.moveaxis(q, 1, 0)
            kT = jnp.moveaxis(k, 1, 0)
            vT = jnp.moveaxis(v, 1, 0)
            gT = jnp.moveaxis(g, 1, 0)
            bT = jnp.moveaxis(beta, 1, 0)
            S0 = jnp.zeros((q.shape[0], H, Kd, Vd), q.dtype)

            def step(S, inp):
                q_t, k_t, v_t, g_t, b_t = inp
                S = S * jnp.exp(g_t)[..., None, None]
                kv = jnp.einsum('bhk,bhkv->bhv', k_t, S)
                delta = (v_t - kv) * b_t[..., None]
                S = S + k_t[..., :, None] * delta[..., None, :]
                o = jnp.einsum('bhk,bhkv->bhv', q_t, S)
                return (S, o)
            _, o = jax.lax.scan(step, S0, (qT, kT, vT, gT, bT))
            return jnp.moveaxis(o, 0, 1)

        def _forward(x, ln1_g, ln1_b, ln2_g, ln2_b, rms_in_w, Wq, Wk, Wv, conv_q_w, conv_k_w, conv_v_w, Wa, dt_bias, A_log, Wb, Wg, o_norm_w, Wo, W2, b2):
            b, t, _ = x.shape
            h = _layernorm(x, ln1_g, ln1_b)
            h = _rmsnorm(h, rms_in_w)
            q = _causal_conv_silu(h @ Wq, conv_q_w).reshape(b, t, H, Kd)
            k = _causal_conv_silu(h @ Wk, conv_k_w).reshape(b, t, H, Kd)
            v = _causal_conv_silu(h @ Wv, conv_v_w).reshape(b, t, H, Vd)
            q = _l2norm(q) * Kd ** (-0.5)
            k = _l2norm(k)
            g = -jnp.exp(A_log) * jax.nn.softplus(h @ Wa + dt_bias)
            beta = jax.nn.sigmoid(h @ Wb)
            o = _gated_delta_rule(q, k, v, g, beta)
            gate = (h @ Wg).reshape(b, t, H, Vd)
            o = _rmsnorm(o, o_norm_w) * jax.nn.silu(gate)
            enc = o.reshape(b, t, VAL_DIM) @ Wo
            x = x + enc
            h2 = _layernorm(x, ln2_g, ln2_b)
            x_out = jax.nn.gelu(h2 @ W2 + b2, approximate=False) + x
            return x_out
        key = jax.random.key(seed)
        ks = jax.random.split(key, 16)
        r = lambda k, shp, s=0.02: jax.random.normal(k, shp, dtype=jnp.float32) * s
        return {'x': jax.random.normal(ks[0], (B, T, D), dtype=jnp.float32), 'ln1_g': jnp.ones((D,), jnp.float32), 'ln1_b': jnp.zeros((D,), jnp.float32), 'ln2_g': jnp.ones((D,), jnp.float32), 'ln2_b': jnp.zeros((D,), jnp.float32), 'rms_in_w': jnp.ones((D,), jnp.float32), 'Wq': r(ks[1], (D, KEY_DIM)), 'Wk': r(ks[2], (D, KEY_DIM)), 'Wv': r(ks[3], (D, VAL_DIM)), 'conv_q_w': r(ks[4], (KEY_DIM, CONV), 0.3), 'conv_k_w': r(ks[5], (KEY_DIM, CONV), 0.3), 'conv_v_w': r(ks[6], (VAL_DIM, CONV), 0.3), 'Wa': r(ks[7], (D, H)), 'dt_bias': r(ks[8], (H,), 0.5), 'A_log': jnp.log(jax.random.uniform(ks[9], (H,), minval=1.0, maxval=16.0)), 'Wb': r(ks[10], (D, H)), 'Wg': r(ks[11], (D, VAL_DIM)), 'o_norm_w': jnp.ones((Vd,), jnp.float32), 'Wo': r(ks[12], (VAL_DIM, D)), 'W2': r(ks[13], (D, D)), 'b2': jnp.zeros((D,), jnp.float32)}
    _L1_attn_in = _L1_attn_setup()

    def _L1_ffn_setup():
        import jax, jax.numpy as jnp
        import numpy as np
        B, S, H, F, E, K = (4, 256, 128, 512, 8, 2)
        key = jax.random.key(seed)
        ks = jax.random.split(key, 4)
        sc = lambda d: 1.0 / np.sqrt(d)
        return {'x': jax.random.normal(ks[0], (B, S, H), jnp.float32), 'gate_w': jax.random.normal(ks[1], (H, E), jnp.float32) * sc(H), 'gate_b': jnp.zeros((E,), jnp.float32), 'w1': jax.random.normal(ks[2], (E, H, F), jnp.float32) * sc(H), 'b1': jnp.zeros((E, F), jnp.float32), 'w2': jax.random.normal(ks[3], (E, F, H), jnp.float32) * sc(F), 'b2': jnp.zeros((E, H), jnp.float32)}
    _L1_ffn_in = _L1_ffn_setup()
    _d = {'L0_attn_x': _L0_attn_in['x'], 'L0_attn_wq': _L0_attn_in['wq'], 'L0_attn_bq': _L0_attn_in['bq'], 'L0_attn_wk': _L0_attn_in['wk'], 'L0_attn_bk': _L0_attn_in['bk'], 'L0_attn_wv': _L0_attn_in['wv'], 'L0_attn_bv': _L0_attn_in['bv'], 'L0_ffn_router_w': _L0_ffn_in['router_w'], 'L0_ffn_router_b': _L0_ffn_in['router_b'], 'L0_ffn_expert_w': _L0_ffn_in['expert_w'], 'L0_ffn_expert_b': _L0_ffn_in['expert_b'], 'L1_attn_ln1_g': _L1_attn_in['ln1_g'], 'L1_attn_ln1_b': _L1_attn_in['ln1_b'], 'L1_attn_ln2_g': _L1_attn_in['ln2_g'], 'L1_attn_ln2_b': _L1_attn_in['ln2_b'], 'L1_attn_rms_in_w': _L1_attn_in['rms_in_w'], 'L1_attn_Wq': _L1_attn_in['Wq'], 'L1_attn_Wk': _L1_attn_in['Wk'], 'L1_attn_Wv': _L1_attn_in['Wv'], 'L1_attn_conv_q_w': _L1_attn_in['conv_q_w'], 'L1_attn_conv_k_w': _L1_attn_in['conv_k_w'], 'L1_attn_conv_v_w': _L1_attn_in['conv_v_w'], 'L1_attn_Wa': _L1_attn_in['Wa'], 'L1_attn_dt_bias': _L1_attn_in['dt_bias'], 'L1_attn_A_log': _L1_attn_in['A_log'], 'L1_attn_Wb': _L1_attn_in['Wb'], 'L1_attn_Wg': _L1_attn_in['Wg'], 'L1_attn_o_norm_w': _L1_attn_in['o_norm_w'], 'L1_attn_Wo': _L1_attn_in['Wo'], 'L1_attn_W2': _L1_attn_in['W2'], 'L1_attn_b2': _L1_attn_in['b2'], 'L1_ffn_gate_w': _L1_ffn_in['gate_w'], 'L1_ffn_gate_b': _L1_ffn_in['gate_b'], 'L1_ffn_w1': _L1_ffn_in['w1'], 'L1_ffn_b1': _L1_ffn_in['b1'], 'L1_ffn_w2': _L1_ffn_in['w2'], 'L1_ffn_b2': _L1_ffn_in['b2']}
    _x0 = _d['L0_attn_x']
    _d['L0_attn_x'] = jax.random.normal(jax.random.fold_in(jax.random.key(seed), 1), (2, 2048, 128), dtype=_x0.dtype)
    del _x0
    return _d

def reference(L0_attn_x, L0_attn_wq, L0_attn_bq, L0_attn_wk, L0_attn_bk, L0_attn_wv, L0_attn_bv, L0_ffn_router_w, L0_ffn_router_b, L0_ffn_expert_w, L0_ffn_expert_b, L1_attn_ln1_g, L1_attn_ln1_b, L1_attn_ln2_g, L1_attn_ln2_b, L1_attn_rms_in_w, L1_attn_Wq, L1_attn_Wk, L1_attn_Wv, L1_attn_conv_q_w, L1_attn_conv_k_w, L1_attn_conv_v_w, L1_attn_Wa, L1_attn_dt_bias, L1_attn_A_log, L1_attn_Wb, L1_attn_Wg, L1_attn_o_norm_w, L1_attn_Wo, L1_attn_W2, L1_attn_b2, L1_ffn_gate_w, L1_ffn_gate_b, L1_ffn_w1, L1_ffn_b1, L1_ffn_w2, L1_ffn_b2):

    def _L0_attn_ref(x, wq, bq, wk, bk, wv, bv):
        import jax, jax.numpy as jnp
        import numpy as np
        DIM = 128
        B, S = (4, 512)
        scale = x.shape[-1] ** (-0.5)
        q = x @ wq.T + bq
        k = x @ wk.T + bk
        v = x @ wv.T + bv
        scores = jnp.einsum('bqd,bkd->bqk', q, k) * scale
        attn = jax.nn.softmax(scores, axis=-1)
        return jnp.einsum('bqk,bkd->bqd', attn, v)

    def _L0_ffn_ref(x, router_w, router_b, expert_w, expert_b):
        import jax, jax.numpy as jnp
        import numpy as np
        B, S, H, E = (4, 256, 128, 8)
        b, s, h = x.shape
        xt = x.reshape(b * s, h)
        logits = xt @ router_w + router_b
        probs = jax.nn.softmax(logits, axis=-1)
        gate = jnp.max(probs, axis=-1)
        idx = jnp.argmax(probs, axis=-1)
        out_all = jnp.einsum('th,ehd->ted', xt, expert_w) + expert_b[None, :, :]
        e_out = jnp.take_along_axis(out_all, idx[:, None, None], axis=1)[:, 0, :]
        y = gate[:, None] * e_out
        return y.reshape(b, s, h)

    def _L1_attn_ref(x, ln1_g, ln1_b, ln2_g, ln2_b, rms_in_w, Wq, Wk, Wv, conv_q_w, conv_k_w, conv_v_w, Wa, dt_bias, A_log, Wb, Wg, o_norm_w, Wo, W2, b2):
        import jax, jax.numpy as jnp
        import numpy as np
        B, T, D = (4, 256, 128)
        H, Kd = (4, 32)
        Vd = 64
        KEY_DIM, VAL_DIM = (H * Kd, H * Vd)
        CONV = 4
        EPS = 1e-06
        LN_EPS = 1e-05

        def _layernorm(x, g, b):
            m = jnp.mean(x, -1, keepdims=True)
            v = jnp.mean((x - m) ** 2, -1, keepdims=True)
            return (x - m) * jax.lax.rsqrt(v + LN_EPS) * g + b

        def _rmsnorm(x, w):
            return x * jax.lax.rsqrt(jnp.mean(x * x, -1, keepdims=True) + EPS) * w

        def _l2norm(x):
            return x * jax.lax.rsqrt(jnp.sum(x * x, -1, keepdims=True) + EPS)

        def _causal_conv_silu(x, w):
            t = x.shape[1]
            xp = jnp.pad(x, ((0, 0), (CONV - 1, 0), (0, 0)))
            y = xp[:, 0:t, :] * w[:, 0]
            for i in range(1, CONV):
                y = y + xp[:, i:i + t, :] * w[:, i]
            return jax.nn.silu(y)

        def _gated_delta_rule(q, k, v, g, beta):
            qT = jnp.moveaxis(q, 1, 0)
            kT = jnp.moveaxis(k, 1, 0)
            vT = jnp.moveaxis(v, 1, 0)
            gT = jnp.moveaxis(g, 1, 0)
            bT = jnp.moveaxis(beta, 1, 0)
            S0 = jnp.zeros((q.shape[0], H, Kd, Vd), q.dtype)

            def step(S, inp):
                q_t, k_t, v_t, g_t, b_t = inp
                S = S * jnp.exp(g_t)[..., None, None]
                kv = jnp.einsum('bhk,bhkv->bhv', k_t, S)
                delta = (v_t - kv) * b_t[..., None]
                S = S + k_t[..., :, None] * delta[..., None, :]
                o = jnp.einsum('bhk,bhkv->bhv', q_t, S)
                return (S, o)
            _, o = jax.lax.scan(step, S0, (qT, kT, vT, gT, bT))
            return jnp.moveaxis(o, 0, 1)

        def _forward(x, ln1_g, ln1_b, ln2_g, ln2_b, rms_in_w, Wq, Wk, Wv, conv_q_w, conv_k_w, conv_v_w, Wa, dt_bias, A_log, Wb, Wg, o_norm_w, Wo, W2, b2):
            b, t, _ = x.shape
            h = _layernorm(x, ln1_g, ln1_b)
            h = _rmsnorm(h, rms_in_w)
            q = _causal_conv_silu(h @ Wq, conv_q_w).reshape(b, t, H, Kd)
            k = _causal_conv_silu(h @ Wk, conv_k_w).reshape(b, t, H, Kd)
            v = _causal_conv_silu(h @ Wv, conv_v_w).reshape(b, t, H, Vd)
            q = _l2norm(q) * Kd ** (-0.5)
            k = _l2norm(k)
            g = -jnp.exp(A_log) * jax.nn.softplus(h @ Wa + dt_bias)
            beta = jax.nn.sigmoid(h @ Wb)
            o = _gated_delta_rule(q, k, v, g, beta)
            gate = (h @ Wg).reshape(b, t, H, Vd)
            o = _rmsnorm(o, o_norm_w) * jax.nn.silu(gate)
            enc = o.reshape(b, t, VAL_DIM) @ Wo
            x = x + enc
            h2 = _layernorm(x, ln2_g, ln2_b)
            x_out = jax.nn.gelu(h2 @ W2 + b2, approximate=False) + x
            return x_out
        return _forward(x, ln1_g, ln1_b, ln2_g, ln2_b, rms_in_w, Wq, Wk, Wv, conv_q_w, conv_k_w, conv_v_w, Wa, dt_bias, A_log, Wb, Wg, o_norm_w, Wo, W2, b2)

    def _L1_ffn_ref(x, gate_w, gate_b, w1, b1, w2, b2):
        import jax, jax.numpy as jnp
        import numpy as np
        B, S, H, F, E, K = (4, 256, 128, 512, 8, 2)
        Bb, Ss, Hh = x.shape
        xf = x.reshape(-1, Hh)
        gate = jax.nn.softmax(xf @ gate_w + gate_b)
        topv, topi = jax.lax.top_k(gate, K)
        topv = topv / topv.sum(-1, keepdims=True)
        combine = (jax.nn.one_hot(topi, gate.shape[-1], dtype=xf.dtype) * topv[..., None]).sum(1)

        def body(acc, p):
            w1e, b1e, w2e, b2e, ce = p
            h = jax.nn.relu(xf @ w1e + b1e)
            y = h @ w2e + b2e
            return (acc + y * ce[:, None], None)
        acc0 = jnp.zeros_like(xf)
        out, _ = jax.lax.scan(body, acc0, (w1, b1, w2, b2, combine.T))
        return out.reshape(Bb, Ss, Hh)
    x = L0_attn_x
    x = x + 0.5 * _L0_ffn_ref(_layernorm(x, axis=-1), L0_ffn_router_w, L0_ffn_router_b, L0_ffn_expert_w, L0_ffn_expert_b)
    x = x + _L0_attn_ref(_layernorm(x, axis=-1), L0_attn_wq, L0_attn_bq, L0_attn_wk, L0_attn_bk, L0_attn_wv, L0_attn_bv)
    x = x + 0.5 * _L0_ffn_ref(_layernorm(x, axis=-1), L0_ffn_router_w, L0_ffn_router_b, L0_ffn_expert_w, L0_ffn_expert_b)
    x = x + 0.5 * _L1_ffn_ref(_layernorm(x, axis=-1), L1_ffn_gate_w, L1_ffn_gate_b, L1_ffn_w1, L1_ffn_b1, L1_ffn_w2, L1_ffn_b2)
    x = x + _L1_attn_ref(_layernorm(x, axis=-1), L1_attn_ln1_g, L1_attn_ln1_b, L1_attn_ln2_g, L1_attn_ln2_b, L1_attn_rms_in_w, L1_attn_Wq, L1_attn_Wk, L1_attn_Wv, L1_attn_conv_q_w, L1_attn_conv_k_w, L1_attn_conv_v_w, L1_attn_Wa, L1_attn_dt_bias, L1_attn_A_log, L1_attn_Wb, L1_attn_Wg, L1_attn_o_norm_w, L1_attn_Wo, L1_attn_W2, L1_attn_b2)
    x = x + 0.5 * _L1_ffn_ref(_layernorm(x, axis=-1), L1_ffn_gate_w, L1_ffn_gate_b, L1_ffn_w1, L1_ffn_b1, L1_ffn_w2, L1_ffn_b2)
    return x

_drawn_inputs = setup_inputs


def setup_inputs(seed=0):
    import zlib

    import numpy as np

    out = dict(_drawn_inputs(seed))
    spreads = {'L0_ffn_router_b': (0.0, 0.1),
     'L0_ffn_expert_b': (0.0, 0.1),
     'L1_attn_ln1_g': (1.0, 0.6),
     'L1_attn_ln1_b': (0.0, 0.8),
     'L1_attn_ln2_g': (1.0, 0.6),
     'L1_attn_ln2_b': (0.0, 0.724),
     'L1_attn_rms_in_w': (1.0, 0.6),
     'L1_attn_o_norm_w': (1.0, 0.6),
     'L1_attn_b2': (0.0, 0.334),
     'L1_ffn_gate_b': (0.0, 0.1),
     'L1_ffn_b1': (0.0, 0.1),
     'L1_ffn_b2': (0.0, 0.1)}
    factors = {'L0_attn_bq': 4.089,
     'L0_attn_bk': 64.0,
     'L1_attn_Wq': 4.0,
     'L1_attn_Wk': 4.089,
     'L1_attn_Wv': 3.945,
     'L1_attn_conv_q_w': 4.062,
     'L1_attn_conv_k_w': 3.865,
     'L1_attn_conv_v_w': 3.814,
     'L1_attn_Wa': 8.0,
     'L1_attn_dt_bias': 8.0,
     'L1_attn_A_log': 8.0,
     'L1_attn_Wb': 8.0,
     'L1_attn_Wg': 3.87,
     'L1_attn_Wo': 3.861}
    for name, (base, spread) in spreads.items():
        noise = np.random.default_rng([zlib.crc32(name.encode()), seed]).standard_normal(out[name].shape)
        drawn = base * np.exp(spread * noise) if base else spread * noise
        out[name] = jnp.asarray(drawn.astype(out[name].dtype))
    for name, factor in factors.items():
        out[name] = (out[name] * factor).astype(out[name].dtype)
    return out
```

```python
import concourse.bass as bass
from concourse import mybir
from contextlib import ExitStack

F32 = mybir.dt.float32
F32R = mybir.dt.float32r
ALU = mybir.AluOpType
ACT = mybir.ActivationFunctionType
AX = mybir.AxisListType

P = 128
B, S, D = 2, 2048, 128
TILES = B * S // P
GT = 4
GROUPS = TILES // GT
GW = GT * P
E = 8
F = 512
FC = F // P
LN_EPS = 1e-5


def wait_alone(eng, passed, sem, value):
    eng.wait_ge(sem, value)
    eng.sem_inc(passed, 1)


class Semaphores:

    def __init__(self, ctx, nc, name):
        self.nc, self.name, self.held, self.stack = nc, name, [], ExitStack()
        ctx.callback(self.clear)

    def __call__(self, name):
        self.held.append(self.stack.enter_context(self.nc.semaphore(f"{self.name}_{name}")))
        return self.held[-1]

    def clear(self):
        with self.nc.Block() as block:
            @block.gpsimd
            def _(pool):
                numbers = sorted(s.num for s in self.held)
                while numbers:
                    n = 1
                    while n < len(numbers) and numbers[n] == numbers[0] + n:
                        n += 1
                    pool.sem_clear(range(numbers[0], numbers[0] + n))
                    numbers = numbers[n:]
        self.stack.close()


class Chain:

    def __init__(self, eng, sem, passed=None):
        self.eng, self.sem, self.base, self.n, self.outer = eng, sem, 0, 0, []
        self.passed = passed

    def turn(self, i, per):
        self.outer.append((self.base, self.n, per))
        self.base, self.n = self.base + self.n + i * per, 0

    def leave(self, count):
        base, n, per = self.outer.pop()
        assert self.n == per, ("links in a pass", self.n, per)
        self.base, self.n = base, n + count * per

    def mark(self, ins):
        ins.then_inc(self.sem, 1)
        self.n += 1
        return self.base + self.n

    def link(self, ins):
        self.eng.wait_ge(self.sem, self.mark(ins))

    def link_alone(self, ins):
        wait_alone(self.eng, self.passed, self.sem, self.mark(ins))


class Front:

    def __init__(self, ctx, sem, nc, name, X, ident, neg_half, banks, psum, passed):
        self.passed = passed
        self.nc, self.X, self.ident, self.neg_half = nc, X, ident, neg_half
        self.banks, self.psum = banks, psum
        sb = lambda n, s, dt=F32: ctx.enter_context(nc.sbuf_tensor(f"{name}_{n}", s, dt))
        self.stats = sb("stats", [P, GT, 6])
        self.mv = sb("mean_var", [P, GT, 2])
        self.veps = sb("var_eps", [P, GT])
        self.rstd = sb("rstd", [P, GT])
        self.xn = sb("xn", [P, GT, D])
        self.var_ready = sem("var_ready")
        self.veps_ready = sem("veps_ready")
        self.rstd_ready = sem("rstd_ready")
        self.xn_ready = sem("xn_ready")
        self.xt_ready = sem("xt_ready")
        self.high_ready = sem("high_ready")
        self.low_ready = sem("low_ready")

    def rows(self, g):
        return self.X[:, bass.ts(g, GT), :]

    def vector_stats(self, dve, chain, g):
        nc, x = self.nc, self.rows(g)
        for t in range(GT):
            ins = nc.vector.bn_stats(self.stats[:, t, :], x[:, t, :])
        chain.link_alone(ins)
        for t in range(GT):
            ins = nc.vector.bn_aggr(self.mv[:, t, :], self.stats[:, t, :])
        ins.then_inc(self.var_ready, 1)

    def gpsimd_rstd(self, pool, g):
        nc = self.nc
        wait_alone(pool, self.passed, self.var_ready, g + 1)
        nc.gpsimd.tensor_scalar(self.veps[:], self.mv[:, :, 1], LN_EPS, None, ALU.add)\
            .then_inc(self.veps_ready, 1)
        wait_alone(pool, self.passed, self.veps_ready, g + 1)
        nc.gpsimd.tensor_tensor(self.rstd[:], self.veps[:], self.neg_half[:], ALU.pow)\
            .then_inc(self.rstd_ready, 1)

    def vector_normalize(self, dve, g, first=False):
        nc, x = self.nc, self.rows(g)
        dve.wait_ge(self.rstd_ready, g + 1)
        if not first:
            dve.wait_ge(self.xt_ready, g)
        for t in range(GT):
            ins = nc.vector.tensor_scalar(self.xn[:, t, :], x[:, t, :], self.mv[:, t, 0:1],
                                          self.rstd[:, t:t + 1], ALU.subtract, ALU.mult)
        ins.then_inc(self.xn_ready, 1)

    def tensor_transpose(self, pe, g, par):
        pe.wait_ge(self.xn_ready, g + 1)
        for t in range(GT):
            ins = self.nc.tensor.transpose(self.psum[:, self.banks[par], t * P:(t + 1) * P],
                                           self.xn[:, t, :], self.ident[:])
        ins.then_inc(self.xt_ready, 1)

    def scalar_high(self, act, g, par, high):
        act.wait_ge(self.xt_ready, g + 1)
        self.nc.scalar.activation(high, self.psum[:, self.banks[par], :], ACT.Copy)\
            .then_inc(self.high_ready, 1)

    def vector_low(self, dve, g, par, high, low):
        dve.wait_ge(self.high_ready, g + 1)
        self.nc.vector.tensor_tensor(low, self.psum[:, self.banks[par], :], high.bitcast(F32),
                                     ALU.subtract).then_inc(self.low_ready, 1)


def three_products(pe_nc, out, left, right, start=True, stop=True, skip=False):
    (lh, ll), (rh, rl) = left, right
    for n, (a, b) in enumerate(((lh, rh), (lh, rl), (ll, rh))):
        ins = pe_nc.tensor.matmul(out, a, b, start=(start and n == 0), stop=(stop and n == 2),
                                  skip_group_check=skip)
    return ins


def first_mixture(nc, name, X, ident, neg_half, psum, W, first_wait):
    with ExitStack() as ctx:
        sb = lambda n, s, dt=F32: ctx.enter_context(nc.sbuf_tensor(f"{name}_{n}", s, dt))
        sem = Semaphores(ctx, nc, name)
        fr = Front(ctx, sem, nc, name, X, ident, neg_half, (0, 1), psum, W.passed)
        xh, xl = sb("xh", [P, 2, GW], F32R), sb("xl", [P, 2, GW], F32R)
        lg, ex, eq = sb("logits", [P, GT, E]), sb("exps", [P, GT, E]), sb("eq", [P, GT, E])
        top, tot, gate, pick = (sb(n, [P, GT]) for n in ("top", "total", "gate", "pick"))
        coef = sb("coef", [P, 2, GT, E])
        coefT = sb("coefT", [E, GW])
        LOGITS, CT, OUT = 2, 3, (4, 6)
        dve_chain = sem("dve_chain")
        logits_ready, shifted_ready, exp_ready = sem("logits_ready"), sem("shifted_ready"), sem("exp_ready")
        coef_ready, ct_ready, coefT_ready = sem("coef_ready"), sem("ct_ready"), sem("coefT_ready")
        bias_ready, bias_used = sem("bias_ready"), sem("bias_used")
        experts_ready, experts_used = sem("experts_ready"), sem("experts_used")

        def bc(ap):
            return ap.unsqueeze(2).to_broadcast([P, GT, E])

        def vector_route(dve, chain, g, par):
            dve.wait_ge(logits_ready, g + 1)
            chain.link(nc.vector.tensor_tensor(
                lg[:], psum[:, LOGITS, 0:GT * E].rearrange("p (t e) -> p t e", e=E),
                W.rb[:].unsqueeze(1).to_broadcast([P, GT, E]), ALU.add))
            chain.link(nc.vector.tensor_reduce(top[:], lg[:], AX.X, ALU.max))
            nc.vector.tensor_tensor(ex[:], lg[:], bc(top[:]), ALU.subtract).then_inc(shifted_ready, 1)
            chain.link(nc.vector.tensor_tensor(eq[:], lg[:], bc(top[:]), ALU.is_equal))
            chain.link(nc.vector.tensor_tensor(eq[:], eq[:], W.rank[:].unsqueeze(1).to_broadcast([P, GT, E]),
                                               ALU.mult))
            chain.link(nc.vector.tensor_reduce(pick[:], eq[:], AX.X, ALU.max))
            dve.wait_ge(exp_ready, g + 1)
            chain.link(nc.vector.tensor_reduce(tot[:], ex[:], AX.X, ALU.add))
            chain.link(nc.vector.reciprocal(gate[:], tot[:]))
            chain.link(nc.vector.tensor_tensor(eq[:], eq[:], bc(pick[:]), ALU.is_equal))
            nc.vector.scalar_tensor_tensor(coef[:, par], eq[:], 0.5, bc(gate[:]), ALU.mult, ALU.mult)\
                .then_inc(coef_ready, 1)

        def vector_combine(dve, chain, g, par, t):
            dve.wait_ge(experts_ready, g * GT + t + 1)
            x = fr.rows(g)[:, t, :]
            for e in range(E):
                bank = OUT[t % 2] + e // 4
                ins = nc.vector.scalar_tensor_tensor(
                    x, psum[:, bank, (e % 4) * D:(e % 4 + 1) * D], coef[:, par, t, e:e + 1], x,
                    ALU.mult, ALU.add)
                if e < E - 1:
                    chain.link(ins)
            ins.then_inc(experts_used, 1)

        def vector_bias(dve, g):
            dve.wait_ge(bias_ready, g + 1)
            x = fr.rows(g)
            nc.vector.tensor_tensor(x, psum[:, CT, :].rearrange("p (t d) -> p t d", d=D), x, ALU.add)\
                .then_inc(bias_used, 1)

        ROUTE_LINKS, COMBINE_LINKS, NORM_LINKS = 8, E - 1, 1

        with nc.Block() as block:
            @block.vector
            def _(dve):
                chain = Chain(dve, dve_chain, W.passed)
                first_wait(dve)

                def step(g, par, last):
                    if not last:
                        fr.vector_stats(dve, chain, g + 1)
                        fr.vector_normalize(dve, g + 1)
                    for t in range(2):
                        vector_combine(dve, chain, g, par, t)
                    if not last:
                        fr.vector_low(dve, g + 1, 1 - par, xh[:, 1 - par], xl[:, 1 - par])
                    vector_combine(dve, chain, g, par, 2)
                    if not last:
                        vector_route(dve, chain, g + 1, 1 - par)
                    vector_combine(dve, chain, g, par, 3)
                    dve.wait_ge(experts_used, g * GT + 4)
                    vector_bias(dve, g)

                fr.vector_stats(dve, chain, 0)
                fr.vector_normalize(dve, 0, first=True)
                fr.vector_low(dve, 0, 0, xh[:, 0], xl[:, 0])
                vector_route(dve, chain, 0, 0)
                with dve.Fori(0, GROUPS // 2 - 1) as j:
                    chain.turn(j, 2 * (NORM_LINKS + ROUTE_LINKS + 4 * COMBINE_LINKS))
                    step(j * 2, 0, False)
                    step(j * 2 + 1, 1, False)
                chain.leave(GROUPS // 2 - 1)
                step(GROUPS - 2, 0, False)
                step(GROUPS - 1, 1, True)
                dve.wait_ge(bias_used, GROUPS)

            @block.gpsimd
            def _(pool):
                with pool.Fori(0, GROUPS) as g:
                    fr.gpsimd_rstd(pool, g)

            @block.scalar
            def _(act):
                def route(g, par):
                    fr.scalar_high(act, g, par, xh[:, par])
                    act.wait_ge(shifted_ready, g + 1)
                    nc.scalar.activation(ex[:], ex[:], ACT.Exp).then_inc(exp_ready, 1)

                def coef_rows(g):
                    act.wait_ge(ct_ready, g + 1)
                    nc.scalar.activation(coefT[:], psum[0:E, CT, :], ACT.Copy).then_inc(coefT_ready, 1)

                route(0, 0)
                with act.Fori(0, GROUPS // 2 - 1) as j:
                    for par in range(2):
                        coef_rows(j * 2 + par)
                        route(j * 2 + par + 1, 1 - par)
                coef_rows(GROUPS - 2)
                route(GROUPS - 1, 1)
                coef_rows(GROUPS - 1)

            @block.tensor
            def _(pe):
                def route(g, par):
                    pe.wait_ge(fr.low_ready, g + 1)
                    for t in range(GT):
                        tok = slice(t * P, (t + 1) * P)
                        ins = three_products(nc, psum[:, LOGITS, t * E:(t + 1) * E],
                                             (xh[:, par, tok], xl[:, par, tok]), (W.rwh[:], W.rwl[:]))
                    ins.then_inc(logits_ready, 1)

                def experts(g, par, t, first=False):
                    tok = slice(t * P, (t + 1) * P)
                    if not (first and t < 2):
                        pe.wait_ge(experts_used, g * GT + t - 1)
                    for half in range(2):
                        cols = slice(half * 4 * D, (half + 1) * 4 * D)
                        ins = three_products(nc, psum[:, OUT[t % 2] + half, :],
                                             (xh[:, par, tok], xl[:, par, tok]),
                                             (W.ewh[:, cols], W.ewl[:, cols]))
                    ins.then_inc(experts_ready, 1)

                def coef_columns(g, par, first=False):
                    pe.wait_ge(coef_ready, g + 1)
                    if not first:
                        pe.wait_ge(bias_used, g)
                    for t in range(GT):
                        ins = nc.tensor.transpose(psum[0:E, CT, t * P:(t + 1) * P], coef[:, par, t, :], ident[:])
                    ins.then_inc(ct_ready, 1)

                def bias(g):
                    pe.wait_ge(coefT_ready, g + 1)
                    for t in range(GT):
                        ins = nc.tensor.matmul(psum[:, CT, t * D:(t + 1) * D], coefT[:, t * P:(t + 1) * P],
                                               W.eb[:], start=True, stop=True)
                    ins.then_inc(bias_ready, 1)

                def step(g, par, first=False, last=False):
                    coef_columns(g, par, first)
                    experts(g, par, 0, first)
                    bias(g)
                    experts(g, par, 1, first)
                    if not last:
                        fr.tensor_transpose(pe, g + 1, 1 - par)
                    experts(g, par, 2)
                    if not last:
                        route(g + 1, 1 - par)
                    experts(g, par, 3)

                fr.tensor_transpose(pe, 0, 0)
                route(0, 0)
                step(0, 0, first=True)
                step(1, 1)
                with pe.Fori(1, GROUPS // 2 - 1) as j:
                    step(j * 2, 0)
                    step(j * 2 + 1, 1)
                step(GROUPS - 2, 0)
                step(GROUPS - 1, 1, last=True)


def attention(nc, name, X, ident, neg_half, psum, W):
    SCALE = float(D) ** -0.5
    NC = S // 512
    QT = S // P
    GB = S // GW
    with ExitStack() as ctx:
        sb = lambda n, s, dt=F32: ctx.enter_context(nc.sbuf_tensor(f"{name}_{n}", s, dt))
        sem = Semaphores(ctx, nc, name)
        fr = Front(ctx, sem, nc, name, X, ident, neg_half, (0, 1), psum, W.passed)
        xh, xl = sb("xh", [P, GW], F32R), sb("xl", [P, GW], F32R)
        kh, kl = sb("kh", [P, S], F32R), sb("kl", [P, S], F32R)
        qh, ql = sb("qh", [P, S], F32R), sb("ql", [P, S], F32R)
        vh, vl = sb("vh", [P, QT, D], F32R), sb("vl", [P, QT, D], F32R)
        v32 = sb("v32", [P, GT, D])
        qsh, qsl = sb("qsh", [P, 2, P], F32R), sb("qsl", [P, 2, P], F32R)
        prob = sb("prob", [P, S])
        ph, pl = sb("ph", [P, 2, 512], F32R), sb("pl", [P, 2, 512], F32R)
        cmax, nmax, nbias = sb("chunk_max", [P, NC]), sb("neg_max", [P, 1]), sb("neg_bias", [P, 2])
        rsum, rtot, rinv = sb("row_sums", [P, 2, NC]), sb("row_total", [P, 1]), sb("row_inverse", [P, 1])
        KB, QB, VB = 2, 3, 4
        TB, OB = (4, 5), (6, 7)
        dve_chain = sem("dve_chain")
        k_ready, q_ready, v_ready = sem("k_ready"), sem("q_ready"), sem("v_ready")
        kh_ready, qh_ready, kl_ready, ql_ready = sem("kh_ready"), sem("qh_ready"), sem("kl_ready"), sem("ql_ready")
        v32_ready, vh_ready, vl_ready = sem("v32_ready"), sem("vh_ready"), sem("vl_ready")
        staged, scores_ready, nbias_ready, exp_ready = sem("staged"), sem("scores_ready"), sem("nbias_ready"), sem("exp_ready")
        pt_ready, ph_ready, pl_ready, out_ready, x_done = (
            sem("pt_ready"), sem("ph_ready"), sem("pl_ready"), sem("out_ready"), sem("x_done"))

        with nc.Block() as block:
            @block.vector
            def _(dve):
                chain = Chain(dve, dve_chain, W.passed)

                def project(g, cols, tiles):
                    fr.vector_stats(dve, chain, g)
                    fr.vector_normalize(dve, g, first=True)
                    fr.vector_low(dve, g, 0, xh[:], xl[:])
                    for ready, high, low, bank, bias, done in ((kh_ready, kh, kl, KB, W.bk, kl_ready),
                                                               (qh_ready, qh, ql, QB, W.bq, ql_ready)):
                        dve.wait_ge(ready, g + 1)
                        nc.vector.scalar_tensor_tensor(low[:, cols], psum[:, bank, :], bias[:],
                                                       high[:, cols].bitcast(F32), ALU.add, ALU.subtract)\
                            .then_inc(done, 1)
                    dve.wait_ge(v_ready, g + 1)
                    nc.vector.tensor_tensor(v32[:], psum[:, VB, :].rearrange("p (t d) -> p t d", d=D),
                                            W.bvb[:].unsqueeze(1).to_broadcast([P, GT, D]), ALU.add)\
                        .then_inc(v32_ready, 1)

                def vector_max(i, par):
                    for c in range(NC):
                        dve.wait_ge(scores_ready, i * NC + c + 1)
                        ins = nc.vector.tensor_reduce(cmax[:, c:c + 1], psum[:, c, :], AX.X, ALU.max)
                    chain.link(ins)
                    chain.link(nc.vector.tensor_reduce(nmax[:], cmax[:], AX.X, ALU.max))
                    nc.vector.tensor_scalar(nbias[:, par:par + 1], nmax[:], -SCALE, None, ALU.mult)\
                        .then_inc(nbias_ready, 1)

                def vector_weigh(i, par):
                    for c in range(NC):
                        dve.wait_ge(ph_ready, i * NC + c + 1)
                        nc.vector.tensor_tensor(pl[:, c % 2, :], psum[:, TB[c % 2], :],
                                                ph[:, c % 2, :].bitcast(F32), ALU.subtract)\
                            .then_inc(pl_ready, 1)
                    chain.link(nc.vector.tensor_reduce(rtot[:], rsum[:, par, :], AX.X, ALU.add))
                    chain.link(nc.vector.reciprocal(rinv[:], rtot[:]))
                    dve.wait_ge(out_ready, i + 1)
                    x = X[:, bass.ds(i, 1), :].rearrange("p o d -> p (o d)")
                    nc.vector.scalar_tensor_tensor(x, psum[:, OB[par], 0:D], rinv[:], x, ALU.mult, ALU.add)\
                        .then_inc(x_done, 1)

                with dve.Fori(0, B) as b:
                    chain.turn(b, GB + QT * 4)
                    with dve.Fori(0, GB) as j:
                        chain.turn(j, 1)
                        project(b * GB + j, bass.ts(j, GW), None)
                    chain.leave(GB)
                    vector_max(b * QT, 0)
                    with dve.Fori(0, QT // 2 - 1) as j:
                        chain.turn(j, 8)
                        for par in range(2):
                            vector_max(b * QT + j * 2 + par + 1, 1 - par)
                            vector_weigh(b * QT + j * 2 + par, par)
                    chain.leave(QT // 2 - 1)
                    vector_max(b * QT + QT - 1, 1)
                    vector_weigh(b * QT + QT - 2, 0)
                    vector_weigh(b * QT + QT - 1, 1)
                chain.leave(B)
                dve.wait_ge(x_done, B * QT)

            @block.gpsimd
            def _(pool):
                def stage(i, j, par):
                    cols = bass.ts(j, P)
                    nc.gpsimd.tensor_copy(qsh[:, par, :], qh[:, cols])
                    nc.gpsimd.tensor_copy(qsl[:, par, :], ql[:, cols]).then_inc(staged, 1)

                with pool.Fori(0, B) as b:
                    with pool.Fori(0, GB) as j:
                        g = b * GB + j
                        fr.gpsimd_rstd(pool, g)
                        wait_alone(pool, W.passed, vh_ready, g + 1)
                        tiles = bass.ts(j, GT)
                        nc.gpsimd.tensor_tensor(vl[:, tiles, :], v32[:], vh[:, tiles, :].bitcast(F32),
                                                ALU.subtract).then_inc(vl_ready, 1)
                    wait_alone(pool, W.passed, qh_ready, b * GB + GB)
                    wait_alone(pool, W.passed, ql_ready, b * GB + GB)
                    stage(None, 0, 0)
                    stage(None, 1, 1)
                    with pool.Fori(1, QT // 2) as j:
                        for par in range(2):
                            wait_alone(pool, W.passed, scores_ready, (b * QT + j * 2 + par - 1) * NC)
                            stage(None, j * 2 + par, par)

            @block.scalar
            def _(act):
                def project(g, cols, tiles):
                    fr.scalar_high(act, g, 0, xh[:])
                    for ready, high, bank, bias, done in ((k_ready, kh, KB, W.bk, kh_ready),
                                                          (q_ready, qh, QB, W.bq, qh_ready)):
                        act.wait_ge(ready, g + 1)
                        nc.scalar.activation(high[:, cols], psum[:, bank, :], ACT.Identity, bias=bias[:])\
                            .then_inc(done, 1)
                    act.wait_ge(v32_ready, g + 1)
                    nc.scalar.activation(vh[:, tiles, :], v32[:], ACT.Copy).then_inc(vh_ready, 1)

                def exps(i, par, c):
                    act.wait_ge(nbias_ready, i + 1)
                    nc.scalar.activation(prob[:, c * 512:(c + 1) * 512], psum[:, c, :], ACT.Exp,
                                         bias=nbias[:, par:par + 1], scale=SCALE,
                                         accum_out=rsum[:, par, c:c + 1]).then_inc(exp_ready, 1)

                def high(i, c):
                    act.wait_ge(pt_ready, i * NC + c + 1)
                    nc.scalar.activation(ph[:, c % 2, :], psum[:, TB[c % 2], :], ACT.Copy)\
                        .then_inc(ph_ready, 1)

                def step(i, par):
                    high(i, 0)
                    high(i, 1)
                    exps(i + 1, 1 - par, 0)
                    high(i, 2)
                    exps(i + 1, 1 - par, 1)
                    high(i, 3)
                    exps(i + 1, 1 - par, 2)
                    exps(i + 1, 1 - par, 3)

                with act.Fori(0, B) as b:
                    with act.Fori(0, GB) as j:
                        project(b * GB + j, bass.ts(j, GW), bass.ts(j, GT))
                    for c in range(NC):
                        exps(b * QT, 0, c)
                    with act.Fori(0, QT // 2 - 1) as j:
                        step(b * QT + j * 2, 0)
                        step(b * QT + j * 2 + 1, 1)
                    step(b * QT + QT - 2, 0)
                    for c in range(NC):
                        high(b * QT + QT - 1, c)

            @block.tensor
            def _(pe):
                def project(g):
                    fr.tensor_transpose(pe, g, 0)
                    pe.wait_ge(fr.low_ready, g + 1)
                    three_products(nc, psum[:, KB, :], (W.wkh[:], W.wkl[:]), (xh[:], xl[:])).then_inc(k_ready, 1)
                    three_products(nc, psum[:, QB, :], (W.wqh[:], W.wql[:]), (xh[:], xl[:])).then_inc(q_ready, 1)
                    for t in range(GT):
                        tok = slice(t * P, (t + 1) * P)
                        ins = three_products(nc, psum[:, VB, tok], (xh[:, tok], xl[:, tok]), (W.wvh[:], W.wvl[:]))
                    ins.then_inc(v_ready, 1)
                    pe.wait_ge(kl_ready, g + 1)
                    pe.wait_ge(ql_ready, g + 1)
                    pe.wait_ge(v32_ready, g + 1)

                def scores(i, par, first=False):
                    pe.wait_ge(staged, i + 1)
                    for c in range(NC):
                        if not first:
                            pe.wait_ge(exp_ready, (i - 1) * NC + c + 1)
                        cols = slice(c * 512, (c + 1) * 512)
                        three_products(nc, psum[:, c, :], (qsh[:, par, :], qsl[:, par, :]),
                                       (kh[:, cols], kl[:, cols])).then_inc(scores_ready, 1)

                def turn(i, c):
                    pe.wait_ge(exp_ready, i * NC + c + 1)
                    for k in range(4):
                        cols = slice((c * 4 + k) * P, (c * 4 + k + 1) * P)
                        ins = nc.tensor.transpose(psum[:, TB[c % 2], k * P:(k + 1) * P], prob[:, cols], ident[:])
                    ins.then_inc(pt_ready, 1)

                def weigh(i, par, c):
                    pe.wait_ge(pl_ready, i * NC + c + 1)
                    for k in range(4):
                        tok = slice(k * P, (k + 1) * P)
                        ins = three_products(nc, psum[:, OB[par], 0:D], (ph[:, c % 2, tok], pl[:, c % 2, tok]),
                                             (vh[:, c * 4 + k, :], vl[:, c * 4 + k, :]),
                                             start=(c == 0 and k == 0), stop=(c == NC - 1 and k == 3))
                    if c == NC - 1:
                        ins.then_inc(out_ready, 1)

                def outputs(i, par):
                    turn(i, 0)
                    turn(i, 1)
                    weigh(i, par, 0)
                    turn(i, 2)
                    weigh(i, par, 1)
                    turn(i, 3)
                    weigh(i, par, 2)
                    weigh(i, par, 3)

                with pe.Fori(0, B) as b:
                    with pe.Fori(0, GB) as j:
                        project(b * GB + j)
                    pe.wait_ge(vl_ready, b * GB + GB)
                    scores(b * QT, 0, first=True)
                    with pe.Fori(0, QT // 2 - 1) as j:
                        for par in range(2):
                            scores(b * QT + j * 2 + par + 1, 1 - par)
                            outputs(b * QT + j * 2 + par, par)
                    scores(b * QT + QT - 1, 1)
                    outputs(b * QT + QT - 2, 0)
                    outputs(b * QT + QT - 1, 1)


def second_mixture(nc, name, X, ident, neg_half, psum, W, A):
    with ExitStack() as ctx:
        sb = lambda n, s, dt=F32: ctx.enter_context(nc.sbuf_tensor(f"{name}_{n}", s, dt))
        sem = Semaphores(ctx, nc, name)
        fr = Front(ctx, sem, nc, name, X, ident, neg_half, (0, 1), psum, W.passed)
        xh, xl = sb("xh", [P, GW], F32R), sb("xl", [P, GW], F32R)
        allh, alll = sb("allh", [P, GROUPS, GW], F32R), sb("alll", [P, GROUPS, GW], F32R)
        lg, ex = sb("logits", [P, TILES, E]), sb("exps", [P, TILES, E])
        one, two, tmp = sb("one", [P, TILES, E]), sb("two", [P, TILES, E]), sb("tmp", [P, TILES, E])
        top, tot, pick = sb("top", [P, TILES]), sb("total", [P, TILES]), sb("pick", [P, TILES])
        coef = sb("coef", [P, TILES, E])
        coefT = sb("coefT", [P, 2, P])
        b2diag = sb("b2diag", [P, TILES // 2 * D])
        diag_zero, b2_loaded = sem("diag_zero"), sem("b2_loaded")
        raw1, raw2 = sb("raw1", [P, 2, F]), sb("raw2", [P, 2, FC, D])
        w1h, w1l = sb("w1h", [P, 2, F], F32R), sb("w1l", [P, 2, F], F32R)
        w2h, w2l = sb("w2h", [P, 2, FC, D], F32R), sb("w2l", [P, 2, FC, D], F32R)
        hh, hl, hf = sb("hh", [P, FC, GW], F32R), sb("hl", [P, FC, GW], F32R), sb("hf", [P, FC, GW])
        LOGITS, CT, YB = 2, 3, (4, 5)
        dve_chain = sem("dve_chain")
        logits_ready, logits_used, copied = sem("logits_ready"), sem("logits_used"), sem("copied")
        shifted_ready, exp_ready, coef_ready = sem("shifted_ready"), sem("exp_ready"), sem("coef_ready")
        ct_ready, coefT_ready, bias_ready, bias_used = (
            sem("ct_ready"), sem("coefT_ready"), sem("bias_ready"), sem("bias_used"))
        raw_loaded = [sem("raw_loaded0"), sem("raw_loaded1")]
        w_high, w_low, expert_done = sem("w_high"), sem("w_low"), sem("expert_done")
        h_ready, hh_ready, hf_ready, hl_ready = sem("h_ready"), sem("hh_ready"), sem("hf_ready"), sem("hl_ready")
        y_ready, y_used = sem("y_ready"), sem("y_used")

        def bc(ap):
            return ap.unsqueeze(2).to_broadcast([P, TILES, E])

        def rank():
            return W.rank[:].unsqueeze(1).to_broadcast([P, TILES, E])

        with nc.Block() as block:
            @block.vector
            def _(dve):
                chain = Chain(dve, dve_chain, W.passed)

                def vector_first(mask):
                    chain.link(nc.vector.tensor_tensor(mask[:], mask[:], rank(), ALU.mult))
                    chain.link(nc.vector.tensor_reduce(pick[:], mask[:], AX.X, ALU.max))
                    chain.link(nc.vector.tensor_tensor(mask[:], mask[:], bc(pick[:]), ALU.is_equal))

                with dve.Fori(0, GROUPS) as g:
                    chain.turn(g, 1)
                    fr.vector_stats(dve, chain, g)
                    fr.vector_normalize(dve, g, first=True)
                    fr.vector_low(dve, g, 0, xh[:], xl[:])
                    dve.wait_ge(logits_ready, g + 1)
                    nc.vector.tensor_tensor(
                        lg[:, bass.ts(g, GT), :], psum[:, LOGITS, 0:GT * E].rearrange("p (t e) -> p t e", e=E),
                        W.gb[:].unsqueeze(1).to_broadcast([P, GT, E]), ALU.add).then_inc(logits_used, 1)
                chain.leave(GROUPS)
                dve.wait_ge(logits_used, GROUPS)
                chain.link(nc.vector.tensor_reduce(top[:], lg[:], AX.X, ALU.max))
                nc.vector.tensor_tensor(ex[:], lg[:], bc(top[:]), ALU.subtract).then_inc(shifted_ready, 1)
                chain.link(nc.vector.tensor_tensor(one[:], lg[:], bc(top[:]), ALU.is_equal))
                vector_first(one)
                chain.link(nc.vector.scalar_tensor_tensor(tmp[:], one[:], -3e38, lg[:], ALU.mult, ALU.add))
                chain.link(nc.vector.tensor_reduce(top[:], tmp[:], AX.X, ALU.max))
                chain.link(nc.vector.tensor_tensor(two[:], tmp[:], bc(top[:]), ALU.is_equal))
                vector_first(two)
                chain.link(nc.vector.tensor_tensor(one[:], one[:], two[:], ALU.add))
                dve.wait_ge(exp_ready, 1)
                chain.link(nc.vector.tensor_tensor(one[:], one[:], ex[:], ALU.mult))
                chain.link(nc.vector.tensor_reduce(tot[:], one[:], AX.X, ALU.add))
                chain.link(nc.vector.reciprocal(top[:], tot[:]))
                nc.vector.scalar_tensor_tensor(coef[:], one[:], 0.5, bc(top[:]), ALU.mult, ALU.mult)\
                    .then_inc(coef_ready, 1)
                for g in range(GROUPS):
                    dve.wait_ge(bias_ready, g + 1)
                    x = fr.rows(g)
                    nc.vector.tensor_tensor(x, psum[:, 4 + g % 4, :].rearrange("p (t d) -> p t d", d=D), x, ALU.add)\
                        .then_inc(bias_used, 1)
                dve.wait_ge(bias_used, GROUPS)
                dve.sem_inc(y_used, 2)

                def hidden(e, g):
                    for c in range(FC):
                        dve.wait_ge(h_ready, (e * GROUPS + g) * FC + c + 1)
                        dve.wait_ge(hh_ready, (e * GROUPS + g) * FC + c + 1)
                        nc.vector.tensor_scalar(hf[:, c, :], psum[:, c, :], W.b1T[:, bass.ds(e * FC + c, 1)], 0.0,
                                                ALU.add, ALU.max).then_inc(hf_ready, 1)

                def combine(e, g, par):
                    dve.wait_ge(y_ready, e * GROUPS + g + 1)
                    for t in range(GT):
                        x = X[:, bass.ds(g * GT + t, 1), :].rearrange("p o d -> p (o d)")
                        c = coef[:, bass.ds(g * GT + t, 1), bass.ds(e, 1)].rearrange("p o d -> p (o d)")
                        ins = nc.vector.scalar_tensor_tensor(x, psum[:, YB[par], t * D:(t + 1) * D], c, x,
                                                             ALU.mult, ALU.add)
                    ins.then_inc(y_used, 1)

                with dve.Fori(0, E) as e:
                    dve.wait_ge(y_used, e * GROUPS + 2)
                    hidden(e, 0)
                    with dve.Fori(0, GROUPS // 2 - 1) as j:
                        for par in range(2):
                            hidden(e, j * 2 + par + 1)
                            combine(e, j * 2 + par, par)
                    hidden(e, GROUPS - 1)
                    combine(e, GROUPS - 2, 0)
                    combine(e, GROUPS - 1, 1)
                dve.wait_ge(y_used, E * GROUPS + 2)

            @block.gpsimd
            def _(pool):
                nc.gpsimd.memset(b2diag[:], 0.0).then_inc(diag_zero, 1)
                with pool.Fori(0, GROUPS) as g:
                    fr.gpsimd_rstd(pool, g)
                    wait_alone(pool, W.passed, fr.low_ready, g + 1)
                    nc.gpsimd.tensor_copy(allh[:, bass.ds(g, 1), :].rearrange("p o d -> p (o d)"), xh[:])
                    nc.gpsimd.tensor_copy(alll[:, bass.ds(g, 1), :].rearrange("p o d -> p (o d)"), xl[:])\
                        .then_inc(copied, 1)
                with pool.Fori(0, E // 2) as j:
                    for par in range(2):
                        e = j * 2 + par
                        wait_alone(pool, W.passed, w_high, e * 2 + 2)
                        nc.gpsimd.tensor_tensor(w1l[:, par, :], raw1[:, par, :], w1h[:, par, :].bitcast(F32),
                                                ALU.subtract).then_inc(w_low, 1)
                        nc.gpsimd.tensor_tensor(w2l[:, par], raw2[:, par], w2h[:, par].bitcast(F32),
                                                ALU.subtract).then_inc(w_low, 1)
                        with pool.Fori(0, GROUPS) as g:
                            for c in range(FC):
                                n = (e * GROUPS + g) * FC + c + 1
                                wait_alone(pool, W.passed, hf_ready, n)
                                nc.gpsimd.tensor_tensor(hl[:, c, :], hf[:, c, :], hh[:, c, :].bitcast(F32),
                                                        ALU.subtract).then_inc(hl_ready, 1)

            @block.sync
            def _(sp):
                sp.wait_ge(diag_zero, 1)
                for t in range(TILES // 2):
                    sp.dma_start(b2diag[t * E:(t + 1) * E, t * D:(t + 1) * D], A["L1_ffn_b2"])\
                        .then_inc(b2_loaded, 16)

                def load(e, par):
                    w1, w2 = A["L1_ffn_w1"], A["L1_ffn_w2"]
                    sp.dma_start(raw1[:, par, :], w1[bass.ds(e, 1), :, :].rearrange("o p f -> p (o f)"))\
                        .then_inc(raw_loaded[par], 16)
                    sp.dma_start(raw2[:, par], w2[bass.ds(e, 1), :, :].rearrange("o (c p) d -> p (o c) d", p=P))\
                        .then_inc(raw_loaded[par], 16)
                load(0, 0)
                load(1, 1)
                with sp.Fori(1, E // 2) as j:
                    for par in range(2):
                        sp.wait_ge(w_low, (j * 2 + par - 2) * 2 + 2)
                        load(j * 2 + par, par)

            @block.scalar
            def _(act):
                with act.Fori(0, GROUPS) as g:
                    fr.scalar_high(act, g, 0, xh[:])
                act.wait_ge(shifted_ready, 1)
                nc.scalar.activation(ex[:], ex[:], ACT.Exp).then_inc(exp_ready, 1)
                act.wait_ge(ct_ready, 1)
                nc.scalar.activation(coefT[:].rearrange("p a b -> p (a b)"), psum[:, CT, 0:2 * P], ACT.Copy)\
                    .then_inc(coefT_ready, 1)

                def parts(e, j, par):
                    act.wait_ge(raw_loaded[par], j * 32 + 32)
                    nc.scalar.activation(w1h[:, par, :], raw1[:, par, :], ACT.Copy).then_inc(w_high, 1)
                    nc.scalar.activation(w2h[:, par], raw2[:, par], ACT.Copy).then_inc(w_high, 1)

                with act.Fori(0, E // 2) as j:
                    for par in range(2):
                        e = j * 2 + par
                        parts(e, j, par)
                        with act.Fori(0, GROUPS) as g:
                            for c in range(FC):
                                act.wait_ge(h_ready, (e * GROUPS + g) * FC + c + 1)
                                nc.scalar.activation(hh[:, c, :], psum[:, c, :], ACT.Relu,
                                                     bias=W.b1T[:, bass.ds(e * FC + c, 1)]).then_inc(hh_ready, 1)

            @block.tensor
            def _(pe):
                with pe.Fori(0, GROUPS) as g:
                    fr.tensor_transpose(pe, g, 0)
                    pe.wait_ge(fr.low_ready, g + 1)
                    for t in range(GT):
                        tok = slice(t * P, (t + 1) * P)
                        ins = three_products(nc, psum[:, LOGITS, t * E:(t + 1) * E],
                                             (xh[:, tok], xl[:, tok]), (W.gwh[:], W.gwl[:]))
                    ins.then_inc(logits_ready, 1)
                    pe.wait_ge(copied, g + 1)
                    pe.wait_ge(logits_used, g + 1)
                pe.wait_ge(coef_ready, 1)
                for n in range(2):
                    ins = nc.tensor.transpose(psum[:, CT, n * P:(n + 1) * P],
                                              coef[:, n * TILES // 2:(n + 1) * TILES // 2, :]
                                              .rearrange("p t e -> p (t e)"), ident[:])
                ins.then_inc(ct_ready, 1)
                pe.wait_ge(coefT_ready, 1)
                pe.wait_ge(b2_loaded, TILES // 2 * 16)
                for g in range(GROUPS):
                    if g >= 4:
                        pe.wait_ge(bias_used, g - 3)
                    n, q = g // 4, g % 4
                    nc.tensor.matmul(psum[:, 4 + g % 4, :], coefT[:, n, :], b2diag[:, q * GW:(q + 1) * GW],
                                     start=True, stop=True).then_inc(bias_ready, 1)
                pe.wait_ge(bias_used, GROUPS)

                def up(e, g, c, par_e):
                    x = [a[:, bass.ds(g, 1), :].rearrange("p o d -> p (o d)") for a in (allh, alll)]
                    cols = slice(c * P, (c + 1) * P)
                    three_products(nc, psum[:, c, :], (w1h[:, par_e, cols], w1l[:, par_e, cols]), x)\
                        .then_inc(h_ready, 1)

                def down(e, g, c, par_e, par):
                    pe.wait_ge(hl_ready, (e * GROUPS + g) * FC + c + 1)
                    if c == 0:
                        pe.wait_ge(y_used, e * GROUPS + g + 1)
                    for t in range(GT):
                        tok = slice(t * P, (t + 1) * P)
                        ins = three_products(nc, psum[:, YB[par], tok], (hh[:, c, tok], hl[:, c, tok]),
                                             (w2h[:, par_e, c, :], w2l[:, par_e, c, :]),
                                             start=(c == 0 and t == 0), stop=(c == FC - 1), skip=True)
                    if c == FC - 1:
                        ins.then_inc(y_ready, 1)

                def group(e, g, par_e, par, last=False):
                    for c in range(FC):
                        if c < 2:
                            up(e, g, c + 2, par_e)
                        elif not last:
                            up(e, g + 1, c - 2, par_e)
                        down(e, g, c, par_e, par)

                with pe.Fori(0, E // 2) as j:
                    for par_e in range(2):
                        e = j * 2 + par_e
                        pe.wait_ge(w_low, e * 2 + 2)
                        up(e, 0, 0, par_e)
                        up(e, 0, 1, par_e)
                        with pe.Fori(0, GROUPS // 2 - 1) as i:
                            group(e, i * 2, par_e, 0)
                            group(e, i * 2 + 1, par_e, 1)
                        group(e, GROUPS - 2, par_e, 0)
                        group(e, GROUPS - 1, par_e, 1, last=True)


class Holder:
    pass


H, KD, VD = 4, 32, 64
KEY, VAL = H * KD, H * VD
CONV = 4
RMS_EPS = 1e-6
NQ = TILES * H


def row_stats(nc, eng, chain, stats, mv, src):
    for t in range(GT):
        ins = nc.vector.bn_stats(stats[:, t, :], src[:, t, :])
    chain.link_alone(ins)
    for t in range(GT):
        ins = nc.vector.bn_aggr(mv[:, t, :], stats[:, t, :])
    return ins


def inverse_root(nc, pool, passed, sem, count, out, src, tmp, scale, eps, power):
    nc.gpsimd.tensor_scalar(tmp, src, scale, eps, ALU.mult, ALU.add).then_inc(sem, 1)
    wait_alone(pool, passed, sem, count + 1)
    nc.gpsimd.tensor_tensor(out, tmp, power, ALU.pow).then_inc(sem, 1)


def delta_inputs(nc, X, ident, neg_half, psum, W, M):
    with ExitStack() as ctx:
        sb = lambda n, s, dt=F32: ctx.enter_context(nc.sbuf_tensor(f"in_{n}", s, dt))
        sem = Semaphores(ctx, nc, "in")
        stats, mv = sb("stats", [P, GT, 6]), sb("mv", [P, GT, 2])
        r1, r2, r3, rt = (sb(n, [P, GT]) for n in ("r1", "r2", "r3", "rt"))
        ss = sb("ss", [P, GT])
        y, sq, h0 = sb("y", [P, GT, D]), sb("sq", [P, GT, D]), sb("h0", [P, GT, D])
        hT = sb("hT", [P, GW])
        cv = sb("cv", [P, 4, GW + CONV - 1])
        acc, th = sb("acc", [P, 4, GW]), sb("th", [P, 4, GW])
        sg = sb("sg", [P, GT, VAL])
        sq2, ss2, rq, rqt = sb("sq2", [P, 2, GW]), sb("ss2", [P, 32]), sb("rq", [P, 32]), sb("rqt", [P, 32])
        fac, nh32 = sb("fac", [P, 32]), sb("nh32", [P, 32])
        dve_chain, pool_chain, act_chain = sem("dve_chain"), sem("pool_chain"), sem("act_chain")
        mv_ready, r1_ready, r2_ready, y_ready, ss_ready, r3_ready, h_ready = (
            sem(n) for n in ("mv_ready", "r1_ready", "r2_ready", "y_ready", "ss_ready", "r3_ready", "h_ready"))
        ht_ready, hT_ready, proj_ready, cv_ready, halo_ready, gate_ready, sg_ready, gate_used = (
            sem(n) for n in ("ht_ready", "hT_ready", "proj_ready", "cv_ready", "halo_ready", "gate_ready",
                             "sg_ready", "gate_used"))
        acc0_ready, acc_ready, th_ready, s2_ready, nat_ready, sq2_ready, ss2_ready, rq_ready, nat_used, v_used = (
            sem(n) for n in ("acc0_ready", "acc_ready", "th_ready", "s2_ready", "nat_ready", "sq2_ready",
                             "ss2_ready", "rq_ready", "nat_used", "v_used"))
        wloaded, consts = sem("wloaded"), sem("consts")
        GATE, AB, TB = (4, 5), 6, 7

        def tiles4(ap):
            return ap.unsqueeze(1).to_broadcast([P, GT, D])

        with nc.Block() as block:
            @block.vector
            def _(dve):
                chain = Chain(dve, dve_chain, W.passed)
                dve.wait_ge(wloaded, 16 * M.n_loads)
                with dve.Fori(0, B) as b:
                    chain.turn(b, 1 + (GROUPS // B) * 15)
                    chain.link_alone(nc.vector.memset(cv[:, :, GW:GW + CONV - 1], 0.0))
                    with dve.Fori(0, GROUPS // B) as j:
                        chain.turn(j, 15)
                        g = b * (GROUPS // B) + j
                        x, rows = X[:, bass.ts(g, GT), :], bass.ts(g, GT)
                        row_stats(nc, dve, chain, stats, mv, x).then_inc(mv_ready, 1)
                        dve.wait_ge(r1_ready, g * 4 + 2)
                        for t in range(GT):
                            ins = nc.vector.tensor_scalar(h0[:, t, :], x[:, t, :], mv[:, t, 0:1], r1[:, t:t + 1],
                                                          ALU.subtract, ALU.mult)
                        nc.vector.tensor_copy(M.mean[:, rows, :], mv[:, :, 0:1])
                        ins = nc.vector.tensor_copy(M.rstd[:, rows], r1[:])
                        chain.link(ins)
                        row_stats(nc, dve, chain, stats, mv, h0).then_inc(mv_ready, 1)
                        dve.wait_ge(r1_ready, g * 4 + 4)
                        for t in range(GT):
                            ins = nc.vector.tensor_scalar(y[:, t, :], h0[:, t, :], mv[:, t, 0:1], r2[:, t:t + 1],
                                                          ALU.subtract, ALU.mult)
                        chain.link(ins)
                        chain.link(nc.vector.tensor_tensor(y[:], y[:], tiles4(M.ln1g[:]), ALU.mult))
                        nc.vector.tensor_tensor(y[:], y[:], tiles4(M.ln1b[:]), ALU.add).then_inc(y_ready, 1)
                        dve.wait_ge(r3_ready, g * 2 + 2)
                        for t in range(GT):
                            ins = nc.vector.tensor_scalar(y[:, t, :], y[:, t, :], r3[:, t:t + 1], None, ALU.mult)
                        ins.then_inc(h_ready, 1)
                        nc.vector.tensor_copy(cv[:, :, 0:CONV - 1], cv[:, :, GW:GW + CONV - 1]).then_inc(halo_ready, 1)
                        for c in range(4):
                            dve.wait_ge(acc0_ready, g * 4 + c + 1)
                            for i in range(1, CONV):
                                ins = nc.vector.scalar_tensor_tensor(acc[:, c, :], cv[:, c, i:i + GW],
                                                                     M.convw[:, c, i:i + 1], acc[:, c, :],
                                                                     ALU.mult, ALU.add)
                                if i < CONV - 1:
                                    chain.link(ins)
                            ins.then_inc(acc_ready, 1)
                        for c in range(4):
                            dve.wait_ge(th_ready, g * 4 + c + 1)
                            nc.vector.scalar_tensor_tensor(th[:, c, :], th[:, c, :], 1.0, acc[:, c, :],
                                                           ALU.add, ALU.mult).then_inc(s2_ready, 1)
                        for n in range(2):
                            dve.wait_ge(sg_ready, g * 2 + n + 1)
                            nc.vector.scalar_tensor_tensor(
                                M.gate[:, bass.ds(g * GT + n * 2, 2), :], sg[:, 2 * n:2 * n + 2, :], 1.0,
                                psum[:, GATE[n], :].rearrange("p (t v) -> p t v", v=VAL), ALU.add, ALU.mult)
                        nc.vector.tensor_copy(M.ab[:, bass.ts(g, GT), :],
                                              psum[:, AB, 0:GT * 2 * H].rearrange("p (t e) -> p t e", e=2 * H))\
                            .then_inc(gate_used, 1)
                        dve.wait_ge(sq2_ready, g + 1)
                        nc.vector.tensor_reduce(ss2[:], sq2[:].rearrange("p a (n k) -> p (a n) k", k=KD), AX.X, ALU.add)\
                            .then_inc(ss2_ready, 1)
                        dve.wait_ge(rq_ready, g * 3 + 3)
                        for n, dst in enumerate((M.q, M.k)):
                            ins = nc.vector.tensor_tensor(
                                dst[:, bass.ts(g, GT), :].rearrange("p t (h k) -> p (t h) k", k=KD),
                                psum[:, n, :].rearrange("p (n k) -> p n k", k=KD),
                                rq[:, n * 16:(n + 1) * 16].unsqueeze(2).to_broadcast([P, 16, KD]), ALU.mult)
                            chain.link(ins)
                        ins = nc.vector.memset(rt[:, 0:1], 0.0)
                        ins.then_inc(nat_used, 1)
                    chain.leave(GROUPS // B)
                chain.leave(B)

            @block.gpsimd
            def _(pool):
                nc.gpsimd.memset(nh32[:], -0.5).then_inc(consts, 1)
                nc.gpsimd.memset(fac[:, 0:16], 0.5 * float(KD) ** -0.5).then_inc(consts, 1)
                nc.gpsimd.memset(fac[:, 16:32], 0.5).then_inc(consts, 1)
                pool.wait_ge(consts, 3)
                with pool.Fori(0, GROUPS) as g:
                    wait_alone(pool, W.passed, mv_ready, g * 2 + 1)
                    inverse_root(nc, pool, W.passed, r1_ready, g * 4, r1[:], mv[:, :, 1], r2[:], 1.0, LN_EPS, neg_half[:])
                    wait_alone(pool, W.passed, mv_ready, g * 2 + 2)
                    inverse_root(nc, pool, W.passed, r1_ready, g * 4 + 2, r2[:], mv[:, :, 1], r1[:], 1.0, LN_EPS, neg_half[:])
                    wait_alone(pool, W.passed, ss_ready, g + 1)
                    inverse_root(nc, pool, W.passed, r3_ready, g * 2, r3[:], ss[:], r1[:], 1.0 / D, RMS_EPS, neg_half[:])
                    wait_alone(pool, W.passed, ss2_ready, g + 1)
                    inverse_root(nc, pool, W.passed, rq_ready, g * 3, rqt[:], ss2[:], rq[:], 0.25, RMS_EPS, nh32[:])
                    wait_alone(pool, W.passed, rq_ready, g * 3 + 2)
                    nc.gpsimd.tensor_tensor(rq[:], rqt[:], fac[:], ALU.mult).then_inc(rq_ready, 1)

            @block.sync
            def _(sp):
                for dst, src in M.loads:
                    sp.dma_start(dst, src).then_inc(wloaded, 16)

            @block.scalar
            def _(act):
                act.wait_ge(wloaded, 16 * M.n_loads)
                with act.Fori(0, GROUPS) as g:
                    act.wait_ge(y_ready, g + 1)
                    for t in range(GT):
                        ins = nc.scalar.activation(sq[:, t, :], y[:, t, :], ACT.Square, accum_out=ss[:, t:t + 1])
                    ins.then_inc(ss_ready, 1)
                    act.wait_ge(ht_ready, g + 1)
                    nc.scalar.activation(hT[:], psum[:, TB, :], ACT.Copy, scale=M.rmsw[:]).then_inc(hT_ready, 1)
                    act.wait_ge(halo_ready, g + 1)
                    for c in range(4):
                        act.wait_ge(proj_ready, g * 4 + c + 1)
                        nc.scalar.activation(cv[:, c, CONV - 1:], psum[:, c, :], ACT.Copy).then_inc(cv_ready, 1)
                    for c in range(4):
                        act.wait_ge(cv_ready, g * 4 + c + 1)
                        nc.scalar.activation(acc[:, c, :], cv[:, c, 0:GW], ACT.Copy, scale=M.convw[:, c, 0:1])\
                            .then_inc(acc0_ready, 1)
                    act.wait_ge(gate_ready, g + 1)
                    for n in range(2):
                        nc.scalar.activation(sg[:, 2 * n:2 * n + 2, :],
                                             psum[:, GATE[n], :].rearrange("p (t v) -> p t v", v=VAL),
                                             ACT.Tanh, scale=0.5).then_inc(sg_ready, 1)
                    for c in range(4):
                        act.wait_ge(acc_ready, g * 4 + c + 1)
                        nc.scalar.activation(th[:, c, :], acc[:, c, :], ACT.Tanh, scale=0.5).then_inc(th_ready, 1)
                    act.wait_ge(nat_ready, g + 1)
                    nc.scalar.activation(sq2[:, 0, :], psum[:, 0, :], ACT.Square)
                    nc.scalar.activation(sq2[:, 1, :], psum[:, 1, :], ACT.Square).then_inc(sq2_ready, 1)
                    for n in range(2):
                        ins = nc.scalar.activation(M.v[:, bass.ds(g * GT + n * 2, 2), :],
                                                   psum[:, 2 + n, :].rearrange("p (t v) -> p t v", v=VAL),
                                                   ACT.Copy, scale=0.5)
                    ins.then_inc(v_used, 1)

            @block.tensor
            def _(pe):
                with pe.Fori(0, GROUPS) as g:
                    pe.wait_ge(h_ready, g + 1)
                    for t in range(GT):
                        ins = nc.tensor.transpose(psum[:, TB, t * P:(t + 1) * P], y[:, t, :], ident[:])
                    ins.then_inc(ht_ready, 1)
                    pe.wait_ge(hT_ready, g + 1)
                    for c, w in enumerate((M.wq[:], M.wk[:], M.wv[:, 0:P], M.wv[:, P:2 * P])):
                        nc.tensor.matmul(psum[:, c, :], w, hT[:], start=True, stop=True).then_inc(proj_ready, 1)
                    for t in range(GT):
                        nc.tensor.matmul(psum[:, GATE[t // 2], (t % 2) * VAL:(t % 2 + 1) * VAL],
                                         hT[:, t * P:(t + 1) * P], M.wg[:], start=True, stop=True)
                    for t in range(GT):
                        ins = nc.tensor.matmul(psum[:, AB, t * 2 * H:(t + 1) * 2 * H], hT[:, t * P:(t + 1) * P],
                                               M.wab[:], start=True, stop=True)
                    ins.then_inc(gate_ready, 1)
                    pe.wait_ge(s2_ready, g * 4 + 4)
                    pe.wait_ge(cv_ready, g * 4 + 4)
                    for t in range(GT):
                        tok = slice(t * P, (t + 1) * P)
                        nc.tensor.transpose(psum[:, 0, tok], th[:, 0, tok], ident[:])
                        nc.tensor.transpose(psum[:, 1, tok], th[:, 1, tok], ident[:])
                        for n in range(2):
                            ins = nc.tensor.transpose(
                                psum[:, 2 + t // 2, (t % 2) * VAL + n * P:(t % 2) * VAL + (n + 1) * P],
                                th[:, 2 + n, tok], ident[:])
                    ins.then_inc(nat_ready, 1)
                    pe.wait_ge(nat_used, g + 1)
                    pe.wait_ge(v_used, g + 1)
                    pe.wait_ge(gate_used, g + 1)


def delta_decays(nc, psum, M):
    with ExitStack() as ctx:
        sb = lambda n, s, dt=F32: ctx.enter_context(nc.sbuf_tensor(f"dec_{n}", s, dt))
        sem = Semaphores(ctx, nc, "dec")
        z, na, u, s_, s2, po = (sb(n, [P, TILES, H]) for n in ("z", "na", "u", "s", "s2", "po"))
        expA = sb("expA", [P, H])
        tmp = sb("tmp", [P, TILES, H])
        tot = sb("tot", [P, TILES, H])
        dve_chain, act_ready, na_ready, pe_ready, g_ready, tot_ready = (
            sem(n) for n in ("dve_chain", "act_ready", "na_ready", "pe_ready", "g_ready", "tot_ready"))
        flat = lambda t: t[:].rearrange("p t h -> p (t h)")

        def bc(ap):
            return ap.unsqueeze(1).to_broadcast([P, TILES, H])

        with nc.Block() as block:
            @block.vector
            def _(dve):
                ch = Chain(dve, dve_chain, M.passed)
                v = nc.vector
                ch.link(v.tensor_tensor(z[:], M.ab[:, :, 0:H], bc(M.dtb[:]), ALU.add))
                ch.link(v.tensor_scalar(na[:], z[:], -1.0, None, ALU.mult))
                v.tensor_tensor(na[:], na[:], z[:], ALU.min).then_inc(na_ready, 1)
                dve.wait_ge(act_ready, 1)
                ch.link(v.tensor_scalar(s_[:], u[:], 2.0, None, ALU.add))
                ch.link(v.reciprocal(s_[:], s_[:]))
                ch.link(v.tensor_tensor(s_[:], s_[:], u[:], ALU.mult))
                ch.link(v.tensor_tensor(s2[:], s_[:], s_[:], ALU.mult))
                ch.link(v.tensor_scalar(po[:], s2[:], 1.0 / 17, 1.0 / 15, ALU.mult, ALU.add))
                for k in (13, 11, 9, 7, 5, 3, 1):
                    ch.link(v.tensor_tensor(po[:], po[:], s2[:], ALU.mult))
                    ch.link(v.tensor_scalar(po[:], po[:], 1.0 / k, None, ALU.add))
                ch.link(v.scalar_tensor_tensor(po[:], po[:], 2.0, s_[:], ALU.mult, ALU.mult))
                ch.link(v.scalar_tensor_tensor(po[:], z[:], 0.0, po[:], ALU.max, ALU.add))
                dve.wait_ge(act_ready, 3)
                ch.link(v.tensor_tensor(po[:], po[:], bc(expA[:]), ALU.mult))
                v.tensor_scalar(M.g[:], po[:], -1.0, -1000.0, ALU.mult, ALU.max).then_inc(g_ready, 1)
                ch.link(v.tensor_scalar(M.beta[:], tmp[:], 0.5, 0.5, ALU.mult, ALU.add))
                dve.wait_ge(tot_ready, 3)
                ch.link(v.tensor_tensor(tmp[:], tot[:], bc(M.hmask[:]), ALU.mult))
                ch.link(v.tensor_reduce(M.dec[:], tmp[:], AX.X, ALU.add))

            @block.scalar
            def _(act):
                act.wait_ge(na_ready, 1)
                nc.scalar.activation(u[:], na[:], ACT.Exp).then_inc(act_ready, 1)
                nc.scalar.activation(expA[:], M.alog[:], ACT.Exp).then_inc(act_ready, 1)
                nc.scalar.activation(tmp[:], M.ab[:, :, H:2 * H], ACT.Tanh, scale=0.5).then_inc(act_ready, 1)
                for n, dst in enumerate((M.gam, M.kap, tot)):
                    act.wait_ge(pe_ready, n + 1)
                    nc.scalar.activation(flat(dst), psum[:, n, 0:NQ], ACT.Exp).then_inc(tot_ready, 1)

            @block.tensor
            def _(pe):
                pe.wait_ge(g_ready, 1)
                for n, mask in enumerate((M.upto, M.after, M.ones)):
                    nc.tensor.matmul(psum[:, n, 0:NQ], mask[:], flat(M.g), start=True, stop=True)\
                        .then_inc(pe_ready, 1)

U = B * H
STEPS = TILES // B
LEVELS = 5


def delta_scan(nc, ident, psum, M):
    with ExitStack() as ctx:
        sb = lambda n, s, dt=F32: ctx.enter_context(nc.sbuf_tensor(f"sc_{n}", s, dt))
        sem = Semaphores(ctx, nc, "sc")
        ks, qs, kb, qg = (sb(n, [P, B, KEY]) for n in ("ks", "qs", "kb", "qg"))
        kt = sb("kt", [P, B, KEY])
        R = sb("R", [P, U, VD + KD])
        gL = sb("gL", [P, U, P])
        T4 = sb("T4", [P, B, 4, P])
        dec = sb("decays", [P, U, P])
        Lt, Ar, At = sb("Lt", [P, U, P]), sb("Ar", [P, U, P]), sb("At", [P, U, P])
        T, TT, X = sb("T", [P, U, 32]), sb("TT", [P, U, 32]), sb("X", [P, U, 32])
        T64 = sb("T64", [64, U, 64])
        X2, X3 = sb("X2", [P, U, 32]), sb("X3", [P, U, 64])
        TTf = sb("TTf", [P, U, P])
        Us, Wn, WT = sb("Us", [P, U, VD]), sb("Wn", [P, U, KD]), sb("WT", [P, B, P])
        Dl = sb("delta", [P, B, VAL])
        Sd, St = sb("state", [P, B, VAL]), sb("state_new", [P, B, VAL])
        dve_chain = sem("dve_chain")
        (staged, scaled, gl_ready, t4_ready, T4_ready, seg_ready, dec_ready, kk_ready, lt_ready, ar_ready, at_ready,
         x_ready, X_ready, y_ready, T_ready, x2_ready, X2_ready, X2b_ready, y2_ready, diag_ready, T64_ready, TT2_ready, x3_ready, X3_ready, y3_ready, TTf_ready,
         uw_ready, Us_ready, Wn_ready, wt_ready, WT_ready, ws_ready, delta_ready, o_ready, o_used, s_ready, S_ready,
         zeroed) = (sem(n) for n in (
            "staged scaled gl_ready t4_ready T4_ready seg_ready dec_ready kk_ready lt_ready ar_ready at_ready "
            "x_ready X_ready y_ready T_ready x2_ready X2_ready X2b_ready y2_ready diag_ready T64_ready TT2_ready x3_ready X3_ready y3_ready TTf_ready "
            "uw_ready Us_ready Wn_ready wt_ready WT_ready ws_ready delta_ready o_ready o_used s_ready S_ready "
            "zeroed").split())
        XB, YB = 0, 1

        def pair(t, i):
            return t[:].rearrange("p (b s) d -> p b s d", b=B)[:, :, bass.ds(i, 1), :].rearrange("p b s d -> p b (s d)")

        def heads(ap, k):
            return ap.rearrange("p b (h k) -> p b h k", k=k)

        def each(t, i, k):
            return pair(t, i).unsqueeze(3).to_broadcast([P, B, H, k])

        def all_units(ap):
            return ap.unsqueeze(1).to_broadcast([P, U, 32])

        def bank(n, w):
            return psum[:, n, 0:U * w].rearrange("p (u k) -> p u k", k=w)

        with nc.Block() as block:
            @block.gpsimd
            def _(pool):
                g_ = nc.gpsimd
                g_.memset(TTf[:], 0.0).then_inc(zeroed, 1)
                g_.memset(T64[:], 0.0).then_inc(zeroed, 1)
                g_.memset(Sd[:], 0.0).then_inc(zeroed, 1)
                pool.wait_ge(zeroed, 3)
                with pool.Fori(0, STEPS) as i:
                    for bb in range(B):
                        g_.tensor_tensor(
                            gL[:, bb * H:(bb + 1) * H, :], M.upto[:].unsqueeze(1).to_broadcast([P, H, P]),
                            pair(M.g, i)[:, bb, :].unsqueeze(2).to_broadcast([P, H, P]), ALU.mult).then_inc(gl_ready, 1)
                    for bb in range(B):
                        g_.tensor_tensor(heads(kb[:], KD)[:, bb], heads(pair(M.k, i), KD)[:, bb], each(M.beta, i, KD)[:, bb], ALU.mult)
                        g_.tensor_tensor(heads(qg[:], KD)[:, bb], heads(pair(M.q, i), KD)[:, bb], each(M.gam, i, KD)[:, bb], ALU.mult)\
                            .then_inc(scaled, 1)
                    for bb in range(B):
                        g_.tensor_tensor(heads(kt[:], KD)[:, bb], heads(pair(M.k, i), KD)[:, bb], each(M.kap, i, KD)[:, bb], ALU.mult)
                        g_.tensor_tensor(R[:, bb * H:(bb + 1) * H, 0:VD], heads(pair(M.v, i), VD)[:, bb], each(M.beta, i, VD)[:, bb], ALU.mult)
                    wait_alone(pool, M.passed, scaled, i * 4 + 2)
                    for bb in range(B):
                        g_.tensor_tensor(R[:, bb * H:(bb + 1) * H, VD:], heads(kb[:], KD)[:, bb], each(M.gam, i, KD)[:, bb], ALU.mult)\
                            .then_inc(scaled, 1)
                    wait_alone(pool, M.passed, ar_ready, i + 1)
                    for bb in range(B):
                        g_.affine_select(At[:, bb * H:(bb + 1) * H, :], Ar[:, bb * H:(bb + 1) * H, :], [[0, H], [1, P]], ALU.is_ge, 0.0,
                                         base=0, channel_multiplier=-1).then_inc(at_ready, 1)
                    wait_alone(pool, M.passed, T_ready, (i + 1) * LEVELS)
                    wait_alone(pool, M.passed, at_ready, (i + 1) * B)
                    for n in range(6):
                        blk = slice(32 * (n % 4), 32 * (n % 4) + 32)
                        dst, src = (TTf, TT) if n < 4 else (T64, T)
                        g_.tensor_copy(dst[blk, :, blk], src[blk]).then_inc(diag_ready, 1)
                        wait_alone(pool, M.passed, diag_ready, i * 6 + n + 1)
                    wait_alone(pool, M.passed, S_ready, (i + 1) * 2)

            @block.scalar
            def _(act):
                a_ = nc.scalar
                with act.Fori(0, STEPS) as i:
                    a_.activation(ks[:], pair(M.k, i), ACT.Copy)
                    a_.activation(qs[:], pair(M.q, i), ACT.Copy).then_inc(staged, 1)
                    for bb in range(B):
                        act.wait_ge(t4_ready, i * B + bb + 1)
                        a_.activation(T4[:, bb].rearrange("p a b -> p (a b)"), psum[:, bb, :], ACT.Copy).then_inc(T4_ready, 1)
                    for bb in range(B):
                        act.wait_ge(seg_ready, i * B + bb + 1)
                        a_.activation(dec[:, bb * H:(bb + 1) * H, :].rearrange("p a b -> p (a b)"), psum[:, 2 + bb, :], ACT.Exp)\
                            .then_inc(dec_ready, 1)
                    act.wait_ge(x2_ready, i + 1)
                    a_.activation(X2[96:128], bank(XB, 32)[96:128], ACT.Copy).then_inc(X2b_ready, 1)
                    act.wait_ge(y2_ready, i + 1)
                    a_.activation(T64[32:64, :, 0:32], bank(YB, 32)[32:64], ACT.Copy, scale=-1.0).then_inc(T64_ready, 1)
                    a_.activation(TTf[64:96, :, 96:128], bank(2, 32)[64:96], ACT.Copy, scale=-1.0).then_inc(TT2_ready, 1)
                    act.wait_ge(y3_ready, i + 1)
                    a_.activation(TTf[0:64, :, 64:128], bank(0, 64)[0:64], ACT.Copy, scale=-1.0).then_inc(TTf_ready, 1)
                    for bb in range(B):
                        act.wait_ge(uw_ready, i * B + bb + 1)
                        a_.activation(Wn[:, bb * H:(bb + 1) * H, :],
                                      psum[:, 1 + bb, 0:H * (VD + KD)].rearrange("p (u k) -> p u k", k=VD + KD)[:, :, VD:],
                                      ACT.Copy).then_inc(Wn_ready, 1)
                    act.wait_ge(wt_ready, i + 1)
                    a_.activation(WT[:].rearrange("p a b -> p (a b)"), psum[:, 3, 0:B * P], ACT.Copy).then_inc(WT_ready, 1)
                    act.wait_ge(o_ready, i + 1)
                    a_.activation(pair(M.v, i), psum[:, 6, :].rearrange("p (b v) -> p b v", b=B), ACT.Copy).then_inc(o_used, 1)
                    act.wait_ge(S_ready, (i + 1) * 2)

            @block.vector
            def _(dve):
                v = nc.vector
                ch = Chain(dve, dve_chain, M.passed)
                LINKS = LEVELS + 1
                dve.wait_ge(zeroed, 3)
                with dve.Fori(0, STEPS) as i:
                    ch.turn(i, LINKS)
                    dve.wait_ge(dec_ready, i * B + 2)
                    dve.wait_ge(kk_ready, i + 1)
                    for bb in range(B):
                        src = psum[:, 0:H, bb * 256:bb * 256 + P]
                        ins = v.tensor_tensor(Lt[:, bb * H:(bb + 1) * H, :], src, dec[:, bb * H:(bb + 1) * H, :], ALU.mult)
                    ins.then_inc(lt_ready, 1)
                    for bb in range(B):
                        src = psum[:, 0:H, bb * 256 + P:(bb + 1) * 256]
                        ins = v.tensor_tensor(Ar[:, bb * H:(bb + 1) * H, :], src, dec[:, bb * H:(bb + 1) * H, :], ALU.mult)
                    ins.then_inc(ar_ready, 1)
                    dve.wait_ge(x_ready, i * LEVELS + 1)
                    v.tensor_tensor(X[:], bank(XB, 32), all_units(M.level[:, 0, :]), ALU.mult).then_inc(X_ready, 1)
                    dve.wait_ge(X_ready, i * LEVELS + 1)
                    ch.link(v.tensor_tensor(T[:], all_units(M.eye32[:]), X[:], ALU.subtract))
                    v.transpose(TT[:], T[:]).then_inc(T_ready, 1)
                    for l in range(1, LEVELS):
                        dve.wait_ge(x_ready, i * LEVELS + l + 1)
                        v.tensor_tensor(X[:], bank(XB, 32), all_units(M.level[:, l, :]), ALU.mult).then_inc(X_ready, 1)
                        dve.wait_ge(y_ready, i * (LEVELS - 1) + l)
                        dve.wait_ge(T_ready, i * LEVELS + l)
                        ch.link(v.tensor_tensor(T[:], T[:], bank(YB, 32), ALU.subtract))
                        v.transpose(TT[:], T[:]).then_inc(T_ready, 1)
                    dve.wait_ge(x2_ready, i + 1)
                    v.tensor_copy(X2[32:64], bank(XB, 32)[32:64]).then_inc(X2_ready, 1)
                    dve.wait_ge(y2_ready, i + 1)
                    v.tensor_scalar(TTf[0:32, :, 32:64], bank(2, 32)[0:32], -1.0, None, ALU.mult).then_inc(TT2_ready, 1)
                    dve.wait_ge(x3_ready, i + 1)
                    v.tensor_copy(X3[64:128], bank(3, 64)[64:128]).then_inc(X3_ready, 1)
                    for bb in range(B):
                        dve.wait_ge(Wn_ready, i * B + bb + 1)
                        v.tensor_copy(Us[:, bb * H:(bb + 1) * H, :],
                                      psum[:, 1 + bb, 0:H * (VD + KD)].rearrange("p (u k) -> p u k", k=VD + KD)[:, :, 0:VD])\
                            .then_inc(Us_ready, 1)
                    dve.wait_ge(Us_ready, i * B + B)
                    dve.wait_ge(ws_ready, i + 1)
                    v.tensor_tensor(Dl[:].rearrange("p b v -> p (b v)"), Us[:].rearrange("p u v -> p (u v)"), psum[:, 5, :], ALU.subtract)\
                        .then_inc(delta_ready, 1)
                    dve.wait_ge(s_ready, i + 1)
                    ch.link(v.tensor_tensor(St[:], psum[:, 7, :].rearrange("p (b v) -> p b v", b=B),
                                            M.bmask[:].unsqueeze(1).to_broadcast([P, B, VAL]), ALU.mult))
                    for bb in range(B):
                        v.scalar_tensor_tensor(Sd[:, bb, :], Sd[:, bb, :], M.dec[:, bass.ds(bb * STEPS + i, 1)], St[:, bb, :],
                                               ALU.mult, ALU.add).then_inc(S_ready, 1)
                ch.leave(STEPS)

            @block.tensor
            def _(pe):
                mm = nc.tensor.matmul
                pe.wait_ge(zeroed, 3)

                def blocks(out_bank, left, right):
                    for u in range(U):
                        for n in range(4):
                            blk = slice(32 * n, 32 * n + 32)
                            ins = mm(bank(out_bank, 32)[blk, u, :], left(u, n, blk), right(u, blk), start=True, stop=True)
                    return ins

                with pe.Fori(0, STEPS) as i:
                    pe.wait_ge(staged, i + 1)
                    pe.wait_ge(scaled, i * 4 + 2)
                    for bb in range(B):
                        for n, t in enumerate((ks, kb, qs, qg)):
                            ins = nc.tensor.transpose(psum[:, bb, n * P:(n + 1) * P], t[:, bb, :], ident[:])
                        ins.then_inc(t4_ready, 1)
                    for bb in range(B):
                        pe.wait_ge(gl_ready, i * B + bb + 1)
                        mm(psum[:, 2 + bb, :], M.after[:], gL[:, bb * H:(bb + 1) * H, :].rearrange("p a b -> p (a b)"),
                           start=True, stop=True).then_inc(seg_ready, 1)
                    pe.wait_ge(T4_ready, (i + 1) * B)
                    pe.wait_ge(dec_ready, (i + 1) * B)
                    for bb in range(B):
                        for h in range(H):
                            rows = slice(32 * h, 32 * h + 32)
                            ins = mm(psum[:, h, bb * 256:(bb + 1) * 256], T4[rows, bb, 0, :],
                                     T4[rows, bb, 1:3, :].rearrange("p a b -> p (a b)"), start=True, stop=True)
                    ins.then_inc(kk_ready, 1)
                    wait_alone(pe, M.passed, lt_ready, i + 1)
                    wait_alone(pe, M.passed, ar_ready, i + 1)
                    blocks(XB, lambda u, n, blk: Lt[blk, u, blk], lambda u, blk: M.eye32[blk]).then_inc(x_ready, 1)
                    for l in range(1, LEVELS):
                        wait_alone(pe, M.passed, T_ready, i * LEVELS + l)
                        blocks(XB, lambda u, n, blk: Lt[blk, u, blk], lambda u, blk: T[blk, u, :]).then_inc(x_ready, 1)
                        wait_alone(pe, M.passed, X_ready, i * LEVELS + l + 1)
                        blocks(YB, lambda u, n, blk: TT[blk, u, :], lambda u, blk: X[blk, u, :]).then_inc(y_ready, 1)
                    wait_alone(pe, M.passed, T_ready, (i + 1) * LEVELS)
                    for u in range(U):
                        for n in (0, 2):
                            top, low = slice(32 * n, 32 * n + 32), slice(32 * n + 32, 32 * n + 64)
                            ins = mm(bank(XB, 32)[low, u, :], Lt[top, u, low], T[top, u, :], start=True, stop=True)
                    ins.then_inc(x2_ready, 1)
                    wait_alone(pe, M.passed, X2_ready, i + 1)
                    wait_alone(pe, M.passed, X2b_ready, i + 1)
                    for u in range(U):
                        mm(bank(YB, 32)[32:64, u, :], TT[32:64, u, :], X2[32:64, u, :], start=True, stop=True)
                    for u in range(U):
                        for n in (0, 2):
                            top, low = slice(32 * n, 32 * n + 32), slice(32 * n + 32, 32 * n + 64)
                            ins = mm(bank(2, 32)[top, u, :], X2[low, u, :], TT[low, u, :], start=True, stop=True)
                    ins.then_inc(y2_ready, 1)
                    wait_alone(pe, M.passed, T64_ready, i + 1)
                    wait_alone(pe, M.passed, diag_ready, i * 6 + 6)
                    wait_alone(pe, M.passed, TT2_ready, i * 2 + 2)
                    for u in range(U):
                        ins = mm(bank(3, 64)[64:128, u, :], Lt[0:64, u, 64:128], T64[0:64, u, :], start=True, stop=True)
                    ins.then_inc(x3_ready, 1)
                    wait_alone(pe, M.passed, X3_ready, i + 1)
                    for u in range(U):
                        ins = mm(bank(0, 64)[0:64, u, :], X3[64:128, u, :], TTf[64:128, u, 64:128], start=True, stop=True)
                    ins.then_inc(y3_ready, 1)
                    pe.wait_ge(TTf_ready, i + 1)
                    pe.wait_ge(scaled, i * 4 + 4)
                    for u in range(U):
                        ins = mm(psum[:, 1 + u // H, (u % H) * 96:(u % H + 1) * 96], TTf[:, u, :], R[:, u, :], start=True, stop=True)
                        if u % H == H - 1:
                            ins.then_inc(uw_ready, 1)
                    for bb in range(B):
                        pe.wait_ge(Wn_ready, i * B + bb + 1)
                        ins = nc.tensor.transpose(psum[:, 3, bb * P:(bb + 1) * P],
                                                  Wn[:, bb * H:(bb + 1) * H, :].rearrange("p u k -> p (u k)"), ident[:])
                    ins.then_inc(wt_ready, 1)
                    pe.wait_ge(WT_ready, i + 1)
                    for bb in range(B):
                        ins = mm(psum[:, 5, bb * VAL:(bb + 1) * VAL], WT[:, bb, :], Sd[:, bb, :], start=True, stop=True)
                    ins.then_inc(ws_ready, 1)
                    for bb in range(B):
                        mm(psum[:, 6, bb * VAL:(bb + 1) * VAL], T4[:, bb, 3, :], Sd[:, bb, :], start=(bb == 0), stop=False,
                           skip_group_check=True)
                    pe.wait_ge(delta_ready, i + 1)
                    for bb in range(B):
                        ins = mm(psum[:, 7, bb * VAL:(bb + 1) * VAL], kt[:, bb, :], Dl[:, bb, :], start=True, stop=True)
                    ins.then_inc(s_ready, 1)
                    pe.wait_ge(at_ready, (i + 1) * B)
                    for bb in range(B):
                        for h in range(H):
                            cols = slice(bb * VAL + h * VD, bb * VAL + (h + 1) * VD)
                            ins = mm(psum[:, 6, cols], At[:, bb * H + h, :], Dl[:, bb, h * VD:(h + 1) * VD],
                                     start=False, stop=True, skip_group_check=True)
                    ins.then_inc(o_ready, 1)
                    pe.wait_ge(o_used, i + 1)
                    pe.wait_ge(S_ready, (i + 1) * 2)


def delta_outputs(nc, X, ident, neg_half, psum, W, M):
    with ExitStack() as ctx:
        sb = lambda n, s, dt=F32: ctx.enter_context(nc.sbuf_tensor(f"out_{n}", s, dt))
        sem = Semaphores(ctx, nc, "out")
        sq, o1 = sb("sq", [P, GT, VAL]), sb("o1", [P, GT, VAL])
        ss, r, rt, nh, half = (sb(n, [P, GT * H]) for n in ("ss", "r", "rt", "nh", "half"))
        oT, hT = sb("oT", [P, 2, GW]), sb("hT", [P, GW])
        x1, y, z = sb("x1", [P, GT, D]), sb("y", [P, GT, D]), sb("z", [P, GT, D])
        stats, mv, r2 = sb("stats", [P, GT, 6]), sb("mv", [P, GT, 2]), sb("r2", [P, GT])
        dve_chain, consts = sem("dve_chain"), sem("consts")
        (sq_ready, ss_ready, r_ready, o1_ready, ot_ready, oT_ready, enc_ready, mv_ready, r2_ready, y_ready, ht_ready,
         hT_ready, z_ready, zb_ready, gelu_ready, x_done) = (sem(n) for n in (
            "sq_ready ss_ready r_ready o1_ready ot_ready oT_ready enc_ready mv_ready r2_ready y_ready ht_ready "
            "hT_ready z_ready zb_ready gelu_ready x_done").split())

        def tiles4(ap):
            return ap.unsqueeze(1).to_broadcast([P, GT, D])

        def by_head(ap):
            return ap.rearrange("p t (h v) -> p (t h) v", v=VD)

        with nc.Block() as block:
            @block.vector
            def _(dve):
                v = nc.vector
                ch = Chain(dve, dve_chain, W.passed)
                LINKS = 9
                with dve.Fori(0, GROUPS) as g:
                    ch.turn(g, LINKS)
                    rows = bass.ts(g, GT)
                    dve.wait_ge(sq_ready, g + 1)
                    v.tensor_reduce(ss[:], by_head(sq[:]), AX.X, ALU.add).then_inc(ss_ready, 1)
                    dve.wait_ge(r_ready, g * 3 + 3)
                    ch.link(v.tensor_tensor(by_head(o1[:]), by_head(M.v[:, rows, :]),
                                            r[:].unsqueeze(2).to_broadcast([P, GT * H, VD]), ALU.mult))
                    ch.link(v.tensor_tensor(by_head(o1[:]), by_head(o1[:]),
                                            M.onw[:].unsqueeze(1).to_broadcast([P, GT * H, VD]), ALU.mult))
                    v.tensor_tensor(o1[:], o1[:], M.gate[:, rows, :], ALU.mult).then_inc(o1_ready, 1)
                    dve.wait_ge(enc_ready, g + 1)
                    for t in range(GT):
                        tile = bass.ds(g * GT + t, 1)
                        ins = v.tensor_scalar(x1[:, t, :], X[:, tile, :].rearrange("p o d -> p (o d)"),
                                              M.mean[:, tile, :].rearrange("p o d -> p (o d)"), M.rstd[:, tile],
                                              ALU.subtract, ALU.mult)
                    ch.link(ins)
                    ch.link(v.tensor_tensor(x1[:], psum[:, 2, :].rearrange("p (t d) -> p t d", d=D), x1[:], ALU.add))
                    row_stats(nc, dve, ch, stats, mv, x1).then_inc(mv_ready, 1)
                    dve.wait_ge(r2_ready, g * 2 + 2)
                    for t in range(GT):
                        ins = v.tensor_scalar(y[:, t, :], x1[:, t, :], mv[:, t, 0:1], r2[:, t:t + 1], ALU.subtract, ALU.mult)
                    ch.link(ins)
                    ch.link(v.tensor_tensor(y[:], y[:], tiles4(M.ln2g[:]), ALU.mult))
                    v.tensor_tensor(y[:], y[:], tiles4(M.ln2b[:]), ALU.add).then_inc(y_ready, 1)
                    dve.wait_ge(z_ready, g + 1)
                    v.tensor_tensor(z[:], psum[:, 4, :].rearrange("p (t d) -> p t d", d=D), tiles4(M.b2[:]), ALU.add)\
                        .then_inc(zb_ready, 1)
                    ch.link(v.tensor_tensor(x1[:], x1[:], X[:, rows, :], ALU.add))
                    dve.wait_ge(gelu_ready, g + 1)
                    ch.link(v.tensor_tensor(X[:, rows, :], x1[:], z[:], ALU.add))
                ch.leave(GROUPS)

            @block.gpsimd
            def _(pool):
                nc.gpsimd.memset(nh[:], -0.5).then_inc(consts, 1)
                nc.gpsimd.memset(half[:], 0.5).then_inc(consts, 1)
                pool.wait_ge(consts, 2)
                with pool.Fori(0, GROUPS) as g:
                    wait_alone(pool, W.passed, ss_ready, g + 1)
                    inverse_root(nc, pool, W.passed, r_ready, g * 3, rt[:], ss[:], r[:], 1.0 / VD, RMS_EPS, nh[:])
                    wait_alone(pool, W.passed, r_ready, g * 3 + 2)
                    nc.gpsimd.tensor_tensor(r[:], rt[:], half[:], ALU.mult).then_inc(r_ready, 1)
                    wait_alone(pool, W.passed, mv_ready, g + 1)
                    inverse_root(nc, pool, W.passed, r2_ready, g * 2, r2[:], mv[:, :, 1], rt[:, 0:GT], 1.0, LN_EPS, neg_half[:])

            @block.scalar
            def _(act):
                with act.Fori(0, GROUPS) as g:
                    nc.scalar.activation(sq[:], M.v[:, bass.ts(g, GT), :], ACT.Square).then_inc(sq_ready, 1)
                    act.wait_ge(ot_ready, g + 1)
                    nc.scalar.activation(oT[:], psum[:, 0:2, :], ACT.Copy).then_inc(oT_ready, 1)
                    act.wait_ge(ht_ready, g + 1)
                    nc.scalar.activation(hT[:], psum[:, 3, :], ACT.Copy).then_inc(hT_ready, 1)
                    act.wait_ge(zb_ready, g + 1)
                    nc.scalar.activation(z[:], z[:], ACT.Gelu).then_inc(gelu_ready, 1)

            @block.tensor
            def _(pe):
                with pe.Fori(0, GROUPS) as g:
                    pe.wait_ge(o1_ready, g + 1)
                    for n in range(2):
                        for t in range(GT):
                            ins = nc.tensor.transpose(psum[:, n, t * P:(t + 1) * P], o1[:, t, n * P:(n + 1) * P], ident[:])
                    ins.then_inc(ot_ready, 1)
                    pe.wait_ge(oT_ready, g + 1)
                    for t in range(GT):
                        for n in range(2):
                            ins = nc.tensor.matmul(psum[:, 2, t * D:(t + 1) * D], oT[:, n, t * P:(t + 1) * P], M.wo[:, n, :],
                                                   start=(n == 0), stop=(n == 1))
                    ins.then_inc(enc_ready, 1)
                    pe.wait_ge(y_ready, g + 1)
                    for t in range(GT):
                        ins = nc.tensor.transpose(psum[:, 3, t * P:(t + 1) * P], y[:, t, :], ident[:])
                    ins.then_inc(ht_ready, 1)
                    pe.wait_ge(hT_ready, g + 1)
                    for t in range(GT):
                        ins = nc.tensor.matmul(psum[:, 4, t * D:(t + 1) * D], hT[:, t * P:(t + 1) * P], M.w2[:],
                                               start=True, stop=True)
                    ins.then_inc(z_ready, 1)


def gated_delta(nc, X, ident, neg_half, psum, W, A):
    with ExitStack() as ctx:
        sb = lambda n, s, dt=F32: ctx.enter_context(nc.sbuf_tensor(f"gd_{n}", s, dt))
        M = Holder()
        M.passed = W.passed
        M.mean, M.rstd = sb("mean", [P, TILES, 1]), sb("rstd", [P, TILES])
        M.q, M.k = sb("q", [P, TILES, KEY]), sb("k", [P, TILES, KEY])
        M.v, M.gate = sb("v", [P, TILES, VAL]), sb("gate", [P, TILES, VAL])
        M.ab = sb("ab", [P, TILES, 2 * H])
        M.g, M.beta, M.gam, M.kap = (sb(n, [P, TILES, H]) for n in ("g", "beta", "gam", "kap"))
        M.dec = sb("dec", [P, TILES])
        M.wq, M.wk, M.wv, M.wg = sb("wq", [P, KEY]), sb("wk", [P, KEY]), sb("wv", [P, VAL]), sb("wg", [P, VAL])
        M.wab, M.wo, M.w2 = sb("wab", [P, 2 * H]), sb("wo", [P, 2, D]), sb("w2", [P, D])
        M.ln1g, M.ln1b, M.ln2g, M.ln2b, M.b2 = (sb(n, [P, D]) for n in ("ln1g", "ln1b", "ln2g", "ln2b", "b2"))
        M.rmsw, M.convw, M.onw = sb("rmsw", [P, 1]), sb("convw", [P, 4, CONV]), sb("onw", [P, VD])
        M.dtb, M.alog = sb("dtb", [P, H]), sb("alog", [P, H])
        consts = sb("masks", [P, MASK_COLS])
        M.upto, M.after, M.ones = (consts[:, n * P:(n + 1) * P] for n in range(3))
        M.bmask, M.hmask = consts[:, 384:640], consts[:, 640:644]
        M.eye32, M.level = consts[:, 644:676], consts[:, 676:836].rearrange("p (l k) -> p l k", k=32)
        a = lambda n: A[f"L1_attn_{n}"]
        row = lambda n: a(n).partition_broadcast(P)
        M.loads = [
            (M.wq[:], a("Wq")), (M.wk[:], a("Wk")), (M.wv[:], a("Wv")), (M.wg[:], a("Wg")),
            (M.wab[:, 0:H], a("Wa")), (M.wab[:, H:], a("Wb")), (M.wo[:], a("Wo").rearrange("(n p) d -> p n d", p=P)),
            (M.w2[:], a("W2")), (M.ln1g[:], row("ln1_g")), (M.ln1b[:], row("ln1_b")), (M.ln2g[:], row("ln2_g")),
            (M.ln2b[:], row("ln2_b")), (M.b2[:], row("b2")), (M.rmsw[:], a("rms_in_w").unsqueeze(1)),
            (M.convw[:, 0, :], a("conv_q_w")), (M.convw[:, 1, :], a("conv_k_w")),
            (M.convw[:, 2:4, :], a("conv_v_w").rearrange("(n p) i -> p n i", p=P)), (M.onw[:], row("o_norm_w")),
            (M.dtb[:], row("dt_bias")), (M.alog[:], row("A_log")), (consts[:], A["masks"]),
        ]
        M.n_loads = len(M.loads)
        delta_inputs(nc, X, ident, neg_half, psum, W, M)
        delta_decays(nc, psum, M)
        delta_scan(nc, ident, psum, M)
        delta_outputs(nc, X, ident, neg_half, psum, W, M)

MASK_COLS = 836


def masks():
    import numpy as np
    r, c = np.arange(P)[:, None], np.arange(P)[None, :]
    upto, after, ones = r <= c, r > c, np.ones((P, P))
    bmask = (r // KD) == (np.arange(VAL)[None, :] // VD)
    hmask = (r // KD) == np.arange(H)[None, :]
    c32 = np.arange(32)[None, :]
    eye = (r % 32) == c32
    level = [(((r % 32) // n) % 2 == 1) & (c32 // n == (r % 32) // n - 1) for n in (1, 2, 4, 8, 16)]
    return np.concatenate([upto, after, ones, bmask, hmask, eye] + level, axis=1).astype(np.float32)


def build(nc, A, out, phases=(0,1,2,3,4,5)):
    ctx = ExitStack()
    with ctx:
        sb = lambda n, s, dt=F32: ctx.enter_context(nc.sbuf_tensor(n, s, dt))
        sem = lambda n: ctx.enter_context(nc.semaphore(n))
        X = sb("X", [P, TILES, D])
        ident = sb("ident", [P, P])
        neg_half = sb("neg_half", [P, GT])
        psum = ctx.enter_context(nc.psum_tensor("psum", [P, 8, 512], F32))
        W = Holder()
        W.passed = sem("passed")
        rw = sb("rw", [P, E])
        W.ewh, W.ewl = sb("ewh", [P, E * D], F32R), sb("ewl", [P, E * D], F32R)
        W.rwh, W.rwl = sb("rwh", [P, E], F32R), sb("rwl", [P, E], F32R)
        W.rb, W.rank, W.eb = sb("rb", [P, E]), sb("rank", [P, E]), sb("eb", [E, D])
        wraw = sb("wraw", [P, 3, D])
        gw, b1raw = sb("gw", [P, E]), sb("b1raw", [E * FC, P])
        W.gwh, W.gwl, W.gb, W.b1T = sb("gwh", [P, E], F32R), sb("gwl", [P, E], F32R), sb("gb", [P, E]), sb("b1T", [P, E * FC])
        b1T_ready = sem("b1T_ready")
        W.wqh, W.wkh, W.wvh = (sb(n, [P, D], F32R) for n in ("wqh", "wkh", "wvh"))
        W.wql, W.wkl, W.wvl = (sb(n, [P, D], F32R) for n in ("wql", "wkl", "wvl"))
        W.bq, W.bk, W.bvb = sb("bq", [P, 1]), sb("bk", [P, 1]), sb("bvb", [P, D])
        qkvT_ready, ident_ready = sem("qkvT_ready"), sem("ident_ready")
        x_loaded, w_loaded = sem("x_loaded"), sem("w_loaded")
        consts_ready, ident_zero, ranks = sem("consts_ready"), sem("ident_zero"), sem("ranks")
        w_high, w_low = sem("w_high"), sem("w_low")

        x_dram = A["L0_attn_x"].rearrange("b (t p) d -> p (b t) d", p=P)
        with nc.sbuf_tensor("ew", [P, E * D], F32) as ew, nc.Block() as block:
            @block.sync
            def _(sp):
                sp.dma_start(ew[:].rearrange("p (e d) -> p e d", d=D),
                             A["L0_ffn_expert_w"].rearrange("e h d -> h e d")).then_inc(w_loaded, 16)
                sp.dma_start(rw[:], A["L0_ffn_router_w"]).then_inc(w_loaded, 16)
                sp.dma_start(W.rb[:], A["L0_ffn_router_b"].partition_broadcast(P)).then_inc(w_loaded, 16)
                sp.dma_start(W.eb[:], A["L0_ffn_expert_b"]).then_inc(w_loaded, 16)
                for n, w in enumerate(("wq", "wk", "wv")):
                    sp.dma_start(wraw[:, n, :], A[f"L0_attn_{w}"]).then_inc(w_loaded, 16)
                sp.dma_start(W.bq[:], A["L0_attn_bq"].unsqueeze(1)).then_inc(w_loaded, 16)
                sp.dma_start(W.bk[:], A["L0_attn_bk"].unsqueeze(1)).then_inc(w_loaded, 16)
                sp.dma_start(W.bvb[:], A["L0_attn_bv"].partition_broadcast(P)).then_inc(w_loaded, 16)
                sp.dma_start(gw[:], A["L1_ffn_gate_w"]).then_inc(w_loaded, 16)
                sp.dma_start(W.gb[:], A["L1_ffn_gate_b"].partition_broadcast(P)).then_inc(w_loaded, 16)
                sp.dma_start(b1raw[:], A["L1_ffn_b1"].rearrange("e (c p) -> (e c) p", p=P)).then_inc(w_loaded, 16)
                sp.dma_start(X[:], x_dram).then_inc(x_loaded, 16)

            @block.gpsimd
            def _(pool):
                nc.gpsimd.memset(ident[:], 0.0).then_inc(ident_zero, 1)
                pool.wait_ge(ident_zero, 1)
                nc.gpsimd.affine_select(ident[:], ident[:], [[-1, P]], ALU.not_equal, 1.0, base=0,
                                        channel_multiplier=1).then_inc(consts_ready, 1)
                nc.gpsimd.memset(neg_half[:], -0.5).then_inc(consts_ready, 1)
                for e in range(E):
                    nc.gpsimd.memset(W.rank[:, e:e + 1], float(E - e)).then_inc(consts_ready, 1)
                pool.wait_ge(x_loaded, 16)

            @block.scalar
            def _(act):
                act.wait_ge(w_loaded, 208)
                nc.scalar.activation(W.ewh[:], ew[:], ACT.Copy).then_inc(w_high, 1)
                nc.scalar.activation(W.rwh[:], rw[:], ACT.Copy).then_inc(w_high, 1)
                nc.scalar.activation(W.gwh[:], gw[:], ACT.Copy).then_inc(w_high, 1)
                act.wait_ge(b1T_ready, 1)
                nc.scalar.activation(W.b1T[:], psum[:, 1, 0:E * FC], ACT.Copy)
                act.wait_ge(qkvT_ready, 1)
                for n, h in enumerate((W.wqh, W.wkh, W.wvh)):
                    nc.scalar.activation(h[:], psum[:, 0, n * D:(n + 1) * D], ACT.Copy).then_inc(w_high, 1)

            @block.tensor
            def _(pe):
                pe.wait_ge(w_loaded, 208)
                pe.wait_ge(consts_ready, 1)
                nc.tensor.transpose(psum[:, 1, 0:E * FC], b1raw[:], ident[0:E * FC, 0:E * FC]).then_inc(b1T_ready, 1)
                for n in range(3):
                    ins = nc.tensor.transpose(psum[:, 0, n * D:(n + 1) * D], wraw[:, n, :], ident[:])
                ins.then_inc(qkvT_ready, 1)

            @block.vector
            def _(dve):
                dve.wait_ge(w_high, 2)
                nc.vector.tensor_tensor(W.ewl[:], ew[:], W.ewh[:].bitcast(F32), ALU.subtract).then_inc(w_low, 1)
                nc.vector.tensor_tensor(W.rwl[:], rw[:], W.rwh[:].bitcast(F32), ALU.subtract).then_inc(w_low, 1)
                dve.wait_ge(w_high, 3)
                nc.vector.tensor_tensor(W.gwl[:], gw[:], W.gwh[:].bitcast(F32), ALU.subtract).then_inc(w_low, 1)
                dve.wait_ge(w_high, 6)
                for n, (h, l) in enumerate(((W.wqh, W.wql), (W.wkh, W.wkl), (W.wvh, W.wvl))):
                    nc.vector.tensor_tensor(l[:], psum[:, 0, n * D:(n + 1) * D], h[:].bitcast(F32),
                                            ALU.subtract).then_inc(w_low, 1)

        loaded = lambda dve: dve.wait_ge(x_loaded, 16)
        for p in phases:
            if p == 0:
                first_mixture(nc, "mix1", X, ident, neg_half, psum, W, loaded)
            if p == 1:
                attention(nc, "attn", X, ident, neg_half, psum, W)
            if p in (3, 5):
                second_mixture(nc, f"ffn{p}", X, ident, neg_half, psum, W, A)
            if p == 4:
                gated_delta(nc, X, ident, neg_half, psum, W, A)
            if p == 2:
                first_mixture(nc, "mix2", X, ident, neg_half, psum, W, loaded)
        stored = sem("stored")
        with nc.Block() as block:
            @block.sync
            def _(sp):
                sp.dma_start(out.rearrange("b (t p) d -> p (b t) d", p=P), X[:]).then_inc(stored, 16)
                sp.wait_ge(stored, 16)


_L1_ATTN = ["ln1_g", "ln1_b", "ln2_g", "ln2_b", "rms_in_w", "Wq", "Wk", "Wv", "conv_q_w", "conv_k_w", "conv_v_w",
            "Wa", "dt_bias", "A_log", "Wb", "Wg", "o_norm_w", "Wo", "W2", "b2"]
_INS = (["L0_attn_" + n for n in ("x", "wq", "bq", "wk", "bk", "wv", "bv")]
        + ["L0_ffn_" + n for n in ("router_w", "router_b", "expert_w", "expert_b")]
        + ["L1_attn_" + n for n in _L1_ATTN]
        + ["L1_ffn_" + n for n in ("gate_w", "gate_b", "w1", "b1", "w2", "b2")])


def kernel(**inputs):
    import numpy as _np
    import concourse.bacc as _bacc
    from concourse import mybir as _mybir
    from concourse.bass_utils import run_bass_kernel_spmd as _run

    nc = _bacc.Bacc("TRN2", target_bir_lowering=False, num_devices=1)
    arrays, access = {}, {}
    for name in _INS + ["masks"]:
        a = masks() if name == "masks" else _np.ascontiguousarray(inputs[name])
        arrays[f"in_{name}_dram"] = a
        access[name] = nc.dram_tensor(f"in_{name}_dram", a.shape, _mybir.dt.from_np(a.dtype),
                                      kind="ExternalInput").ap()
    out = nc.dram_tensor("out_0_dram", (B, S, D), _mybir.dt.float32, kind="ExternalOutput").ap()
    build(nc, access, out)
    r = _run(nc, [arrays], core_ids=[0])
    return r.results[0]["out_0_dram"]
```

```python
import concourse.bass as bass
from concourse import mybir
from contextlib import ExitStack

F32 = mybir.dt.float32
F32R = mybir.dt.float32r
ALU = mybir.AluOpType
ACT = mybir.ActivationFunctionType
AX = mybir.AxisListType

P = 128
B, S, D = 2, 2048, 128
TILES = B * S // P
GT = 4
GROUPS = TILES // GT
GW = GT * P
E = 8
F = 512
FC = F // P
LN_EPS = 1e-5


def wait_alone(eng, passed, sem, value):
    eng.wait_ge(sem, value)
    eng.sem_inc(passed, 1)


class Semaphores:

    def __init__(self, ctx, nc, name):
        self.nc, self.name, self.held, self.stack = nc, name, [], ExitStack()
        ctx.callback(self.clear)

    def __call__(self, name):
        self.held.append(self.stack.enter_context(self.nc.semaphore(f"{self.name}_{name}")))
        return self.held[-1]

    def clear(self):
        with self.nc.Block() as block:
            @block.gpsimd
            def _(pool):
                numbers = sorted(s.num for s in self.held)
                while numbers:
                    n = 1
                    while n < len(numbers) and numbers[n] == numbers[0] + n:
                        n += 1
                    pool.sem_clear(range(numbers[0], numbers[0] + n))
                    numbers = numbers[n:]
        self.stack.close()


class Chain:

    def __init__(self, eng, sem, passed=None):
        self.eng, self.sem, self.base, self.n, self.outer = eng, sem, 0, 0, []
        self.passed = passed

    def turn(self, i, per):
        self.outer.append((self.base, self.n, per))
        self.base, self.n = self.base + self.n + i * per, 0

    def leave(self, count):
        base, n, per = self.outer.pop()
        assert self.n == per, ("links in a pass", self.n, per)
        self.base, self.n = base, n + count * per

    def mark(self, ins):
        ins.then_inc(self.sem, 1)
        self.n += 1
        return self.base + self.n

    def link(self, ins):
        self.eng.wait_ge(self.sem, self.mark(ins))

    def link_alone(self, ins):
        wait_alone(self.eng, self.passed, self.sem, self.mark(ins))


def three_products(pe_nc, out, left, right, start=True, stop=True, skip=False):
    (lh, ll), (rh, rl) = left, right
    for n, (a, b) in enumerate(((lh, rh), (lh, rl), (ll, rh))):
        ins = pe_nc.tensor.matmul(out, a, b, start=(start and n == 0), stop=(stop and n == 2),
                                  skip_group_check=skip)
    return ins


class WholeFront:

    PARTS = slice(0, 2 * GT), slice(2 * GT, TILES)

    def __init__(self, ctx, sem, nc, name, X, ident, psum, banks, passed):
        self.nc, self.X, self.ident, self.psum, self.banks, self.passed = nc, X, ident, psum, banks, passed
        sb = lambda n, s, dt=F32: ctx.enter_context(nc.sbuf_tensor(f"{name}_{n}", s, dt))
        self.stats, self.mv = sb("stats", [P, TILES, 6]), sb("mean_var", [P, TILES, 2])
        self.veps, self.rstd, self.power = sb("var_eps", [P, TILES]), sb("rstd", [P, TILES]), sb("power", [P, TILES])
        self.xn = sb("xn", [P, 2, GT, D])
        self.power_ready, self.var_ready, self.veps_ready, self.rstd_ready = (
            sem("power_ready"), sem("var_ready"), sem("veps_ready"), sem("rstd_ready"))
        self.xn_ready, self.xt_ready = sem("xn_ready"), sem("xt_ready")

    def rows(self, g):
        return self.X[:, bass.ts(g, GT), :]

    def vector_stats(self, dve, chain):
        nc = self.nc
        for part in self.PARTS:
            for t in range(part.start, part.stop):
                ins = nc.vector.bn_stats(self.stats[:, t, :], self.X[:, t, :])
            chain.link(ins)
            for t in range(part.start, part.stop):
                ins = nc.vector.bn_aggr(self.mv[:, t, :], self.stats[:, t, :])
            ins.then_inc(self.var_ready, 1)

    def gpsimd_rstd(self, pool):
        nc = self.nc
        nc.gpsimd.memset(self.power[:], -0.5).then_inc(self.power_ready, 1)
        pool.wait_ge(self.power_ready, 1)
        for n, part in enumerate(self.PARTS):
            pool.wait_ge(self.var_ready, n + 1)
            nc.gpsimd.tensor_scalar(self.veps[:, part], self.mv[:, part, 1], LN_EPS, None, ALU.add)\
                .then_inc(self.veps_ready, 1)
            pool.wait_ge(self.veps_ready, n + 1)
            nc.gpsimd.tensor_tensor(self.rstd[:, part], self.veps[:, part], self.power[:, part], ALU.pow)\
                .then_inc(self.rstd_ready, 1)

    def vector_normalize(self, dve, g, par, first=False):
        if first:
            dve.wait_ge(self.rstd_ready, 1)
        else:
            dve.wait_ge(self.rstd_ready, 2)
            dve.wait_ge(self.xt_ready, g - 1)
        for t in range(GT):
            tile = bass.ds(g * GT + t, 1)
            row = lambda ap: ap.rearrange("p o d -> p (o d)")
            ins = self.nc.vector.tensor_scalar(self.xn[:, par, t, :], row(self.X[:, tile, :]),
                                               row(self.mv[:, tile, 0:1]), self.rstd[:, tile],
                                               ALU.subtract, ALU.mult)
        ins.then_inc(self.xn_ready, 1)

    def tensor_transpose(self, pe, g, par):
        pe.wait_ge(self.xn_ready, g + 1)
        for t in range(GT):
            ins = self.nc.tensor.transpose(self.psum[:, self.banks[par], t * P:(t + 1) * P],
                                           self.xn[:, par, t, :], self.ident[:])
        ins.then_inc(self.xt_ready, 1)


class WholeFront:

    PARTS = slice(0, 2 * GT), slice(2 * GT, TILES)

    def __init__(self, ctx, sem, nc, name, X, ident, psum, banks, passed):
        self.nc, self.X, self.ident, self.psum, self.banks, self.passed = nc, X, ident, psum, banks, passed
        sb = lambda n, s, dt=F32: ctx.enter_context(nc.sbuf_tensor(f"{name}_{n}", s, dt))
        self.stats, self.mv = sb("stats", [P, TILES, 6]), sb("mean_var", [P, TILES, 2])
        self.veps, self.rstd, self.power = sb("var_eps", [P, TILES]), sb("rstd", [P, TILES]), sb("power", [P, TILES])
        self.xn = sb("xn", [P, 2, GT, D])
        self.power_ready, self.var_ready, self.veps_ready, self.rstd_ready = (
            sem("power_ready"), sem("var_ready"), sem("veps_ready"), sem("rstd_ready"))
        self.xn_ready, self.xt_ready = sem("xn_ready"), sem("xt_ready")

    def rows(self, g):
        return self.X[:, bass.ts(g, GT), :]

    def vector_stats(self, dve, chain):
        nc = self.nc
        for part in self.PARTS:
            for t in range(part.start, part.stop):
                ins = nc.vector.bn_stats(self.stats[:, t, :], self.X[:, t, :])
            chain.link(ins)
            for t in range(part.start, part.stop):
                ins = nc.vector.bn_aggr(self.mv[:, t, :], self.stats[:, t, :])
            ins.then_inc(self.var_ready, 1)

    def gpsimd_rstd(self, pool):
        nc = self.nc
        nc.gpsimd.memset(self.power[:], -0.5).then_inc(self.power_ready, 1)
        pool.wait_ge(self.power_ready, 1)
        for n, part in enumerate(self.PARTS):
            pool.wait_ge(self.var_ready, n + 1)
            nc.gpsimd.tensor_scalar(self.veps[:, part], self.mv[:, part, 1], LN_EPS, None, ALU.add)\
                .then_inc(self.veps_ready, 1)
            pool.wait_ge(self.veps_ready, n + 1)
            nc.gpsimd.tensor_tensor(self.rstd[:, part], self.veps[:, part], self.power[:, part], ALU.pow)\
                .then_inc(self.rstd_ready, 1)

    def vector_normalize(self, dve, g, par, first=False):
        if first:
            dve.wait_ge(self.rstd_ready, 1)
        else:
            dve.wait_ge(self.rstd_ready, 2)
            dve.wait_ge(self.xt_ready, g - 1)
        for t in range(GT):
            tile = bass.ds(g * GT + t, 1)
            row = lambda ap: ap.rearrange("p o d -> p (o d)")
            ins = self.nc.vector.tensor_scalar(self.xn[:, par, t, :], row(self.X[:, tile, :]),
                                               row(self.mv[:, tile, 0:1]), self.rstd[:, tile],
                                               ALU.subtract, ALU.mult)
        ins.then_inc(self.xn_ready, 1)

    def tensor_transpose(self, pe, g, par):
        pe.wait_ge(self.xn_ready, g + 1)
        for t in range(GT):
            ins = self.nc.tensor.transpose(self.psum[:, self.banks[par], t * P:(t + 1) * P],
                                           self.xn[:, par, t, :], self.ident[:])
        ins.then_inc(self.xt_ready, 1)


class Router(WholeFront):

    def __init__(self, ctx, sem, nc, name, X, ident, psum, W, router_w, router_b):
        super().__init__(ctx, sem, nc, name, X, ident, psum, (0, 1), W.passed)
        sb = lambda n, s, dt=F32: ctx.enter_context(nc.sbuf_tensor(f"{name}_{n}", s, dt))
        self.W, self.router_w, self.router_b = W, router_w, router_b
        self.LOGITS, self.CT, self.BIAS = (6, 7), 6, (6, 7)
        self.xh, self.xl = sb("xh", [P, GROUPS, GW], F32R), sb("xl", [P, GROUPS, GW], F32R)
        self.xT = sb("xT", [P, 2, GW])
        self.lg, self.ex = sb("logits", [P, TILES, E]), sb("exps", [P, TILES, E])
        self.one, self.two, self.tmp = (sb(n, [P, TILES, E]) for n in ("one", "two", "tmp"))
        self.top, self.tot, self.pick = (sb(n, [P, TILES]) for n in ("top", "total", "pick"))
        self.coef = sb("coef", [P, TILES, E])
        self.coefT = sb("coefT", [P, 2, P])
        self.bdiag = sb("bdiag", [P, TILES // 2 * D])
        self.diag_zero, self.bias_loaded = sem("diag_zero"), sem("bias_loaded")
        self.high_ready, self.xT_ready, self.low_ready = sem("high_ready"), sem("xT_ready"), sem("low_ready")
        self.logits_ready, self.logits_used = sem("logits_ready"), sem("logits_used")
        self.shifted_ready, self.exp_ready, self.coef_ready = sem("shifted_ready"), sem("exp_ready"), sem("coef_ready")
        self.ct_ready, self.coefT_ready, self.bias_ready, self.bias_used = (
            sem("ct_ready"), sem("coefT_ready"), sem("bias_ready"), sem("bias_used"))

    def flat(self, t, g):
        return t[:, bass.ds(g, 1), :].rearrange("p o d -> p (o d)")

    def each(self, ap):
        return ap.unsqueeze(2).to_broadcast([P, TILES, E])

    def vector_front(self, dve, chain):
        nc = self.nc

        def low(g, par):
            dve.wait_ge(self.high_ready, g + 1)
            nc.vector.tensor_tensor(self.flat(self.xl, g), self.psum[:, self.banks[par], :],
                                    self.flat(self.xh, g).bitcast(F32), ALU.subtract).then_inc(self.low_ready, 1)

        def add_bias(g, par):
            dve.wait_ge(self.logits_ready, g + 1)
            nc.vector.tensor_tensor(
                self.lg[:, bass.ts(g, GT), :],
                self.psum[:, self.LOGITS[par], 0:GT * E].rearrange("p (t e) -> p t e", e=E),
                self.router_b.unsqueeze(1).to_broadcast([P, GT, E]), ALU.add).then_inc(self.logits_used, 1)

        self.vector_stats(dve, chain)
        self.vector_normalize(dve, 0, 0, first=True)
        self.vector_normalize(dve, 1, 1, first=True)
        low(0, 0)
        with dve.Fori(0, GROUPS // 2 - 1) as j:
            for par in range(2):
                self.vector_normalize(dve, j * 2 + par + 2, par)
                low(j * 2 + par + 1, 1 - par)
                add_bias(j * 2 + par, par)
        low(GROUPS - 1, 1)
        add_bias(GROUPS - 2, 0)
        add_bias(GROUPS - 1, 1)
        dve.wait_ge(self.logits_used, GROUPS)

    def vector_first(self, chain, mask):
        v, rank = self.nc.vector, self.W.rank[:].unsqueeze(1).to_broadcast([P, TILES, E])
        chain.link(v.tensor_tensor(mask[:], mask[:], rank, ALU.mult))
        chain.link(v.tensor_reduce(self.pick[:], mask[:], AX.X, ALU.max))
        chain.link(v.tensor_tensor(mask[:], mask[:], self.each(self.pick[:]), ALU.is_equal))

    def vector_best(self, chain):
        v = self.nc.vector
        chain.link(v.tensor_reduce(self.top[:], self.lg[:], AX.X, ALU.max))
        v.tensor_tensor(self.ex[:], self.lg[:], self.each(self.top[:]), ALU.subtract).then_inc(self.shifted_ready, 1)
        chain.link(v.tensor_tensor(self.one[:], self.lg[:], self.each(self.top[:]), ALU.is_equal))
        self.vector_first(chain, self.one)

    def vector_top1(self, dve, chain):
        v = self.nc.vector
        self.vector_best(chain)
        dve.wait_ge(self.exp_ready, 1)
        chain.link(v.tensor_reduce(self.tot[:], self.ex[:], AX.X, ALU.add))
        chain.link(v.reciprocal(self.top[:], self.tot[:]))
        v.scalar_tensor_tensor(self.coef[:], self.one[:], 0.5, self.each(self.top[:]), ALU.mult, ALU.mult)\
            .then_inc(self.coef_ready, 1)
        dve.wait_ge(self.coef_ready, 1)

    def vector_top2(self, dve, chain):
        v, one, two, tmp, ex = self.nc.vector, self.one, self.two, self.tmp, self.ex
        self.vector_best(chain)
        chain.link(v.scalar_tensor_tensor(tmp[:], one[:], -3e38, self.lg[:], ALU.mult, ALU.add))
        chain.link(v.tensor_reduce(self.top[:], tmp[:], AX.X, ALU.max))
        chain.link(v.tensor_tensor(two[:], tmp[:], self.each(self.top[:]), ALU.is_equal))
        self.vector_first(chain, two)
        chain.link(v.tensor_tensor(one[:], one[:], two[:], ALU.add))
        dve.wait_ge(self.exp_ready, 1)
        chain.link(v.tensor_tensor(one[:], one[:], ex[:], ALU.mult))
        chain.link(v.tensor_reduce(self.tot[:], one[:], AX.X, ALU.add))
        chain.link(v.reciprocal(self.top[:], self.tot[:]))
        v.scalar_tensor_tensor(self.coef[:], one[:], 0.5, self.each(self.top[:]), ALU.mult, ALU.mult)\
            .then_inc(self.coef_ready, 1)
        dve.wait_ge(self.coef_ready, 1)

    def vector_bias(self, dve, g):
        dve.wait_ge(self.bias_ready, g + 1)
        x = self.rows(g)
        self.nc.vector.tensor_tensor(x, self.psum[:, self.BIAS[g % 2], :].rearrange("p (t d) -> p t d", d=D), x,
                                     ALU.add).then_inc(self.bias_used, 1)

    def gpsimd_front(self, pool):
        self.gpsimd_rstd(pool)
        self.nc.gpsimd.memset(self.bdiag[:], 0.0).then_inc(self.diag_zero, 1)

    def sync_bias(self, sp, bias):
        sp.wait_ge(self.diag_zero, 1)
        for t in range(TILES // 2):
            sp.dma_start(self.bdiag[t * E:(t + 1) * E, t * D:(t + 1) * D], bias).then_inc(self.bias_loaded, 16)

    def scalar_front(self, act):
        nc = self.nc

        def parts(g, par):
            act.wait_ge(self.xt_ready, g + 1)
            nc.scalar.activation(self.xT[:, par, :], self.psum[:, self.banks[par], :], ACT.Copy)\
                .then_inc(self.xT_ready, 1)
            nc.scalar.activation(self.flat(self.xh, g), self.psum[:, self.banks[par], :], ACT.Copy)\
                .then_inc(self.high_ready, 1)

        with act.Fori(0, GROUPS // 2) as j:
            parts(j * 2, 0)
            parts(j * 2 + 1, 1)

    def scalar_exp(self, act):
        act.wait_ge(self.shifted_ready, 1)
        self.nc.scalar.activation(self.ex[:], self.ex[:], ACT.Exp).then_inc(self.exp_ready, 1)

    def scalar_coef_rows(self, act):
        act.wait_ge(self.ct_ready, 1)
        self.nc.scalar.activation(self.coefT[:].rearrange("p a b -> p (a b)"), self.psum[:, self.CT, 0:2 * P], ACT.Copy)\
            .then_inc(self.coefT_ready, 1)

    def tensor_front(self, pe):
        nc = self.nc

        def logits(g, par, first=False):
            pe.wait_ge(self.xT_ready, g + 1)
            if not first:
                pe.wait_ge(self.logits_used, g - 1)
            for t in range(GT):
                tok = slice(t * P, (t + 1) * P)
                ins = nc.tensor.matmul(self.psum[:, self.LOGITS[par], t * E:(t + 1) * E], self.xT[:, par, tok],
                                       self.router_w, start=True, stop=True)
            ins.then_inc(self.logits_ready, 1)

        self.tensor_transpose(pe, 0, 0)
        self.tensor_transpose(pe, 1, 1)
        for par in range(2):
            logits(par, par, first=True)
            pe.wait_ge(self.low_ready, par + 1)
            self.tensor_transpose(pe, par + 2, par)
        with pe.Fori(1, GROUPS // 2 - 1) as j:
            for par in range(2):
                logits(j * 2 + par, par)
                pe.wait_ge(self.low_ready, j * 2 + par + 1)
                self.tensor_transpose(pe, j * 2 + par + 2, par)
        logits(GROUPS - 2, 0)
        logits(GROUPS - 1, 1)
        pe.wait_ge(self.low_ready, GROUPS)

    def tensor_coef(self, pe):
        nc = self.nc
        pe.wait_ge(self.coef_ready, 1)
        for n in range(2):
            ins = nc.tensor.transpose(self.psum[:, self.CT, n * P:(n + 1) * P],
                                      self.coef[:, n * TILES // 2:(n + 1) * TILES // 2, :]
                                      .rearrange("p t e -> p (t e)"), self.ident[:])
        ins.then_inc(self.ct_ready, 1)

    def tensor_bias(self, pe, g):
        if g == 0:
            pe.wait_ge(self.coefT_ready, 1)
            pe.wait_ge(self.bias_loaded, TILES // 2 * 16)
        if g >= 2:
            pe.wait_ge(self.bias_used, g - 1)
        n, q = g // (GROUPS // 2), g % (GROUPS // 2)
        self.nc.tensor.matmul(self.psum[:, self.BIAS[g % 2], :], self.coefT[:, n, :],
                              self.bdiag[:, q * GW:(q + 1) * GW], start=True, stop=True).then_inc(self.bias_ready, 1)


def first_mixture(nc, name, X, ident, psum, W, A):
    with ExitStack() as ctx:
        sb = lambda n, s, dt=F32: ctx.enter_context(nc.sbuf_tensor(f"{name}_{n}", s, dt))
        sem = Semaphores(ctx, nc, name)
        ro = Router(ctx, sem, nc, name, X, ident, psum, W, W.rw[:], W.rb[:])
        coef = ro.coef
        sh, sl = sb("staged_high", [P, 2, GW], F32R), sb("staged_low", [P, 2, GW], F32R)
        side = sb("side", [P, 4, E // 2, D])
        pairs, total = sb("pairs", [P, 2, 2, D]), sb("side_total", [P, 4, D])
        dve_chain = sem("dve_chain")
        staged, experts_ready, side_ready, pairs_ready, total_ready, x_ready, added = (
            sem("staged"), sem("experts_ready"), sem("side_ready"), sem("pairs_ready"), sem("total_ready"),
            sem("x_ready"), sem("added"))

        def weight(t, e):
            return coef[:, bass.ds(t, 1), e:e + 1].rearrange("p o d -> p (o d)")

        def out(n, e):
            return psum[:, 2 * n + e // 4, (e % 4) * D:(e % 4 + 1) * D]

        with nc.Block() as block:
            @block.vector
            def _(dve):
                chain = Chain(dve, dve_chain, W.passed)

                def combine(g, n):
                    last = {}
                    for e in range(E // 2):
                        for k in (n, n + 1):
                            if e == 0:
                                dve.wait_ge(experts_ready, g * GT + k + 1)
                            else:
                                dve.wait_ge(dve_chain, last[k])
                            x = ro.flat(X, g * GT + k)
                            ins = nc.vector.scalar_tensor_tensor(x, out(k, e), weight(g * GT + k, e), x,
                                                                 ALU.mult, ALU.add)
                            if e < E // 2 - 1:
                                last[k] = chain.mark(ins)
                            else:
                                ins.then_inc(x_ready, 1)

                def add_side(g, n):
                    for k in (n, n + 1):
                        dve.wait_ge(total_ready, g * GT + k + 1)
                        dve.wait_ge(x_ready, g * GT + k + 1)
                        x = ro.flat(X, g * GT + k)
                        nc.vector.tensor_tensor(x, x, total[:, k, :], ALU.add).then_inc(added, 1)

                ro.vector_front(dve, chain)
                ro.vector_top1(dve, chain)
                combine(0, 0)
                with dve.Fori(0, GROUPS - 1) as g:
                    chain.turn(g, 4 * (E // 2 - 1))
                    combine(g, 2)
                    add_side(g, 0)
                    combine(g + 1, 0)
                    add_side(g, 2)
                chain.leave(GROUPS - 1)
                combine(GROUPS - 1, 2)
                add_side(GROUPS - 1, 0)
                add_side(GROUPS - 1, 2)
                dve.wait_ge(added, TILES)
                for g in range(GROUPS):
                    ro.vector_bias(dve, g)

            @block.gpsimd
            def _(pool):
                def add_up(g, k, first=False):
                    t = g * GT + k
                    pool.wait_ge(side_ready, (t + 1) * (E // 2))
                    if not first or k >= 2:
                        pool.wait_ge(total_ready, t - 1)
                    nc.gpsimd.tensor_tensor(pairs[:, k % 2], side[:, k, 0:2, :], side[:, k, 2:4, :], ALU.add)\
                        .then_inc(pairs_ready, 1)
                    pool.wait_ge(pairs_ready, t + 1)
                    if not first:
                        pool.wait_ge(added, t - 3)
                    nc.gpsimd.tensor_tensor(total[:, k, :], pairs[:, k % 2, 0, :], pairs[:, k % 2, 1, :], ALU.add)\
                        .then_inc(total_ready, 1)

                ro.gpsimd_front(pool)
                for k in range(GT):
                    add_up(0, k, first=True)
                with pool.Fori(1, GROUPS) as g:
                    for k in range(GT):
                        add_up(g, k)

            @block.sync
            def _(sp):
                ro.sync_bias(sp, A["L0_ffn_expert_b"])

            @block.scalar
            def _(act):
                def stage(g, par):
                    nc.scalar.activation(sh[:, par, :], ro.flat(ro.xh, g), ACT.Copy)
                    nc.scalar.activation(sl[:, par, :], ro.flat(ro.xl, g), ACT.Copy).then_inc(staged, 1)

                def weigh_side(g, k, first=False):
                    t = g * GT + k
                    wait_alone(act, W.passed, experts_ready, t + 1)
                    if not first:
                        wait_alone(act, W.passed, pairs_ready, t - 3)
                    for e in range(E // 2, E):
                        nc.scalar.activation(side[:, k, e - E // 2, :], out(k, e), ACT.Copy, scale=weight(t, e))\
                            .then_inc(side_ready, 1)

                ro.scalar_front(act)
                act.wait_ge(ro.low_ready, 2)
                stage(0, 0)
                stage(1, 1)
                ro.scalar_exp(act)
                ro.scalar_coef_rows(act)
                for k in range(GT):
                    weigh_side(0, k, first=True)
                stage(2, 0)
                for k in range(GT):
                    weigh_side(1, k)
                with act.Fori(1, GROUPS // 2 - 1) as j:
                    for par in range(2):
                        stage(j * 2 + par + 1, 1 - par)
                        for k in range(GT):
                            weigh_side(j * 2 + par, k)
                stage(GROUPS - 1, 1)
                for k in range(GT):
                    weigh_side(GROUPS - 2, k)
                for k in range(GT):
                    weigh_side(GROUPS - 1, k)

            @block.tensor
            def _(pe):
                def experts(g, par, k, first=False):
                    tok = slice(k * P, (k + 1) * P)
                    if not first:
                        pe.wait_ge(x_ready, g * GT + k - 3)
                        pe.wait_ge(side_ready, (g * GT + k - 3) * (E // 2))
                    for half in range(2):
                        cols = slice(half * 4 * D, (half + 1) * 4 * D)
                        ins = three_products(nc, psum[:, 2 * k + half, :], (sh[:, par, tok], sl[:, par, tok]),
                                             (W.ewh[:, cols], W.ewl[:, cols]))
                    ins.then_inc(experts_ready, 1)

                ro.tensor_front(pe)
                pe.wait_ge(staged, 1)
                experts(0, 0, 0, first=True)
                experts(0, 0, 1, first=True)
                ro.tensor_coef(pe)
                pe.wait_ge(ro.coefT_ready, 1)
                experts(0, 0, 2, first=True)
                experts(0, 0, 3, first=True)
                pe.wait_ge(staged, 2)
                for k in range(GT):
                    experts(1, 1, k)
                with pe.Fori(1, GROUPS // 2) as j:
                    for par in range(2):
                        pe.wait_ge(staged, j * 2 + par + 1)
                        for k in range(GT):
                            experts(j * 2 + par, par, k)
                pe.wait_ge(x_ready, TILES)
                pe.wait_ge(side_ready, TILES * (E // 2))
                for g in range(GROUPS):
                    ro.tensor_bias(pe, g)


def attention(nc, name, X, ident, neg_half, psum, W):
    SCALE = float(D) ** -0.5
    NC = S // 512
    QT = S // P
    with ExitStack() as ctx:
        sb = lambda n, s, dt=F32: ctx.enter_context(nc.sbuf_tensor(f"{name}_{n}", s, dt))
        sem = Semaphores(ctx, nc, name)
        XB, KB, QB, VB = (0, 1), (2, 3), (4, 5), (6, 7)
        TB, OB = (4, 5), (6, 7)
        fr = WholeFront(ctx, sem, nc, name, X, ident, psum, XB, W.passed)
        xh, xl, xT = sb("xh", [P, 2, GW], F32R), sb("xl", [P, 2, GW], F32R), sb("xT", [P, 2, GW])
        kh, kl = sb("kh", [P, B * S], F32R), sb("kl", [P, B * S], F32R)
        qh, ql = sb("qh", [P, B * S], F32R), sb("ql", [P, B * S], F32R)
        v = sb("v", [P, TILES, D])
        qsh, qsl = sb("qsh", [P, 2, P], F32R), sb("qsl", [P, 2, P], F32R)
        prob, pT = sb("prob", [P, S]), sb("pT", [P, NC, 512])
        cmax, nmax, nbias = sb("chunk_max", [P, NC]), sb("neg_max", [P, 1]), sb("neg_bias", [P, 2])
        rsum, rtot, rinv = sb("row_sums", [P, 2, NC]), sb("row_total", [P, 1]), sb("row_inverse", [P, 1])
        dve_chain = sem("dve_chain")
        xT_ready, high_ready, low_ready = sem("xT_ready"), sem("high_ready"), sem("low_ready")
        k_ready, q_ready, v_ready = sem("k_ready"), sem("q_ready"), sem("v_ready")
        kh_ready, qh_ready, kl_ready, ql_ready, v_done = (
            sem("kh_ready"), sem("qh_ready"), sem("kl_ready"), sem("ql_ready"), sem("v_done"))
        staged, scores_ready, nbias_ready, exp_ready = (
            sem("staged"), sem("scores_ready"), sem("nbias_ready"), sem("exp_ready"))
        pt_ready, pT_even, pT_odd, out_ready, x_done = (
            sem("pt_ready"), sem("pT_even"), sem("pT_odd"), sem("out_ready"), sem("x_done"))

        with nc.Block() as block:
            @block.vector
            def _(dve):
                chain = Chain(dve, dve_chain, W.passed)

                def low(g, par):
                    dve.wait_ge(high_ready, g + 1)
                    nc.vector.tensor_tensor(xl[:, par, :], psum[:, XB[par], :], xh[:, par, :].bitcast(F32),
                                            ALU.subtract).then_inc(low_ready, 1)

                def project(g, par):
                    dve.wait_ge(v_ready, g + 1)
                    nc.vector.tensor_tensor(v[:, bass.ts(g, GT), :],
                                            psum[:, VB[par], :].rearrange("p (t d) -> p t d", d=D),
                                            W.bvb[:].unsqueeze(1).to_broadcast([P, GT, D]), ALU.add)\
                        .then_inc(v_done, 1)
                    cols = bass.ts(g, GW)
                    for ready, high, rest, bank, bias, done in ((kh_ready, kh, kl, KB, W.bk, kl_ready),
                                                                (qh_ready, qh, ql, QB, W.bq, ql_ready)):
                        dve.wait_ge(ready, g + 1)
                        nc.vector.scalar_tensor_tensor(rest[:, cols], psum[:, bank[par], :], bias[:],
                                                       high[:, cols].bitcast(F32), ALU.add, ALU.subtract)\
                            .then_inc(done, 1)

                def vector_max(i, par):
                    for c in range(NC):
                        dve.wait_ge(scores_ready, i * NC + c + 1)
                        ins = nc.vector.tensor_reduce(cmax[:, c:c + 1], psum[:, c, :], AX.X, ALU.max)
                    chain.link(ins)
                    chain.link(nc.vector.tensor_reduce(nmax[:], cmax[:], AX.X, ALU.max))
                    nc.vector.tensor_scalar(nbias[:, par:par + 1], nmax[:], -SCALE, None, ALU.mult)\
                        .then_inc(nbias_ready, 1)

                def vector_odd(i, c):
                    dve.wait_ge(pt_ready, i * NC + c + 1)
                    nc.vector.tensor_copy(pT[:, c, :], psum[:, TB[c % 2], :]).then_inc(pT_odd, 1)

                def vector_outputs(i, par):
                    chain.link(nc.vector.tensor_reduce(rtot[:], rsum[:, par, :], AX.X, ALU.add))
                    chain.link(nc.vector.reciprocal(rinv[:], rtot[:]))
                    dve.wait_ge(out_ready, i + 1)
                    x = X[:, bass.ds(i, 1), :].rearrange("p o d -> p (o d)")
                    nc.vector.scalar_tensor_tensor(x, psum[:, OB[par], 0:D], rinv[:], x, ALU.mult, ALU.add)\
                        .then_inc(x_done, 1)

                fr.vector_stats(dve, chain)
                fr.vector_normalize(dve, 0, 0, first=True)
                fr.vector_normalize(dve, 1, 1, first=True)
                low(0, 0)
                with dve.Fori(0, GROUPS // 2 - 1) as j:
                    for par in range(2):
                        fr.vector_normalize(dve, j * 2 + par + 2, par)
                        low(j * 2 + par + 1, 1 - par)
                        project(j * 2 + par, par)
                low(GROUPS - 1, 1)
                project(GROUPS - 2, 0)
                project(GROUPS - 1, 1)

                vector_max(0, 0)
                vector_odd(0, 1)
                with dve.Fori(0, TILES // 2 - 1) as j:
                    chain.turn(j, 8)
                    for par in range(2):
                        i = j * 2 + par
                        vector_max(i + 1, 1 - par)
                        vector_odd(i, 3)
                        vector_outputs(i, par)
                        vector_odd(i + 1, 1)
                chain.leave(TILES // 2 - 1)
                vector_max(TILES - 1, 1)
                vector_odd(TILES - 2, 3)
                vector_outputs(TILES - 2, 0)
                vector_odd(TILES - 1, 1)
                vector_odd(TILES - 1, 3)
                vector_outputs(TILES - 1, 1)
                dve.wait_ge(x_done, TILES)

            @block.gpsimd
            def _(pool):
                def stage(i, par):
                    cols = bass.ts(i, P)
                    nc.gpsimd.tensor_copy(qsh[:, par, :], qh[:, cols])
                    nc.gpsimd.tensor_copy(qsl[:, par, :], ql[:, cols]).then_inc(staged, 1)

                fr.gpsimd_rstd(pool)
                pool.wait_ge(qh_ready, 1)
                pool.wait_ge(ql_ready, 1)
                stage(0, 0)
                stage(1, 1)
                pool.wait_ge(ql_ready, GROUPS)
                with pool.Fori(1, TILES // 2) as j:
                    for par in range(2):
                        wait_alone(pool, W.passed, scores_ready, (j * 2 + par - 1) * NC)
                        stage(j * 2 + par, par)

            @block.scalar
            def _(act):
                def parts(g, par):
                    act.wait_ge(fr.xt_ready, g + 1)
                    nc.scalar.activation(xT[:, par, :], psum[:, XB[par], :], ACT.Copy).then_inc(xT_ready, 1)
                    nc.scalar.activation(xh[:, par, :], psum[:, XB[par], :], ACT.Copy).then_inc(high_ready, 1)

                def project(g, par):
                    cols = bass.ts(g, GW)
                    for ready, high, bank, bias, done in ((k_ready, kh, KB, W.bk, kh_ready),
                                                          (q_ready, qh, QB, W.bq, qh_ready)):
                        act.wait_ge(ready, g + 1)
                        nc.scalar.activation(high[:, cols], psum[:, bank[par], :], ACT.Identity, bias=bias[:])\
                            .then_inc(done, 1)

                def exps(i, par, c, first=False):
                    act.wait_ge(nbias_ready, i + 1)
                    if not first:
                        act.wait_ge(pt_ready, (i - 1) * NC + c + 1)
                    nc.scalar.activation(prob[:, c * 512:(c + 1) * 512], psum[:, c, :], ACT.Exp,
                                         bias=nbias[:, par:par + 1], scale=SCALE,
                                         accum_out=rsum[:, par, c:c + 1]).then_inc(exp_ready, 1)

                def even(i, c):
                    act.wait_ge(pt_ready, i * NC + c + 1)
                    nc.scalar.activation(pT[:, c, :], psum[:, TB[c % 2], :], ACT.Copy).then_inc(pT_even, 1)

                def step(i, par):
                    even(i, 2)
                    for c in range(NC):
                        exps(i + 1, 1 - par, c)
                    even(i + 1, 0)

                parts(0, 0)
                with act.Fori(0, GROUPS // 2 - 1) as j:
                    for par in range(2):
                        parts(j * 2 + par + 1, 1 - par)
                        project(j * 2 + par, par)
                parts(GROUPS - 1, 1)
                project(GROUPS - 2, 0)
                project(GROUPS - 1, 1)
                for c in range(NC):
                    exps(0, 0, c, first=True)
                even(0, 0)
                with act.Fori(0, TILES // 2 - 1) as j:
                    step(j * 2, 0)
                    step(j * 2 + 1, 1)
                step(TILES - 2, 0)
                even(TILES - 1, 2)

            @block.tensor
            def _(pe):
                def project(g, par, first=False):
                    pe.wait_ge(xT_ready, g + 1)
                    if not first:
                        pe.wait_ge(v_done, g - 1)
                        pe.wait_ge(kl_ready, g - 1)
                        pe.wait_ge(ql_ready, g - 1)
                    for t in range(GT):
                        tok = slice(t * P, (t + 1) * P)
                        ins = nc.tensor.matmul(psum[:, VB[par], tok], xT[:, par, tok], W.wv[:], start=True, stop=True)
                    ins.then_inc(v_ready, 1)
                    pe.wait_ge(low_ready, g + 1)
                    x = (xh[:, par, :], xl[:, par, :])
                    three_products(nc, psum[:, KB[par], :], (W.wkh[:], W.wkl[:]), x).then_inc(k_ready, 1)
                    three_products(nc, psum[:, QB[par], :], (W.wqh[:], W.wql[:]), x).then_inc(q_ready, 1)

                def scores(i, par, b, c, first=False):
                    if c == 0:
                        pe.wait_ge(staged, i + 1)
                    if not first:
                        pe.wait_ge(exp_ready, (i - 1) * NC + c + 1)
                    cols = slice(b * S + c * 512, b * S + (c + 1) * 512)
                    three_products(nc, psum[:, c, :], (qsh[:, par, :], qsl[:, par, :]),
                                   (kh[:, cols], kl[:, cols])).then_inc(scores_ready, 1)

                def turn(i, c):
                    pe.wait_ge(exp_ready, i * NC + c + 1)
                    if c >= 2:
                        pe.wait_ge(pT_odd if c % 2 else pT_even, i * 2 + 1)
                    for k in range(4):
                        cols = slice((c * 4 + k) * P, (c * 4 + k + 1) * P)
                        ins = nc.tensor.transpose(psum[:, TB[c % 2], k * P:(k + 1) * P], prob[:, cols], ident[:])
                    ins.then_inc(pt_ready, 1)

                def weigh(i, par, b, c):
                    pe.wait_ge(pT_odd if c % 2 else pT_even, i * 2 + c // 2 + 1)
                    for k in range(4):
                        ins = nc.tensor.matmul(psum[:, OB[par], 0:D], pT[:, c, k * P:(k + 1) * P],
                                               v[:, b * QT + c * 4 + k, :],
                                               start=(c == 0 and k == 0), stop=(c == NC - 1 and k == 3))
                    if c == NC - 1:
                        ins.then_inc(out_ready, 1)

                def step(i, par, b, ahead):
                    more = (lambda c: scores(i + 1, 1 - par, ahead, c)) if ahead is not None else (lambda c: None)
                    more(0)
                    turn(i, 0)
                    more(1)
                    turn(i, 1)
                    more(2)
                    weigh(i, par, b, 0)
                    more(3)
                    weigh(i, par, b, 1)
                    turn(i, 2)
                    turn(i, 3)
                    weigh(i, par, b, 2)
                    weigh(i, par, b, 3)

                fr.tensor_transpose(pe, 0, 0)
                fr.tensor_transpose(pe, 1, 1)
                project(0, 0, first=True)
                fr.tensor_transpose(pe, 2, 0)
                project(1, 1, first=True)
                fr.tensor_transpose(pe, 3, 1)
                with pe.Fori(1, GROUPS // 2 - 1) as j:
                    for par in range(2):
                        project(j * 2 + par, par)
                        fr.tensor_transpose(pe, j * 2 + par + 2, par)
                project(GROUPS - 2, 0)
                project(GROUPS - 1, 1)
                for done in (kl_ready, ql_ready, v_done):
                    pe.wait_ge(done, GROUPS)
                for c in range(NC):
                    scores(0, 0, 0, c, first=True)
                for b in range(B):
                    with pe.Fori(b * QT // 2, (b + 1) * QT // 2 - 1) as j:
                        step(j * 2, 0, b, b)
                        step(j * 2 + 1, 1, b, b)
                    step((b + 1) * QT - 2, 0, b, b)
                    step((b + 1) * QT - 1, 1, b, b + 1 if b + 1 < B else None)


def second_mixture(nc, name, X, ident, neg_half, psum, W, A):
    with ExitStack() as ctx:
        sb = lambda n, s, dt=F32: ctx.enter_context(nc.sbuf_tensor(f"{name}_{n}", s, dt))
        sem = Semaphores(ctx, nc, name)
        HB, YB = (0, 1, 2, 3), (4, 5)
        ro = Router(ctx, sem, nc, name, X, ident, psum, W, W.gw[:], W.gb[:])
        coef, flat = ro.coef, ro.flat
        w1, w2 = sb("w1", [P, E, F]), sb("w2", [P, E, FC * D])
        w1h, w1l = sb("w1h", [P, 2, F], F32R), sb("w1l", [P, 2, F], F32R)
        h = sb("h", [P, 2, FC, GW])
        dve_chain = sem("dve_chain")
        w1_loaded, w2_loaded = sem("w1_loaded"), sem("w2_loaded")
        w_high, w_low = sem("w_high"), sem("w_low")
        up_ready, h_ready, y_ready, y_used = sem("up_ready"), sem("h_ready"), sem("y_ready"), sem("y_used")

        with nc.Block() as block:
            @block.vector
            def _(dve):
                chain = Chain(dve, dve_chain, W.passed)

                ro.vector_front(dve, chain)
                ro.vector_top2(dve, chain)
                dve.sem_inc(y_used, 2)

                def combine(e, g, par):
                    dve.wait_ge(y_ready, e * GROUPS + g + 1)
                    for t in range(GT):
                        x = flat(X, g * GT + t)
                        c = coef[:, bass.ds(g * GT + t, 1), bass.ds(e, 1)].rearrange("p o d -> p (o d)")
                        ins = nc.vector.scalar_tensor_tensor(x, psum[:, YB[par], t * D:(t + 1) * D], c, x,
                                                             ALU.mult, ALU.add)
                    ins.then_inc(y_used, 1)

                with dve.Fori(0, E - 1) as e:
                    wait_alone(dve, W.passed, y_used, e * GROUPS + 2)
                    with dve.Fori(0, GROUPS // 2) as j:
                        combine(e, j * 2, 0)
                        combine(e, j * 2 + 1, 1)
                dve.wait_ge(y_used, (E - 1) * GROUPS + 2)
                for g in range(GROUPS):
                    if g > 0:
                        combine(E - 1, g - 1, (g - 1) % 2)
                    ro.vector_bias(dve, g)
                    dve.wait_ge(ro.bias_used, g + 1)
                combine(E - 1, GROUPS - 1, 1)

            @block.gpsimd
            def _(pool):
                def low(e, par):
                    wait_alone(pool, W.passed, w_high, e + 1)
                    nc.gpsimd.tensor_tensor(w1l[:, par, :], flat(w1, e), w1h[:, par, :].bitcast(F32),
                                            ALU.subtract).then_inc(w_low, 1)

                ro.gpsimd_front(pool)
                with pool.Fori(0, E // 2) as j:
                    low(j * 2, 0)
                    low(j * 2 + 1, 1)

            @block.sync
            def _(sp):
                for half in range(2):
                    es = slice(half * E // 2, (half + 1) * E // 2)
                    sp.dma_start(w1[:, es, :], A["L1_ffn_w1"][es].rearrange("e p f -> p e f")).then_inc(w1_loaded, 16)
                for half in range(2):
                    es = slice(half * E // 2, (half + 1) * E // 2)
                    for e in range(es.start, es.stop):
                        sp.dma_start(w2[:, e, :].rearrange("p (c d) -> p c d", d=D),
                                     A["L1_ffn_w2"][e].rearrange("(c p) d -> p c d", p=P)).then_inc(w2_loaded, 16)
                ro.sync_bias(sp, A["L1_ffn_b2"])

            @block.scalar
            def _(act):
                def high(e, par):
                    nc.scalar.activation(w1h[:, par, :], flat(w1, e), ACT.Copy).then_inc(w_high, 1)

                def hidden(e, g, par):
                    for c in range(FC):
                        wait_alone(act, W.passed, up_ready, (e * GROUPS + g) * FC + c + 1)
                        nc.scalar.activation(h[:, par, c, :], psum[:, HB[c], :], ACT.Relu,
                                             bias=W.b1T[:, bass.ds(e * FC + c, 1)]).then_inc(h_ready, 1)

                ro.scalar_front(act)
                act.wait_ge(w1_loaded, 32)
                high(0, 0)
                ro.scalar_exp(act)
                high(1, 1)
                ro.scalar_coef_rows(act)

                def expert(e, par_e, ahead=True):
                    with act.Fori(0, GROUPS // 2) as i:
                        hidden(e, i * 2, 0)
                        hidden(e, i * 2 + 1, 1)
                    if ahead:
                        high(e + 2, par_e)

                with act.Fori(0, E // 2 - 1) as j:
                    expert(j * 2, 0)
                    expert(j * 2 + 1, 1)
                expert(E - 2, 0, ahead=False)
                expert(E - 1, 1, ahead=False)

            @block.tensor
            def _(pe):
                def up(e, g, c, par_e):
                    x = [flat(a, g) for a in (ro.xh, ro.xl)]
                    cols = slice(c * P, (c + 1) * P)
                    three_products(nc, psum[:, HB[c], :], (w1h[:, par_e, cols], w1l[:, par_e, cols]), x)\
                        .then_inc(up_ready, 1)

                def down(e, g, c, par):
                    if c == 0:
                        pe.wait_ge(y_used, e * GROUPS + g + 1)
                    for t in range(GT):
                        tok = slice(t * P, (t + 1) * P)
                        ins = nc.tensor.matmul(psum[:, YB[par], tok], h[:, par, c, tok],
                                               w2[:, bass.ds(e, 1), c * D:(c + 1) * D].rearrange("p o d -> p (o d)"),
                                               start=(c == 0 and t == 0), stop=(c == FC - 1), skip_group_check=True)
                    if c == FC - 1:
                        ins.then_inc(y_ready, 1)

                ro.tensor_front(pe)
                pe.wait_ge(w_low, 1)
                for c in range(FC):
                    up(0, 0, c, 0)
                ro.tensor_coef(pe)
                pe.wait_ge(w2_loaded, E * 16)

                def group(e, g, par, ahead):
                    for c in range(FC):
                        pe.wait_ge(h_ready, (e * GROUPS + g) * FC + c + 1)
                        if ahead:
                            up(*ahead[0:2], c, ahead[2])
                        down(e, g, c, par)

                def expert(e, par_e):
                    with pe.Fori(0, GROUPS // 2 - 1) as i:
                        group(e, i * 2, 0, (e, i * 2 + 1, par_e))
                        group(e, i * 2 + 1, 1, (e, i * 2 + 2, par_e))
                    group(e, GROUPS - 2, 0, (e, GROUPS - 1, par_e))
                    pe.wait_ge(w_low, e + 2)
                    group(e, GROUPS - 1, 1, (e + 1, 0, 1 - par_e))

                with pe.Fori(0, E // 2 - 1) as j:
                    expert(j * 2, 0)
                    expert(j * 2 + 1, 1)
                expert(E - 2, 0)
                for g in range(GROUPS):
                    ro.tensor_bias(pe, g)
                    group(E - 1, g, g % 2, (E - 1, g + 1, 1) if g + 1 < GROUPS else None)


class Holder:
    pass


H, KD, VD = 4, 32, 64
KEY, VAL = H * KD, H * VD
CONV = 4
RMS_EPS = 1e-6
NQ = TILES * H


def row_stats(nc, eng, chain, stats, mv, src):
    for t in range(GT):
        ins = nc.vector.bn_stats(stats[:, t, :], src[:, t, :])
    chain.link_alone(ins)
    for t in range(GT):
        ins = nc.vector.bn_aggr(mv[:, t, :], stats[:, t, :])
    return ins


def inverse_root(nc, pool, passed, sem, count, out, src, tmp, scale, eps, power):
    nc.gpsimd.tensor_scalar(tmp, src, scale, eps, ALU.mult, ALU.add).then_inc(sem, 1)
    wait_alone(pool, passed, sem, count + 1)
    nc.gpsimd.tensor_tensor(out, tmp, power, ALU.pow).then_inc(sem, 1)


def delta_inputs(nc, X, ident, neg_half, psum, W, M):
    with ExitStack() as ctx:
        sb = lambda n, s, dt=F32: ctx.enter_context(nc.sbuf_tensor(f"in_{n}", s, dt))
        sem = Semaphores(ctx, nc, "in")
        stats, mv = sb("stats", [P, GT, 6]), sb("mv", [P, GT, 2])
        r1, r2, r3, rt = (sb(n, [P, GT]) for n in ("r1", "r2", "r3", "rt"))
        ss = sb("ss", [P, GT])
        y, sq, h0 = sb("y", [P, GT, D]), sb("sq", [P, GT, D]), sb("h0", [P, GT, D])
        hT = sb("hT", [P, GW])
        cv = sb("cv", [P, 4, GW + CONV - 1])
        acc, th = sb("acc", [P, 4, GW]), sb("th", [P, 4, GW])
        sg = sb("sg", [P, GT, VAL])
        sq2, ss2, rq, rqt = sb("sq2", [P, 2, GW]), sb("ss2", [P, 32]), sb("rq", [P, 32]), sb("rqt", [P, 32])
        fac, nh32 = sb("fac", [P, 32]), sb("nh32", [P, 32])
        dve_chain, pool_chain, act_chain = sem("dve_chain"), sem("pool_chain"), sem("act_chain")
        mv_ready, r1_ready, r2_ready, y_ready, ss_ready, r3_ready, h_ready = (
            sem(n) for n in ("mv_ready", "r1_ready", "r2_ready", "y_ready", "ss_ready", "r3_ready", "h_ready"))
        ht_ready, hT_ready, proj_ready, cv_ready, halo_ready, gate_ready, sg_ready, gate_used = (
            sem(n) for n in ("ht_ready", "hT_ready", "proj_ready", "cv_ready", "halo_ready", "gate_ready",
                             "sg_ready", "gate_used"))
        acc0_ready, acc_ready, th_ready, s2_ready, nat_ready, sq2_ready, ss2_ready, rq_ready, nat_used, v_used = (
            sem(n) for n in ("acc0_ready", "acc_ready", "th_ready", "s2_ready", "nat_ready", "sq2_ready",
                             "ss2_ready", "rq_ready", "nat_used", "v_used"))
        wloaded, consts = sem("wloaded"), sem("consts")
        GATE, AB, TB = (4, 5), 6, 7

        def tiles4(ap):
            return ap.unsqueeze(1).to_broadcast([P, GT, D])

        with nc.Block() as block:
            @block.vector
            def _(dve):
                chain = Chain(dve, dve_chain, W.passed)
                dve.wait_ge(wloaded, 16 * M.n_loads)
                with dve.Fori(0, B) as b:
                    chain.turn(b, 1 + (GROUPS // B) * 15)
                    chain.link_alone(nc.vector.memset(cv[:, :, GW:GW + CONV - 1], 0.0))
                    with dve.Fori(0, GROUPS // B) as j:
                        chain.turn(j, 15)
                        g = b * (GROUPS // B) + j
                        x, rows = X[:, bass.ts(g, GT), :], bass.ts(g, GT)
                        row_stats(nc, dve, chain, stats, mv, x).then_inc(mv_ready, 1)
                        dve.wait_ge(r1_ready, g * 4 + 2)
                        for t in range(GT):
                            ins = nc.vector.tensor_scalar(h0[:, t, :], x[:, t, :], mv[:, t, 0:1], r1[:, t:t + 1],
                                                          ALU.subtract, ALU.mult)
                        nc.vector.tensor_copy(M.mean[:, rows, :], mv[:, :, 0:1])
                        ins = nc.vector.tensor_copy(M.rstd[:, rows], r1[:])
                        chain.link(ins)
                        row_stats(nc, dve, chain, stats, mv, h0).then_inc(mv_ready, 1)
                        dve.wait_ge(r1_ready, g * 4 + 4)
                        for t in range(GT):
                            ins = nc.vector.tensor_scalar(y[:, t, :], h0[:, t, :], mv[:, t, 0:1], r2[:, t:t + 1],
                                                          ALU.subtract, ALU.mult)
                        chain.link(ins)
                        chain.link(nc.vector.tensor_tensor(y[:], y[:], tiles4(M.ln1g[:]), ALU.mult))
                        nc.vector.tensor_tensor(y[:], y[:], tiles4(M.ln1b[:]), ALU.add).then_inc(y_ready, 1)
                        dve.wait_ge(r3_ready, g * 2 + 2)
                        for t in range(GT):
                            ins = nc.vector.tensor_scalar(y[:, t, :], y[:, t, :], r3[:, t:t + 1], None, ALU.mult)
                        ins.then_inc(h_ready, 1)
                        nc.vector.tensor_copy(cv[:, :, 0:CONV - 1], cv[:, :, GW:GW + CONV - 1]).then_inc(halo_ready, 1)
                        for c in range(4):
                            dve.wait_ge(acc0_ready, g * 4 + c + 1)
                            for i in range(1, CONV):
                                ins = nc.vector.scalar_tensor_tensor(acc[:, c, :], cv[:, c, i:i + GW],
                                                                     M.convw[:, c, i:i + 1], acc[:, c, :],
                                                                     ALU.mult, ALU.add)
                                if i < CONV - 1:
                                    chain.link(ins)
                            ins.then_inc(acc_ready, 1)
                        for c in range(4):
                            dve.wait_ge(th_ready, g * 4 + c + 1)
                            nc.vector.scalar_tensor_tensor(th[:, c, :], th[:, c, :], 1.0, acc[:, c, :],
                                                           ALU.add, ALU.mult).then_inc(s2_ready, 1)
                        for n in range(2):
                            dve.wait_ge(sg_ready, g * 2 + n + 1)
                            nc.vector.scalar_tensor_tensor(
                                M.gate[:, bass.ds(g * GT + n * 2, 2), :], sg[:, 2 * n:2 * n + 2, :], 1.0,
                                psum[:, GATE[n], :].rearrange("p (t v) -> p t v", v=VAL), ALU.add, ALU.mult)
                        nc.vector.tensor_copy(M.ab[:, bass.ts(g, GT), :],
                                              psum[:, AB, 0:GT * 2 * H].rearrange("p (t e) -> p t e", e=2 * H))\
                            .then_inc(gate_used, 1)
                        dve.wait_ge(sq2_ready, g + 1)
                        nc.vector.tensor_reduce(ss2[:], sq2[:].rearrange("p a (n k) -> p (a n) k", k=KD), AX.X, ALU.add)\
                            .then_inc(ss2_ready, 1)
                        dve.wait_ge(rq_ready, g * 3 + 3)
                        for n, dst in enumerate((M.q, M.k)):
                            ins = nc.vector.tensor_tensor(
                                dst[:, bass.ts(g, GT), :].rearrange("p t (h k) -> p (t h) k", k=KD),
                                psum[:, n, :].rearrange("p (n k) -> p n k", k=KD),
                                rq[:, n * 16:(n + 1) * 16].unsqueeze(2).to_broadcast([P, 16, KD]), ALU.mult)
                            chain.link(ins)
                        ins = nc.vector.memset(rt[:, 0:1], 0.0)
                        ins.then_inc(nat_used, 1)
                    chain.leave(GROUPS // B)
                chain.leave(B)

            @block.gpsimd
            def _(pool):
                nc.gpsimd.memset(nh32[:], -0.5).then_inc(consts, 1)
                nc.gpsimd.memset(fac[:, 0:16], 0.5 * float(KD) ** -0.5).then_inc(consts, 1)
                nc.gpsimd.memset(fac[:, 16:32], 0.5).then_inc(consts, 1)
                pool.wait_ge(consts, 3)
                with pool.Fori(0, GROUPS) as g:
                    wait_alone(pool, W.passed, mv_ready, g * 2 + 1)
                    inverse_root(nc, pool, W.passed, r1_ready, g * 4, r1[:], mv[:, :, 1], r2[:], 1.0, LN_EPS, neg_half[:])
                    wait_alone(pool, W.passed, mv_ready, g * 2 + 2)
                    inverse_root(nc, pool, W.passed, r1_ready, g * 4 + 2, r2[:], mv[:, :, 1], r1[:], 1.0, LN_EPS, neg_half[:])
                    wait_alone(pool, W.passed, ss_ready, g + 1)
                    inverse_root(nc, pool, W.passed, r3_ready, g * 2, r3[:], ss[:], r1[:], 1.0 / D, RMS_EPS, neg_half[:])
                    wait_alone(pool, W.passed, ss2_ready, g + 1)
                    inverse_root(nc, pool, W.passed, rq_ready, g * 3, rqt[:], ss2[:], rq[:], 0.25, RMS_EPS, nh32[:])
                    wait_alone(pool, W.passed, rq_ready, g * 3 + 2)
                    nc.gpsimd.tensor_tensor(rq[:], rqt[:], fac[:], ALU.mult).then_inc(rq_ready, 1)

            @block.sync
            def _(sp):
                for dst, src in M.loads:
                    sp.dma_start(dst, src).then_inc(wloaded, 16)

            @block.scalar
            def _(act):
                act.wait_ge(wloaded, 16 * M.n_loads)
                with act.Fori(0, GROUPS) as g:
                    act.wait_ge(y_ready, g + 1)
                    for t in range(GT):
                        ins = nc.scalar.activation(sq[:, t, :], y[:, t, :], ACT.Square, accum_out=ss[:, t:t + 1])
                    ins.then_inc(ss_ready, 1)
                    act.wait_ge(ht_ready, g + 1)
                    nc.scalar.activation(hT[:], psum[:, TB, :], ACT.Copy, scale=M.rmsw[:]).then_inc(hT_ready, 1)
                    act.wait_ge(halo_ready, g + 1)
                    for c in range(4):
                        act.wait_ge(proj_ready, g * 4 + c + 1)
                        nc.scalar.activation(cv[:, c, CONV - 1:], psum[:, c, :], ACT.Copy).then_inc(cv_ready, 1)
                    for c in range(4):
                        act.wait_ge(cv_ready, g * 4 + c + 1)
                        nc.scalar.activation(acc[:, c, :], cv[:, c, 0:GW], ACT.Copy, scale=M.convw[:, c, 0:1])\
                            .then_inc(acc0_ready, 1)
                    act.wait_ge(gate_ready, g + 1)
                    for n in range(2):
                        nc.scalar.activation(sg[:, 2 * n:2 * n + 2, :],
                                             psum[:, GATE[n], :].rearrange("p (t v) -> p t v", v=VAL),
                                             ACT.Tanh, scale=0.5).then_inc(sg_ready, 1)
                    for c in range(4):
                        act.wait_ge(acc_ready, g * 4 + c + 1)
                        nc.scalar.activation(th[:, c, :], acc[:, c, :], ACT.Tanh, scale=0.5).then_inc(th_ready, 1)
                    act.wait_ge(nat_ready, g + 1)
                    nc.scalar.activation(sq2[:, 0, :], psum[:, 0, :], ACT.Square)
                    nc.scalar.activation(sq2[:, 1, :], psum[:, 1, :], ACT.Square).then_inc(sq2_ready, 1)
                    for n in range(2):
                        ins = nc.scalar.activation(M.v[:, bass.ds(g * GT + n * 2, 2), :],
                                                   psum[:, 2 + n, :].rearrange("p (t v) -> p t v", v=VAL),
                                                   ACT.Copy, scale=0.5)
                    ins.then_inc(v_used, 1)

            @block.tensor
            def _(pe):
                with pe.Fori(0, GROUPS) as g:
                    pe.wait_ge(h_ready, g + 1)
                    for t in range(GT):
                        ins = nc.tensor.transpose(psum[:, TB, t * P:(t + 1) * P], y[:, t, :], ident[:])
                    ins.then_inc(ht_ready, 1)
                    pe.wait_ge(hT_ready, g + 1)
                    for c, w in enumerate((M.wq[:], M.wk[:], M.wv[:, 0:P], M.wv[:, P:2 * P])):
                        nc.tensor.matmul(psum[:, c, :], w, hT[:], start=True, stop=True).then_inc(proj_ready, 1)
                    for t in range(GT):
                        nc.tensor.matmul(psum[:, GATE[t // 2], (t % 2) * VAL:(t % 2 + 1) * VAL],
                                         hT[:, t * P:(t + 1) * P], M.wg[:], start=True, stop=True)
                    for t in range(GT):
                        ins = nc.tensor.matmul(psum[:, AB, t * 2 * H:(t + 1) * 2 * H], hT[:, t * P:(t + 1) * P],
                                               M.wab[:], start=True, stop=True)
                    ins.then_inc(gate_ready, 1)
                    pe.wait_ge(s2_ready, g * 4 + 4)
                    pe.wait_ge(cv_ready, g * 4 + 4)
                    for t in range(GT):
                        tok = slice(t * P, (t + 1) * P)
                        nc.tensor.transpose(psum[:, 0, tok], th[:, 0, tok], ident[:])
                        nc.tensor.transpose(psum[:, 1, tok], th[:, 1, tok], ident[:])
                        for n in range(2):
                            ins = nc.tensor.transpose(
                                psum[:, 2 + t // 2, (t % 2) * VAL + n * P:(t % 2) * VAL + (n + 1) * P],
                                th[:, 2 + n, tok], ident[:])
                    ins.then_inc(nat_ready, 1)
                    pe.wait_ge(nat_used, g + 1)
                    pe.wait_ge(v_used, g + 1)
                    pe.wait_ge(gate_used, g + 1)


def delta_decays(nc, psum, M):
    with ExitStack() as ctx:
        sb = lambda n, s, dt=F32: ctx.enter_context(nc.sbuf_tensor(f"dec_{n}", s, dt))
        sem = Semaphores(ctx, nc, "dec")
        z, na, u, s_, s2, po = (sb(n, [P, TILES, H]) for n in ("z", "na", "u", "s", "s2", "po"))
        expA = sb("expA", [P, H])
        tmp = sb("tmp", [P, TILES, H])
        tot = sb("tot", [P, TILES, H])
        dve_chain, act_ready, na_ready, pe_ready, g_ready, tot_ready = (
            sem(n) for n in ("dve_chain", "act_ready", "na_ready", "pe_ready", "g_ready", "tot_ready"))
        flat = lambda t: t[:].rearrange("p t h -> p (t h)")

        def bc(ap):
            return ap.unsqueeze(1).to_broadcast([P, TILES, H])

        with nc.Block() as block:
            @block.vector
            def _(dve):
                ch = Chain(dve, dve_chain, M.passed)
                v = nc.vector
                ch.link(v.tensor_tensor(z[:], M.ab[:, :, 0:H], bc(M.dtb[:]), ALU.add))
                ch.link(v.tensor_scalar(na[:], z[:], -1.0, None, ALU.mult))
                v.tensor_tensor(na[:], na[:], z[:], ALU.min).then_inc(na_ready, 1)
                dve.wait_ge(act_ready, 1)
                ch.link(v.tensor_scalar(s_[:], u[:], 2.0, None, ALU.add))
                ch.link(v.reciprocal(s_[:], s_[:]))
                ch.link(v.tensor_tensor(s_[:], s_[:], u[:], ALU.mult))
                ch.link(v.tensor_tensor(s2[:], s_[:], s_[:], ALU.mult))
                ch.link(v.tensor_scalar(po[:], s2[:], 1.0 / 17, 1.0 / 15, ALU.mult, ALU.add))
                for k in (13, 11, 9, 7, 5, 3, 1):
                    ch.link(v.tensor_tensor(po[:], po[:], s2[:], ALU.mult))
                    ch.link(v.tensor_scalar(po[:], po[:], 1.0 / k, None, ALU.add))
                ch.link(v.scalar_tensor_tensor(po[:], po[:], 2.0, s_[:], ALU.mult, ALU.mult))
                ch.link(v.scalar_tensor_tensor(po[:], z[:], 0.0, po[:], ALU.max, ALU.add))
                dve.wait_ge(act_ready, 3)
                ch.link(v.tensor_tensor(po[:], po[:], bc(expA[:]), ALU.mult))
                v.tensor_scalar(M.g[:], po[:], -1.0, -1000.0, ALU.mult, ALU.max).then_inc(g_ready, 1)
                ch.link(v.tensor_scalar(M.beta[:], tmp[:], 0.5, 0.5, ALU.mult, ALU.add))
                dve.wait_ge(tot_ready, 3)
                ch.link(v.tensor_tensor(tmp[:], tot[:], bc(M.hmask[:]), ALU.mult))
                ch.link(v.tensor_reduce(M.dec[:], tmp[:], AX.X, ALU.add))

            @block.scalar
            def _(act):
                act.wait_ge(na_ready, 1)
                nc.scalar.activation(u[:], na[:], ACT.Exp).then_inc(act_ready, 1)
                nc.scalar.activation(expA[:], M.alog[:], ACT.Exp).then_inc(act_ready, 1)
                nc.scalar.activation(tmp[:], M.ab[:, :, H:2 * H], ACT.Tanh, scale=0.5).then_inc(act_ready, 1)
                for n, dst in enumerate((M.gam, M.kap, tot)):
                    act.wait_ge(pe_ready, n + 1)
                    nc.scalar.activation(flat(dst), psum[:, n, 0:NQ], ACT.Exp).then_inc(tot_ready, 1)

            @block.tensor
            def _(pe):
                pe.wait_ge(g_ready, 1)
                for n, mask in enumerate((M.upto, M.after, M.ones)):
                    nc.tensor.matmul(psum[:, n, 0:NQ], mask[:], flat(M.g), start=True, stop=True)\
                        .then_inc(pe_ready, 1)

U = B * H
STEPS = TILES // B
LEVELS = 5


def delta_scan(nc, ident, psum, M):
    with ExitStack() as ctx:
        sb = lambda n, s, dt=F32: ctx.enter_context(nc.sbuf_tensor(f"sc_{n}", s, dt))
        sem = Semaphores(ctx, nc, "sc")
        ks, qs, kb, qg = (sb(n, [P, B, KEY]) for n in ("ks", "qs", "kb", "qg"))
        kt = sb("kt", [P, B, KEY])
        R = sb("R", [P, U, VD + KD])
        gL = sb("gL", [P, U, P])
        T4 = sb("T4", [P, B, 4, P])
        dec = sb("decays", [P, U, P])
        Lt, Ar, At = sb("Lt", [P, U, P]), sb("Ar", [P, U, P]), sb("At", [P, U, P])
        T, TT, X = sb("T", [P, U, 32]), sb("TT", [P, U, 32]), sb("X", [P, U, 32])
        T64 = sb("T64", [64, U, 64])
        X2, X3 = sb("X2", [P, U, 32]), sb("X3", [P, U, 64])
        TTf = sb("TTf", [P, U, P])
        Us, Wn, WT = sb("Us", [P, U, VD]), sb("Wn", [P, U, KD]), sb("WT", [P, B, P])
        Dl = sb("delta", [P, B, VAL])
        Sd, St = sb("state", [P, B, VAL]), sb("state_new", [P, B, VAL])
        dve_chain = sem("dve_chain")
        (staged, scaled, gl_ready, t4_ready, T4_ready, seg_ready, dec_ready, kk_ready, lt_ready, ar_ready, at_ready,
         x_ready, X_ready, y_ready, T_ready, x2_ready, X2_ready, X2b_ready, y2_ready, diag_ready, T64_ready, TT2_ready, x3_ready, X3_ready, y3_ready, TTf_ready,
         uw_ready, Us_ready, Wn_ready, wt_ready, WT_ready, ws_ready, delta_ready, o_ready, o_used, s_ready, S_ready,
         zeroed) = (sem(n) for n in (
            "staged scaled gl_ready t4_ready T4_ready seg_ready dec_ready kk_ready lt_ready ar_ready at_ready "
            "x_ready X_ready y_ready T_ready x2_ready X2_ready X2b_ready y2_ready diag_ready T64_ready TT2_ready x3_ready X3_ready y3_ready TTf_ready "
            "uw_ready Us_ready Wn_ready wt_ready WT_ready ws_ready delta_ready o_ready o_used s_ready S_ready "
            "zeroed").split())
        XB, YB = 0, 1

        def pair(t, i):
            return t[:].rearrange("p (b s) d -> p b s d", b=B)[:, :, bass.ds(i, 1), :].rearrange("p b s d -> p b (s d)")

        def heads(ap, k):
            return ap.rearrange("p b (h k) -> p b h k", k=k)

        def each(t, i, k):
            return pair(t, i).unsqueeze(3).to_broadcast([P, B, H, k])

        def all_units(ap):
            return ap.unsqueeze(1).to_broadcast([P, U, 32])

        def bank(n, w):
            return psum[:, n, 0:U * w].rearrange("p (u k) -> p u k", k=w)

        with nc.Block() as block:
            @block.gpsimd
            def _(pool):
                g_ = nc.gpsimd
                g_.memset(TTf[:], 0.0).then_inc(zeroed, 1)
                g_.memset(T64[:], 0.0).then_inc(zeroed, 1)
                g_.memset(Sd[:], 0.0).then_inc(zeroed, 1)
                pool.wait_ge(zeroed, 3)
                with pool.Fori(0, STEPS) as i:
                    for bb in range(B):
                        g_.tensor_tensor(
                            gL[:, bb * H:(bb + 1) * H, :], M.upto[:].unsqueeze(1).to_broadcast([P, H, P]),
                            pair(M.g, i)[:, bb, :].unsqueeze(2).to_broadcast([P, H, P]), ALU.mult).then_inc(gl_ready, 1)
                    for bb in range(B):
                        g_.tensor_tensor(heads(kb[:], KD)[:, bb], heads(pair(M.k, i), KD)[:, bb], each(M.beta, i, KD)[:, bb], ALU.mult)
                        g_.tensor_tensor(heads(qg[:], KD)[:, bb], heads(pair(M.q, i), KD)[:, bb], each(M.gam, i, KD)[:, bb], ALU.mult)\
                            .then_inc(scaled, 1)
                    for bb in range(B):
                        g_.tensor_tensor(heads(kt[:], KD)[:, bb], heads(pair(M.k, i), KD)[:, bb], each(M.kap, i, KD)[:, bb], ALU.mult)
                        g_.tensor_tensor(R[:, bb * H:(bb + 1) * H, 0:VD], heads(pair(M.v, i), VD)[:, bb], each(M.beta, i, VD)[:, bb], ALU.mult)
                    wait_alone(pool, M.passed, scaled, i * 4 + 2)
                    for bb in range(B):
                        g_.tensor_tensor(R[:, bb * H:(bb + 1) * H, VD:], heads(kb[:], KD)[:, bb], each(M.gam, i, KD)[:, bb], ALU.mult)\
                            .then_inc(scaled, 1)
                    wait_alone(pool, M.passed, ar_ready, i + 1)
                    for bb in range(B):
                        g_.affine_select(At[:, bb * H:(bb + 1) * H, :], Ar[:, bb * H:(bb + 1) * H, :], [[0, H], [1, P]], ALU.is_ge, 0.0,
                                         base=0, channel_multiplier=-1).then_inc(at_ready, 1)
                    wait_alone(pool, M.passed, T_ready, (i + 1) * LEVELS)
                    wait_alone(pool, M.passed, at_ready, (i + 1) * B)
                    for n in range(6):
                        blk = slice(32 * (n % 4), 32 * (n % 4) + 32)
                        dst, src = (TTf, TT) if n < 4 else (T64, T)
                        g_.tensor_copy(dst[blk, :, blk], src[blk]).then_inc(diag_ready, 1)
                        wait_alone(pool, M.passed, diag_ready, i * 6 + n + 1)
                    wait_alone(pool, M.passed, S_ready, (i + 1) * 2)

            @block.scalar
            def _(act):
                a_ = nc.scalar
                with act.Fori(0, STEPS) as i:
                    a_.activation(ks[:], pair(M.k, i), ACT.Copy)
                    a_.activation(qs[:], pair(M.q, i), ACT.Copy).then_inc(staged, 1)
                    for bb in range(B):
                        act.wait_ge(t4_ready, i * B + bb + 1)
                        a_.activation(T4[:, bb].rearrange("p a b -> p (a b)"), psum[:, bb, :], ACT.Copy).then_inc(T4_ready, 1)
                    for bb in range(B):
                        act.wait_ge(seg_ready, i * B + bb + 1)
                        a_.activation(dec[:, bb * H:(bb + 1) * H, :].rearrange("p a b -> p (a b)"), psum[:, 2 + bb, :], ACT.Exp)\
                            .then_inc(dec_ready, 1)
                    act.wait_ge(x2_ready, i + 1)
                    a_.activation(X2[96:128], bank(XB, 32)[96:128], ACT.Copy).then_inc(X2b_ready, 1)
                    act.wait_ge(y2_ready, i + 1)
                    a_.activation(T64[32:64, :, 0:32], bank(YB, 32)[32:64], ACT.Copy, scale=-1.0).then_inc(T64_ready, 1)
                    a_.activation(TTf[64:96, :, 96:128], bank(2, 32)[64:96], ACT.Copy, scale=-1.0).then_inc(TT2_ready, 1)
                    act.wait_ge(y3_ready, i + 1)
                    a_.activation(TTf[0:64, :, 64:128], bank(0, 64)[0:64], ACT.Copy, scale=-1.0).then_inc(TTf_ready, 1)
                    for bb in range(B):
                        act.wait_ge(uw_ready, i * B + bb + 1)
                        a_.activation(Wn[:, bb * H:(bb + 1) * H, :],
                                      psum[:, 1 + bb, 0:H * (VD + KD)].rearrange("p (u k) -> p u k", k=VD + KD)[:, :, VD:],
                                      ACT.Copy).then_inc(Wn_ready, 1)
                    act.wait_ge(wt_ready, i + 1)
                    a_.activation(WT[:].rearrange("p a b -> p (a b)"), psum[:, 3, 0:B * P], ACT.Copy).then_inc(WT_ready, 1)
                    act.wait_ge(o_ready, i + 1)
                    a_.activation(pair(M.v, i), psum[:, 6, :].rearrange("p (b v) -> p b v", b=B), ACT.Copy).then_inc(o_used, 1)
                    act.wait_ge(S_ready, (i + 1) * 2)

            @block.vector
            def _(dve):
                v = nc.vector
                ch = Chain(dve, dve_chain, M.passed)
                LINKS = LEVELS + 1
                dve.wait_ge(zeroed, 3)
                with dve.Fori(0, STEPS) as i:
                    ch.turn(i, LINKS)
                    dve.wait_ge(dec_ready, i * B + 2)
                    dve.wait_ge(kk_ready, i + 1)
                    for bb in range(B):
                        src = psum[:, 0:H, bb * 256:bb * 256 + P]
                        ins = v.tensor_tensor(Lt[:, bb * H:(bb + 1) * H, :], src, dec[:, bb * H:(bb + 1) * H, :], ALU.mult)
                    ins.then_inc(lt_ready, 1)
                    for bb in range(B):
                        src = psum[:, 0:H, bb * 256 + P:(bb + 1) * 256]
                        ins = v.tensor_tensor(Ar[:, bb * H:(bb + 1) * H, :], src, dec[:, bb * H:(bb + 1) * H, :], ALU.mult)
                    ins.then_inc(ar_ready, 1)
                    dve.wait_ge(x_ready, i * LEVELS + 1)
                    v.tensor_tensor(X[:], bank(XB, 32), all_units(M.level[:, 0, :]), ALU.mult).then_inc(X_ready, 1)
                    dve.wait_ge(X_ready, i * LEVELS + 1)
                    ch.link(v.tensor_tensor(T[:], all_units(M.eye32[:]), X[:], ALU.subtract))
                    v.transpose(TT[:], T[:]).then_inc(T_ready, 1)
                    for l in range(1, LEVELS):
                        dve.wait_ge(x_ready, i * LEVELS + l + 1)
                        v.tensor_tensor(X[:], bank(XB, 32), all_units(M.level[:, l, :]), ALU.mult).then_inc(X_ready, 1)
                        dve.wait_ge(y_ready, i * (LEVELS - 1) + l)
                        dve.wait_ge(T_ready, i * LEVELS + l)
                        ch.link(v.tensor_tensor(T[:], T[:], bank(YB, 32), ALU.subtract))
                        v.transpose(TT[:], T[:]).then_inc(T_ready, 1)
                    dve.wait_ge(x2_ready, i + 1)
                    v.tensor_copy(X2[32:64], bank(XB, 32)[32:64]).then_inc(X2_ready, 1)
                    dve.wait_ge(y2_ready, i + 1)
                    v.tensor_scalar(TTf[0:32, :, 32:64], bank(2, 32)[0:32], -1.0, None, ALU.mult).then_inc(TT2_ready, 1)
                    dve.wait_ge(x3_ready, i + 1)
                    v.tensor_copy(X3[64:128], bank(3, 64)[64:128]).then_inc(X3_ready, 1)
                    for bb in range(B):
                        dve.wait_ge(Wn_ready, i * B + bb + 1)
                        v.tensor_copy(Us[:, bb * H:(bb + 1) * H, :],
                                      psum[:, 1 + bb, 0:H * (VD + KD)].rearrange("p (u k) -> p u k", k=VD + KD)[:, :, 0:VD])\
                            .then_inc(Us_ready, 1)
                    dve.wait_ge(Us_ready, i * B + B)
                    dve.wait_ge(ws_ready, i + 1)
                    v.tensor_tensor(Dl[:].rearrange("p b v -> p (b v)"), Us[:].rearrange("p u v -> p (u v)"), psum[:, 5, :], ALU.subtract)\
                        .then_inc(delta_ready, 1)
                    dve.wait_ge(s_ready, i + 1)
                    ch.link(v.tensor_tensor(St[:], psum[:, 7, :].rearrange("p (b v) -> p b v", b=B),
                                            M.bmask[:].unsqueeze(1).to_broadcast([P, B, VAL]), ALU.mult))
                    for bb in range(B):
                        v.scalar_tensor_tensor(Sd[:, bb, :], Sd[:, bb, :], M.dec[:, bass.ds(bb * STEPS + i, 1)], St[:, bb, :],
                                               ALU.mult, ALU.add).then_inc(S_ready, 1)
                ch.leave(STEPS)

            @block.tensor
            def _(pe):
                mm = nc.tensor.matmul
                pe.wait_ge(zeroed, 3)

                def blocks(out_bank, left, right):
                    for u in range(U):
                        for n in range(4):
                            blk = slice(32 * n, 32 * n + 32)
                            ins = mm(bank(out_bank, 32)[blk, u, :], left(u, n, blk), right(u, blk), start=True, stop=True)
                    return ins

                with pe.Fori(0, STEPS) as i:
                    pe.wait_ge(staged, i + 1)
                    pe.wait_ge(scaled, i * 4 + 2)
                    for bb in range(B):
                        for n, t in enumerate((ks, kb, qs, qg)):
                            ins = nc.tensor.transpose(psum[:, bb, n * P:(n + 1) * P], t[:, bb, :], ident[:])
                        ins.then_inc(t4_ready, 1)
                    for bb in range(B):
                        pe.wait_ge(gl_ready, i * B + bb + 1)
                        mm(psum[:, 2 + bb, :], M.after[:], gL[:, bb * H:(bb + 1) * H, :].rearrange("p a b -> p (a b)"),
                           start=True, stop=True).then_inc(seg_ready, 1)
                    pe.wait_ge(T4_ready, (i + 1) * B)
                    pe.wait_ge(dec_ready, (i + 1) * B)
                    for bb in range(B):
                        for h in range(H):
                            rows = slice(32 * h, 32 * h + 32)
                            ins = mm(psum[:, h, bb * 256:(bb + 1) * 256], T4[rows, bb, 0, :],
                                     T4[rows, bb, 1:3, :].rearrange("p a b -> p (a b)"), start=True, stop=True)
                    ins.then_inc(kk_ready, 1)
                    wait_alone(pe, M.passed, lt_ready, i + 1)
                    wait_alone(pe, M.passed, ar_ready, i + 1)
                    blocks(XB, lambda u, n, blk: Lt[blk, u, blk], lambda u, blk: M.eye32[blk]).then_inc(x_ready, 1)
                    for l in range(1, LEVELS):
                        wait_alone(pe, M.passed, T_ready, i * LEVELS + l)
                        blocks(XB, lambda u, n, blk: Lt[blk, u, blk], lambda u, blk: T[blk, u, :]).then_inc(x_ready, 1)
                        wait_alone(pe, M.passed, X_ready, i * LEVELS + l + 1)
                        blocks(YB, lambda u, n, blk: TT[blk, u, :], lambda u, blk: X[blk, u, :]).then_inc(y_ready, 1)
                    wait_alone(pe, M.passed, T_ready, (i + 1) * LEVELS)
                    for u in range(U):
                        for n in (0, 2):
                            top, low = slice(32 * n, 32 * n + 32), slice(32 * n + 32, 32 * n + 64)
                            ins = mm(bank(XB, 32)[low, u, :], Lt[top, u, low], T[top, u, :], start=True, stop=True)
                    ins.then_inc(x2_ready, 1)
                    wait_alone(pe, M.passed, X2_ready, i + 1)
                    wait_alone(pe, M.passed, X2b_ready, i + 1)
                    for u in range(U):
                        mm(bank(YB, 32)[32:64, u, :], TT[32:64, u, :], X2[32:64, u, :], start=True, stop=True)
                    for u in range(U):
                        for n in (0, 2):
                            top, low = slice(32 * n, 32 * n + 32), slice(32 * n + 32, 32 * n + 64)
                            ins = mm(bank(2, 32)[top, u, :], X2[low, u, :], TT[low, u, :], start=True, stop=True)
                    ins.then_inc(y2_ready, 1)
                    wait_alone(pe, M.passed, T64_ready, i + 1)
                    wait_alone(pe, M.passed, diag_ready, i * 6 + 6)
                    wait_alone(pe, M.passed, TT2_ready, i * 2 + 2)
                    for u in range(U):
                        ins = mm(bank(3, 64)[64:128, u, :], Lt[0:64, u, 64:128], T64[0:64, u, :], start=True, stop=True)
                    ins.then_inc(x3_ready, 1)
                    wait_alone(pe, M.passed, X3_ready, i + 1)
                    for u in range(U):
                        ins = mm(bank(0, 64)[0:64, u, :], X3[64:128, u, :], TTf[64:128, u, 64:128], start=True, stop=True)
                    ins.then_inc(y3_ready, 1)
                    pe.wait_ge(TTf_ready, i + 1)
                    pe.wait_ge(scaled, i * 4 + 4)
                    for u in range(U):
                        ins = mm(psum[:, 1 + u // H, (u % H) * 96:(u % H + 1) * 96], TTf[:, u, :], R[:, u, :], start=True, stop=True)
                        if u % H == H - 1:
                            ins.then_inc(uw_ready, 1)
                    for bb in range(B):
                        pe.wait_ge(Wn_ready, i * B + bb + 1)
                        ins = nc.tensor.transpose(psum[:, 3, bb * P:(bb + 1) * P],
                                                  Wn[:, bb * H:(bb + 1) * H, :].rearrange("p u k -> p (u k)"), ident[:])
                    ins.then_inc(wt_ready, 1)
                    pe.wait_ge(WT_ready, i + 1)
                    for bb in range(B):
                        ins = mm(psum[:, 5, bb * VAL:(bb + 1) * VAL], WT[:, bb, :], Sd[:, bb, :], start=True, stop=True)
                    ins.then_inc(ws_ready, 1)
                    for bb in range(B):
                        mm(psum[:, 6, bb * VAL:(bb + 1) * VAL], T4[:, bb, 3, :], Sd[:, bb, :], start=(bb == 0), stop=False,
                           skip_group_check=True)
                    pe.wait_ge(delta_ready, i + 1)
                    for bb in range(B):
                        ins = mm(psum[:, 7, bb * VAL:(bb + 1) * VAL], kt[:, bb, :], Dl[:, bb, :], start=True, stop=True)
                    ins.then_inc(s_ready, 1)
                    pe.wait_ge(at_ready, (i + 1) * B)
                    for bb in range(B):
                        for h in range(H):
                            cols = slice(bb * VAL + h * VD, bb * VAL + (h + 1) * VD)
                            ins = mm(psum[:, 6, cols], At[:, bb * H + h, :], Dl[:, bb, h * VD:(h + 1) * VD],
                                     start=False, stop=True, skip_group_check=True)
                    ins.then_inc(o_ready, 1)
                    pe.wait_ge(o_used, i + 1)
                    pe.wait_ge(S_ready, (i + 1) * 2)


def delta_outputs(nc, X, ident, neg_half, psum, W, M):
    with ExitStack() as ctx:
        sb = lambda n, s, dt=F32: ctx.enter_context(nc.sbuf_tensor(f"out_{n}", s, dt))
        sem = Semaphores(ctx, nc, "out")
        sq, o1 = sb("sq", [P, GT, VAL]), sb("o1", [P, GT, VAL])
        ss, r, rt, nh, half = (sb(n, [P, GT * H]) for n in ("ss", "r", "rt", "nh", "half"))
        oT, hT = sb("oT", [P, 2, GW]), sb("hT", [P, GW])
        x1, y, z = sb("x1", [P, GT, D]), sb("y", [P, GT, D]), sb("z", [P, GT, D])
        stats, mv, r2 = sb("stats", [P, GT, 6]), sb("mv", [P, GT, 2]), sb("r2", [P, GT])
        dve_chain, consts = sem("dve_chain"), sem("consts")
        (sq_ready, ss_ready, r_ready, o1_ready, ot_ready, oT_ready, enc_ready, mv_ready, r2_ready, y_ready, ht_ready,
         hT_ready, z_ready, zb_ready, gelu_ready, x_done) = (sem(n) for n in (
            "sq_ready ss_ready r_ready o1_ready ot_ready oT_ready enc_ready mv_ready r2_ready y_ready ht_ready "
            "hT_ready z_ready zb_ready gelu_ready x_done").split())

        def tiles4(ap):
            return ap.unsqueeze(1).to_broadcast([P, GT, D])

        def by_head(ap):
            return ap.rearrange("p t (h v) -> p (t h) v", v=VD)

        with nc.Block() as block:
            @block.vector
            def _(dve):
                v = nc.vector
                ch = Chain(dve, dve_chain, W.passed)
                LINKS = 9
                with dve.Fori(0, GROUPS) as g:
                    ch.turn(g, LINKS)
                    rows = bass.ts(g, GT)
                    dve.wait_ge(sq_ready, g + 1)
                    v.tensor_reduce(ss[:], by_head(sq[:]), AX.X, ALU.add).then_inc(ss_ready, 1)
                    dve.wait_ge(r_ready, g * 3 + 3)
                    ch.link(v.tensor_tensor(by_head(o1[:]), by_head(M.v[:, rows, :]),
                                            r[:].unsqueeze(2).to_broadcast([P, GT * H, VD]), ALU.mult))
                    ch.link(v.tensor_tensor(by_head(o1[:]), by_head(o1[:]),
                                            M.onw[:].unsqueeze(1).to_broadcast([P, GT * H, VD]), ALU.mult))
                    v.tensor_tensor(o1[:], o1[:], M.gate[:, rows, :], ALU.mult).then_inc(o1_ready, 1)
                    dve.wait_ge(enc_ready, g + 1)
                    for t in range(GT):
                        tile = bass.ds(g * GT + t, 1)
                        ins = v.tensor_scalar(x1[:, t, :], X[:, tile, :].rearrange("p o d -> p (o d)"),
                                              M.mean[:, tile, :].rearrange("p o d -> p (o d)"), M.rstd[:, tile],
                                              ALU.subtract, ALU.mult)
                    ch.link(ins)
                    ch.link(v.tensor_tensor(x1[:], psum[:, 2, :].rearrange("p (t d) -> p t d", d=D), x1[:], ALU.add))
                    row_stats(nc, dve, ch, stats, mv, x1).then_inc(mv_ready, 1)
                    dve.wait_ge(r2_ready, g * 2 + 2)
                    for t in range(GT):
                        ins = v.tensor_scalar(y[:, t, :], x1[:, t, :], mv[:, t, 0:1], r2[:, t:t + 1], ALU.subtract, ALU.mult)
                    ch.link(ins)
                    ch.link(v.tensor_tensor(y[:], y[:], tiles4(M.ln2g[:]), ALU.mult))
                    v.tensor_tensor(y[:], y[:], tiles4(M.ln2b[:]), ALU.add).then_inc(y_ready, 1)
                    dve.wait_ge(z_ready, g + 1)
                    v.tensor_tensor(z[:], psum[:, 4, :].rearrange("p (t d) -> p t d", d=D), tiles4(M.b2[:]), ALU.add)\
                        .then_inc(zb_ready, 1)
                    ch.link(v.tensor_tensor(x1[:], x1[:], X[:, rows, :], ALU.add))
                    dve.wait_ge(gelu_ready, g + 1)
                    ch.link(v.tensor_tensor(X[:, rows, :], x1[:], z[:], ALU.add))
                ch.leave(GROUPS)

            @block.gpsimd
            def _(pool):
                nc.gpsimd.memset(nh[:], -0.5).then_inc(consts, 1)
                nc.gpsimd.memset(half[:], 0.5).then_inc(consts, 1)
                pool.wait_ge(consts, 2)
                with pool.Fori(0, GROUPS) as g:
                    wait_alone(pool, W.passed, ss_ready, g + 1)
                    inverse_root(nc, pool, W.passed, r_ready, g * 3, rt[:], ss[:], r[:], 1.0 / VD, RMS_EPS, nh[:])
                    wait_alone(pool, W.passed, r_ready, g * 3 + 2)
                    nc.gpsimd.tensor_tensor(r[:], rt[:], half[:], ALU.mult).then_inc(r_ready, 1)
                    wait_alone(pool, W.passed, mv_ready, g + 1)
                    inverse_root(nc, pool, W.passed, r2_ready, g * 2, r2[:], mv[:, :, 1], rt[:, 0:GT], 1.0, LN_EPS, neg_half[:])

            @block.scalar
            def _(act):
                with act.Fori(0, GROUPS) as g:
                    nc.scalar.activation(sq[:], M.v[:, bass.ts(g, GT), :], ACT.Square).then_inc(sq_ready, 1)
                    act.wait_ge(ot_ready, g + 1)
                    nc.scalar.activation(oT[:], psum[:, 0:2, :], ACT.Copy).then_inc(oT_ready, 1)
                    act.wait_ge(ht_ready, g + 1)
                    nc.scalar.activation(hT[:], psum[:, 3, :], ACT.Copy).then_inc(hT_ready, 1)
                    act.wait_ge(zb_ready, g + 1)
                    nc.scalar.activation(z[:], z[:], ACT.Gelu).then_inc(gelu_ready, 1)

            @block.tensor
            def _(pe):
                with pe.Fori(0, GROUPS) as g:
                    pe.wait_ge(o1_ready, g + 1)
                    for n in range(2):
                        for t in range(GT):
                            ins = nc.tensor.transpose(psum[:, n, t * P:(t + 1) * P], o1[:, t, n * P:(n + 1) * P], ident[:])
                    ins.then_inc(ot_ready, 1)
                    pe.wait_ge(oT_ready, g + 1)
                    for t in range(GT):
                        for n in range(2):
                            ins = nc.tensor.matmul(psum[:, 2, t * D:(t + 1) * D], oT[:, n, t * P:(t + 1) * P], M.wo[:, n, :],
                                                   start=(n == 0), stop=(n == 1))
                    ins.then_inc(enc_ready, 1)
                    pe.wait_ge(y_ready, g + 1)
                    for t in range(GT):
                        ins = nc.tensor.transpose(psum[:, 3, t * P:(t + 1) * P], y[:, t, :], ident[:])
                    ins.then_inc(ht_ready, 1)
                    pe.wait_ge(hT_ready, g + 1)
                    for t in range(GT):
                        ins = nc.tensor.matmul(psum[:, 4, t * D:(t + 1) * D], hT[:, t * P:(t + 1) * P], M.w2[:],
                                               start=True, stop=True)
                    ins.then_inc(z_ready, 1)


def gated_delta(nc, X, ident, neg_half, psum, W, A):
    with ExitStack() as ctx:
        sb = lambda n, s, dt=F32: ctx.enter_context(nc.sbuf_tensor(f"gd_{n}", s, dt))
        M = Holder()
        M.passed = W.passed
        M.mean, M.rstd = sb("mean", [P, TILES, 1]), sb("rstd", [P, TILES])
        M.q, M.k = sb("q", [P, TILES, KEY]), sb("k", [P, TILES, KEY])
        M.v, M.gate = sb("v", [P, TILES, VAL]), sb("gate", [P, TILES, VAL])
        M.ab = sb("ab", [P, TILES, 2 * H])
        M.g, M.beta, M.gam, M.kap = (sb(n, [P, TILES, H]) for n in ("g", "beta", "gam", "kap"))
        M.dec = sb("dec", [P, TILES])
        M.wq, M.wk, M.wv, M.wg = sb("wq", [P, KEY]), sb("wk", [P, KEY]), sb("wv", [P, VAL]), sb("wg", [P, VAL])
        M.wab, M.wo, M.w2 = sb("wab", [P, 2 * H]), sb("wo", [P, 2, D]), sb("w2", [P, D])
        M.ln1g, M.ln1b, M.ln2g, M.ln2b, M.b2 = (sb(n, [P, D]) for n in ("ln1g", "ln1b", "ln2g", "ln2b", "b2"))
        M.rmsw, M.convw, M.onw = sb("rmsw", [P, 1]), sb("convw", [P, 4, CONV]), sb("onw", [P, VD])
        M.dtb, M.alog = sb("dtb", [P, H]), sb("alog", [P, H])
        consts = sb("masks", [P, MASK_COLS])
        M.upto, M.after, M.ones = (consts[:, n * P:(n + 1) * P] for n in range(3))
        M.bmask, M.hmask = consts[:, 384:640], consts[:, 640:644]
        M.eye32, M.level = consts[:, 644:676], consts[:, 676:836].rearrange("p (l k) -> p l k", k=32)
        a = lambda n: A[f"L1_attn_{n}"]
        row = lambda n: a(n).partition_broadcast(P)
        M.loads = [
            (M.wq[:], a("Wq")), (M.wk[:], a("Wk")), (M.wv[:], a("Wv")), (M.wg[:], a("Wg")),
            (M.wab[:, 0:H], a("Wa")), (M.wab[:, H:], a("Wb")), (M.wo[:], a("Wo").rearrange("(n p) d -> p n d", p=P)),
            (M.w2[:], a("W2")), (M.ln1g[:], row("ln1_g")), (M.ln1b[:], row("ln1_b")), (M.ln2g[:], row("ln2_g")),
            (M.ln2b[:], row("ln2_b")), (M.b2[:], row("b2")), (M.rmsw[:], a("rms_in_w").unsqueeze(1)),
            (M.convw[:, 0, :], a("conv_q_w")), (M.convw[:, 1, :], a("conv_k_w")),
            (M.convw[:, 2:4, :], a("conv_v_w").rearrange("(n p) i -> p n i", p=P)), (M.onw[:], row("o_norm_w")),
            (M.dtb[:], row("dt_bias")), (M.alog[:], row("A_log")), (consts[:], A["masks"]),
        ]
        M.n_loads = len(M.loads)
        delta_inputs(nc, X, ident, neg_half, psum, W, M)
        delta_decays(nc, psum, M)
        delta_scan(nc, ident, psum, M)
        delta_outputs(nc, X, ident, neg_half, psum, W, M)

MASK_COLS = 836


def masks():
    import numpy as np
    r, c = np.arange(P)[:, None], np.arange(P)[None, :]
    upto, after, ones = r <= c, r > c, np.ones((P, P))
    bmask = (r // KD) == (np.arange(VAL)[None, :] // VD)
    hmask = (r // KD) == np.arange(H)[None, :]
    c32 = np.arange(32)[None, :]
    eye = (r % 32) == c32
    level = [(((r % 32) // n) % 2 == 1) & (c32 // n == (r % 32) // n - 1) for n in (1, 2, 4, 8, 16)]
    return np.concatenate([upto, after, ones, bmask, hmask, eye] + level, axis=1).astype(np.float32)


def build(nc, A, out, phases=(0,1,2,3,4,5)):
    ctx = ExitStack()
    with ctx:
        sb = lambda n, s, dt=F32: ctx.enter_context(nc.sbuf_tensor(n, s, dt))
        sem = lambda n: ctx.enter_context(nc.semaphore(n))
        X = sb("X", [P, TILES, D])
        ident = sb("ident", [P, P])
        neg_half = sb("neg_half", [P, GT])
        psum = ctx.enter_context(nc.psum_tensor("psum", [P, 8, 512], F32))
        W = Holder()
        W.passed = sem("passed")
        rw = sb("rw", [P, E])
        W.ewh, W.ewl = sb("ewh", [P, E * D], F32R), sb("ewl", [P, E * D], F32R)
        W.rb, W.rank = sb("rb", [P, E]), sb("rank", [P, E])
        wraw = sb("wraw", [P, 3, D])
        gw, b1raw = sb("gw", [P, E]), sb("b1raw", [E * FC, P])
        W.gw, W.rw = gw, rw
        W.gb, W.b1T = sb("gb", [P, E]), sb("b1T", [P, E * FC])
        b1T_ready = sem("b1T_ready")
        W.wqh, W.wkh, W.wql, W.wkl = (sb(n, [P, D], F32R) for n in ("wqh", "wkh", "wql", "wkl"))
        W.wv = sb("wv", [P, D])
        W.bq, W.bk, W.bvb = sb("bq", [P, 1]), sb("bk", [P, 1]), sb("bvb", [P, D])
        qkvT_ready, ident_ready = sem("qkvT_ready"), sem("ident_ready")
        x_loaded, w_loaded = sem("x_loaded"), sem("w_loaded")
        consts_ready, ident_zero, ranks = sem("consts_ready"), sem("ident_zero"), sem("ranks")
        w_high, w_low = sem("w_high"), sem("w_low")

        x_dram = A["L0_attn_x"].rearrange("b (t p) d -> p (b t) d", p=P)
        with nc.sbuf_tensor("ew", [P, E * D], F32) as ew, nc.Block() as block:
            @block.sync
            def _(sp):
                sp.dma_start(ew[:].rearrange("p (e d) -> p e d", d=D),
                             A["L0_ffn_expert_w"].rearrange("e h d -> h e d")).then_inc(w_loaded, 16)
                sp.dma_start(rw[:], A["L0_ffn_router_w"]).then_inc(w_loaded, 16)
                sp.dma_start(W.rb[:], A["L0_ffn_router_b"].partition_broadcast(P)).then_inc(w_loaded, 16)
                for n, w in enumerate(("wq", "wk", "wv")):
                    sp.dma_start(wraw[:, n, :], A[f"L0_attn_{w}"]).then_inc(w_loaded, 16)
                sp.dma_start(W.bq[:], A["L0_attn_bq"].unsqueeze(1)).then_inc(w_loaded, 16)
                sp.dma_start(W.bk[:], A["L0_attn_bk"].unsqueeze(1)).then_inc(w_loaded, 16)
                sp.dma_start(W.bvb[:], A["L0_attn_bv"].partition_broadcast(P)).then_inc(w_loaded, 16)
                sp.dma_start(gw[:], A["L1_ffn_gate_w"]).then_inc(w_loaded, 16)
                sp.dma_start(W.gb[:], A["L1_ffn_gate_b"].partition_broadcast(P)).then_inc(w_loaded, 16)
                sp.dma_start(b1raw[:], A["L1_ffn_b1"].rearrange("e (c p) -> (e c) p", p=P)).then_inc(w_loaded, 16)
                sp.dma_start(X[:], x_dram).then_inc(x_loaded, 16)

            @block.gpsimd
            def _(pool):
                nc.gpsimd.memset(ident[:], 0.0).then_inc(ident_zero, 1)
                pool.wait_ge(ident_zero, 1)
                nc.gpsimd.affine_select(ident[:], ident[:], [[-1, P]], ALU.not_equal, 1.0, base=0,
                                        channel_multiplier=1).then_inc(consts_ready, 1)
                nc.gpsimd.memset(neg_half[:], -0.5).then_inc(consts_ready, 1)
                for e in range(E):
                    nc.gpsimd.memset(W.rank[:, e:e + 1], float(E - e)).then_inc(consts_ready, 1)
                pool.wait_ge(x_loaded, 16)

            @block.scalar
            def _(act):
                act.wait_ge(w_loaded, 192)
                nc.scalar.activation(W.ewh[:], ew[:], ACT.Copy).then_inc(w_high, 1)
                act.wait_ge(b1T_ready, 1)
                nc.scalar.activation(W.b1T[:], psum[:, 1, 0:E * FC], ACT.Copy)
                act.wait_ge(qkvT_ready, 1)
                for n, h in enumerate((W.wqh, W.wkh, W.wv)):
                    nc.scalar.activation(h[:], psum[:, 0, n * D:(n + 1) * D], ACT.Copy).then_inc(w_high, 1)

            @block.tensor
            def _(pe):
                pe.wait_ge(w_loaded, 192)
                pe.wait_ge(consts_ready, 1)
                nc.tensor.transpose(psum[:, 1, 0:E * FC], b1raw[:], ident[0:E * FC, 0:E * FC]).then_inc(b1T_ready, 1)
                for n in range(3):
                    ins = nc.tensor.transpose(psum[:, 0, n * D:(n + 1) * D], wraw[:, n, :], ident[:])
                ins.then_inc(qkvT_ready, 1)

            @block.vector
            def _(dve):
                dve.wait_ge(w_high, 1)
                nc.vector.tensor_tensor(W.ewl[:], ew[:], W.ewh[:].bitcast(F32), ALU.subtract).then_inc(w_low, 1)
                dve.wait_ge(w_high, 4)
                for n, (h, l) in enumerate(((W.wqh, W.wql), (W.wkh, W.wkl))):
                    nc.vector.tensor_tensor(l[:], psum[:, 0, n * D:(n + 1) * D], h[:].bitcast(F32),
                                            ALU.subtract).then_inc(w_low, 1)

        for p in phases:
            if p == 0:
                first_mixture(nc, "mix1", X, ident, psum, W, A)
            if p == 1:
                attention(nc, "attn", X, ident, neg_half, psum, W)
            if p in (3, 5):
                second_mixture(nc, f"ffn{p}", X, ident, neg_half, psum, W, A)
            if p == 4:
                gated_delta(nc, X, ident, neg_half, psum, W, A)
            if p == 2:
                first_mixture(nc, "mix2", X, ident, psum, W, A)
        stored = sem("stored")
        with nc.Block() as block:
            @block.sync
            def _(sp):
                sp.dma_start(out.rearrange("b (t p) d -> p (b t) d", p=P), X[:]).then_inc(stored, 16)
                sp.wait_ge(stored, 16)


_L1_ATTN = ["ln1_g", "ln1_b", "ln2_g", "ln2_b", "rms_in_w", "Wq", "Wk", "Wv", "conv_q_w", "conv_k_w", "conv_v_w",
            "Wa", "dt_bias", "A_log", "Wb", "Wg", "o_norm_w", "Wo", "W2", "b2"]
_INS = (["L0_attn_" + n for n in ("x", "wq", "bq", "wk", "bk", "wv", "bv")]
        + ["L0_ffn_" + n for n in ("router_w", "router_b", "expert_w", "expert_b")]
        + ["L1_attn_" + n for n in _L1_ATTN]
        + ["L1_ffn_" + n for n in ("gate_w", "gate_b", "w1", "b1", "w2", "b2")])


def kernel(**inputs):
    import numpy as _np
    import concourse.bacc as _bacc
    from concourse import mybir as _mybir
    from concourse.bass_utils import run_bass_kernel_spmd as _run

    nc = _bacc.Bacc("TRN2", target_bir_lowering=False, num_devices=1)
    arrays, access = {}, {}
    for name in _INS + ["masks"]:
        a = masks() if name == "masks" else _np.ascontiguousarray(inputs[name])
        arrays[f"in_{name}_dram"] = a
        access[name] = nc.dram_tensor(f"in_{name}_dram", a.shape, _mybir.dt.from_np(a.dtype),
                                      kind="ExternalInput").ap()
    out = nc.dram_tensor("out_0_dram", (B, S, D), _mybir.dt.float32, kind="ExternalOutput").ap()
    build(nc, access, out)
    r = _run(nc, [arrays], core_ids=[0])
    return r.results[0]["out_0_dram"]
```

```python
import concourse.bass as bass
from concourse import mybir
from contextlib import ExitStack

F32 = mybir.dt.float32
F32R = mybir.dt.float32r
ALU = mybir.AluOpType
ACT = mybir.ActivationFunctionType
AX = mybir.AxisListType

P = 128
B, S, D = 2, 2048, 128
TILES = B * S // P
GT = 4
GROUPS = TILES // GT
GW = GT * P
E = 8
F = 512
FC = F // P
LN_EPS = 1e-5


def wait_alone(eng, passed, sem, value):
    eng.wait_ge(sem, value)
    eng.sem_inc(passed, 1)


class Semaphores:

    def __init__(self, ctx, nc, name):
        self.nc, self.name, self.held, self.stack = nc, name, [], ExitStack()
        ctx.callback(self.clear)

    def __call__(self, name):
        self.held.append(self.stack.enter_context(self.nc.semaphore(f"{self.name}_{name}")))
        return self.held[-1]

    def clear(self):
        with self.nc.Block() as block:
            @block.gpsimd
            def _(pool):
                numbers = sorted(s.num for s in self.held)
                while numbers:
                    n = 1
                    while n < len(numbers) and numbers[n] == numbers[0] + n:
                        n += 1
                    pool.sem_clear(range(numbers[0], numbers[0] + n))
                    numbers = numbers[n:]
        self.stack.close()


class Chain:

    def __init__(self, eng, sem, passed=None):
        self.eng, self.sem, self.base, self.n, self.outer = eng, sem, 0, 0, []
        self.passed = passed

    def turn(self, i, per):
        self.outer.append((self.base, self.n, per))
        self.base, self.n = self.base + self.n + i * per, 0

    def leave(self, count):
        base, n, per = self.outer.pop()
        assert self.n == per, ("links in a pass", self.n, per)
        self.base, self.n = base, n + count * per

    def mark(self, ins):
        ins.then_inc(self.sem, 1)
        self.n += 1
        return self.base + self.n

    def link(self, ins):
        self.eng.wait_ge(self.sem, self.mark(ins))

    def link_alone(self, ins):
        wait_alone(self.eng, self.passed, self.sem, self.mark(ins))


def three_products(nc, out, left, right, start=True, stop=True):
    (lh, ll), (rh, rl) = left, right
    for n, (a, b) in enumerate(((lh, rh), (lh, rl), (ll, rh))):
        ins = nc.tensor.matmul(out, a, b, start=(start and n == 0), stop=(stop and n == 2))
    return ins


class WholeFront:

    PARTS = slice(0, 2 * GT), slice(2 * GT, TILES)

    def __init__(self, ctx, sem, nc, name, X, ident, psum, banks, W, known=False):
        self.nc, self.X, self.ident, self.psum, self.banks, self.W = nc, X, ident, psum, banks, W
        self.mv, self.known, self.passed = W.mv, known, W.passed
        sb = lambda n, s, dt=F32: ctx.enter_context(nc.sbuf_tensor(f"{name}_{n}", s, dt))
        if not known:
            self.stats = sb("stats", [P, TILES, 6])
        self.veps, self.rstd, self.power = sb("var_eps", [P, TILES]), sb("rstd", [P, TILES]), sb("power", [P, TILES])
        self.xn = sb("xn", [P, 2, GT, D])
        self.power_ready, self.var_ready, self.veps_ready, self.rstd_ready = (
            sem("power_ready"), sem("var_ready"), sem("veps_ready"), sem("rstd_ready"))
        self.xn_ready, self.xt_ready = sem("xn_ready"), sem("xt_ready")

    def rows(self, g):
        return self.X[:, bass.ts(g, GT), :]

    def vector_stats(self, dve, chain):
        nc = self.nc
        for part in () if self.known else self.PARTS:
            for t in range(part.start, part.stop):
                ins = nc.vector.bn_stats(self.stats[:, t, :], self.X[:, t, :])
            chain.link(ins)
            for t in range(part.start, part.stop):
                ins = nc.vector.bn_aggr(self.mv[:, t, :], self.stats[:, t, :])
            ins.then_inc(self.var_ready, 1)

    def gpsimd_rstd(self, pool):
        nc = self.nc
        nc.gpsimd.memset(self.power[:], -0.5).then_inc(self.power_ready, 1)
        pool.wait_ge(self.power_ready, 1)
        for n, part in enumerate(self.PARTS):
            if not self.known:
                pool.wait_ge(self.var_ready, n + 1)
            nc.gpsimd.tensor_scalar(self.veps[:, part], self.mv[:, part, 1], LN_EPS, None, ALU.add)\
                .then_inc(self.veps_ready, 1)
            pool.wait_ge(self.veps_ready, n + 1)
            nc.gpsimd.tensor_tensor(self.rstd[:, part], self.veps[:, part], self.power[:, part], ALU.pow)\
                .then_inc(self.rstd_ready, 1)

    def vector_normalize(self, dve, g, par, first=False):
        if first:
            dve.wait_ge(self.rstd_ready, 1)
        else:
            dve.wait_ge(self.rstd_ready, 2)
            dve.wait_ge(self.xt_ready, g - 1)
        for t in range(GT):
            tile = bass.ds(g * GT + t, 1)
            row = lambda ap: ap.rearrange("p o d -> p (o d)")
            ins = self.nc.vector.tensor_scalar(self.xn[:, par, t, :], row(self.X[:, tile, :]),
                                               row(self.mv[:, tile, 0:1]), self.rstd[:, tile],
                                               ALU.subtract, ALU.mult)
        ins.then_inc(self.xn_ready, 1)

    def tensor_transpose(self, pe, g, par):
        pe.wait_ge(self.xn_ready, g + 1)
        for t in range(GT):
            ins = self.nc.tensor.transpose(self.psum[:, self.banks[par], t * P:(t + 1) * P],
                                           self.xn[:, par, t, :], self.ident[:])
        ins.then_inc(self.xt_ready, 1)


class Router(WholeFront):

    def __init__(self, ctx, sem, nc, name, X, ident, psum, W, router_w, router_b, biases=False, known=False):
        super().__init__(ctx, sem, nc, name, X, ident, psum, (0, 1), W, known)
        sb = lambda n, s, dt=F32: ctx.enter_context(nc.sbuf_tensor(f"{name}_{n}", s, dt))
        self.router_w, self.router_b = router_w, router_b
        self.LOGITS, self.CT, self.BIAS = (6, 7), 6, (6, 7)
        self.xh, self.xl = sb("xh", [P, GROUPS, GW], F32R), sb("xl", [P, GROUPS, GW], F32R)
        self.xT = sb("xT", [P, 2, GW])
        self.lg, self.ex = sb("logits", [P, TILES, E]), sb("exps", [P, TILES, E])
        self.one, self.two, self.tmp = (sb(n, [P, TILES, E]) for n in ("one", "two", "tmp"))
        self.top, self.tot, self.pick = (sb(n, [P, TILES]) for n in ("top", "total", "pick"))
        self.coef = sb("coef", [P, TILES, E])
        self.coefT = sb("coefT", [P, 2, P])
        if biases:
            self.bdiag = sb("bdiag", [P, TILES // 2 * D])
        self.diag_zero, self.bias_loaded = sem("diag_zero"), sem("bias_loaded")
        self.high_ready, self.xT_ready, self.low_ready = sem("high_ready"), sem("xT_ready"), sem("low_ready")
        self.logits_ready, self.logits_used = sem("logits_ready"), sem("logits_used")
        self.shifted_ready, self.exp_ready, self.coef_ready = sem("shifted_ready"), sem("exp_ready"), sem("coef_ready")
        self.ct_ready, self.coefT_ready, self.bias_ready, self.bias_used = (
            sem("ct_ready"), sem("coefT_ready"), sem("bias_ready"), sem("bias_used"))

    def flat(self, t, g):
        return t[:, bass.ds(g, 1), :].rearrange("p o d -> p (o d)")

    def each(self, ap):
        return ap.unsqueeze(2).to_broadcast([P, TILES, E])

    def vector_front(self, dve, chain):
        nc = self.nc

        def low(g, par):
            dve.wait_ge(self.high_ready, g + 1)
            nc.vector.tensor_tensor(self.flat(self.xl, g), self.psum[:, self.banks[par], :],
                                    self.flat(self.xh, g).bitcast(F32), ALU.subtract).then_inc(self.low_ready, 1)

        def add_bias(g, par):
            dve.wait_ge(self.logits_ready, g + 1)
            nc.vector.tensor_tensor(
                self.lg[:, bass.ts(g, GT), :],
                self.psum[:, self.LOGITS[par], 0:GT * E].rearrange("p (t e) -> p t e", e=E),
                self.router_b.unsqueeze(1).to_broadcast([P, GT, E]), ALU.add).then_inc(self.logits_used, 1)

        self.vector_stats(dve, chain)
        self.vector_normalize(dve, 0, 0, first=True)
        self.vector_normalize(dve, 1, 1, first=True)
        low(0, 0)
        with dve.Fori(0, GROUPS // 2 - 1) as j:
            for par in range(2):
                self.vector_normalize(dve, j * 2 + par + 2, par)
                low(j * 2 + par + 1, 1 - par)
                add_bias(j * 2 + par, par)
        low(GROUPS - 1, 1)
        add_bias(GROUPS - 2, 0)
        add_bias(GROUPS - 1, 1)
        dve.wait_ge(self.logits_used, GROUPS)

    def vector_first(self, chain, mask):
        v, rank = self.nc.vector, self.W.rank[:].unsqueeze(1).to_broadcast([P, TILES, E])
        chain.link(v.tensor_tensor(mask[:], mask[:], rank, ALU.mult))
        chain.link(v.tensor_reduce(self.pick[:], mask[:], AX.X, ALU.max))
        chain.link(v.tensor_tensor(mask[:], mask[:], self.each(self.pick[:]), ALU.is_equal))

    def vector_best(self, chain):
        v = self.nc.vector
        chain.link(v.tensor_reduce(self.top[:], self.lg[:], AX.X, ALU.max))
        v.tensor_tensor(self.ex[:], self.lg[:], self.each(self.top[:]), ALU.subtract).then_inc(self.shifted_ready, 1)
        chain.link(v.tensor_tensor(self.one[:], self.lg[:], self.each(self.top[:]), ALU.is_equal))
        self.vector_first(chain, self.one)

    def vector_top1(self, dve, chain):
        v = self.nc.vector
        self.vector_best(chain)
        dve.wait_ge(self.exp_ready, 1)
        chain.link(v.tensor_reduce(self.tot[:], self.ex[:], AX.X, ALU.add))
        chain.link(v.reciprocal(self.top[:], self.tot[:]))
        v.scalar_tensor_tensor(self.coef[:], self.one[:], 0.5, self.each(self.top[:]), ALU.mult, ALU.mult)\
            .then_inc(self.coef_ready, 1)
        dve.wait_ge(self.coef_ready, 1)

    def vector_top2(self, dve, chain):
        v, one, two, tmp, ex = self.nc.vector, self.one, self.two, self.tmp, self.ex
        self.vector_best(chain)
        chain.link(v.scalar_tensor_tensor(tmp[:], one[:], -3e38, self.lg[:], ALU.mult, ALU.add))
        chain.link(v.tensor_reduce(self.top[:], tmp[:], AX.X, ALU.max))
        chain.link(v.tensor_tensor(two[:], tmp[:], self.each(self.top[:]), ALU.is_equal))
        self.vector_first(chain, two)
        chain.link(v.tensor_tensor(one[:], one[:], two[:], ALU.add))
        dve.wait_ge(self.exp_ready, 1)
        chain.link(v.tensor_tensor(one[:], one[:], ex[:], ALU.mult))
        chain.link(v.tensor_reduce(self.tot[:], one[:], AX.X, ALU.add))
        chain.link(v.reciprocal(self.top[:], self.tot[:]))
        v.scalar_tensor_tensor(self.coef[:], one[:], 0.5, self.each(self.top[:]), ALU.mult, ALU.mult)\
            .then_inc(self.coef_ready, 1)
        dve.wait_ge(self.coef_ready, 1)

    def vector_bias(self, dve, g):
        dve.wait_ge(self.bias_ready, g + 1)
        x = self.rows(g)
        self.nc.vector.tensor_tensor(x, self.psum[:, self.BIAS[g % 2], :].rearrange("p (t d) -> p t d", d=D), x,
                                     ALU.add).then_inc(self.bias_used, 1)

    def gpsimd_front(self, pool):
        self.gpsimd_rstd(pool)
        self.nc.gpsimd.memset(self.bdiag[:], 0.0).then_inc(self.diag_zero, 1)

    def sync_bias(self, sp, bias):
        sp.wait_ge(self.diag_zero, 1)
        for t in range(TILES // 2):
            sp.dma_start(self.bdiag[t * E:(t + 1) * E, t * D:(t + 1) * D], bias).then_inc(self.bias_loaded, 16)

    def scalar_front(self, act):
        nc = self.nc

        def parts(g, par):
            act.wait_ge(self.xt_ready, g + 1)
            nc.scalar.activation(self.xT[:, par, :], self.psum[:, self.banks[par], :], ACT.Copy)\
                .then_inc(self.xT_ready, 1)
            nc.scalar.activation(self.flat(self.xh, g), self.psum[:, self.banks[par], :], ACT.Copy)\
                .then_inc(self.high_ready, 1)

        with act.Fori(0, GROUPS // 2) as j:
            parts(j * 2, 0)
            parts(j * 2 + 1, 1)

    def scalar_exp(self, act):
        act.wait_ge(self.shifted_ready, 1)
        self.nc.scalar.activation(self.ex[:], self.ex[:], ACT.Exp).then_inc(self.exp_ready, 1)

    def scalar_coef_rows(self, act):
        act.wait_ge(self.ct_ready, 1)
        self.nc.scalar.activation(self.coefT[:].rearrange("p a b -> p (a b)"), self.psum[:, self.CT, 0:2 * P], ACT.Copy)\
            .then_inc(self.coefT_ready, 1)

    def tensor_front(self, pe):
        nc = self.nc

        def logits(g, par, first=False):
            pe.wait_ge(self.xT_ready, g + 1)
            if not first:
                pe.wait_ge(self.logits_used, g - 1)
            for t in range(GT):
                tok = slice(t * P, (t + 1) * P)
                ins = nc.tensor.matmul(self.psum[:, self.LOGITS[par], t * E:(t + 1) * E], self.xT[:, par, tok],
                                       self.router_w, start=True, stop=True)
            ins.then_inc(self.logits_ready, 1)

        self.tensor_transpose(pe, 0, 0)
        self.tensor_transpose(pe, 1, 1)
        for par in range(2):
            logits(par, par, first=True)
            pe.wait_ge(self.low_ready, par + 1)
            self.tensor_transpose(pe, par + 2, par)
        with pe.Fori(1, GROUPS // 2 - 1) as j:
            for par in range(2):
                logits(j * 2 + par, par)
                pe.wait_ge(self.low_ready, j * 2 + par + 1)
                self.tensor_transpose(pe, j * 2 + par + 2, par)
        logits(GROUPS - 2, 0)
        logits(GROUPS - 1, 1)
        pe.wait_ge(self.low_ready, GROUPS)

    def tensor_coef(self, pe):
        nc = self.nc
        pe.wait_ge(self.coef_ready, 1)
        for n in range(2):
            ins = nc.tensor.transpose(self.psum[:, self.CT, n * P:(n + 1) * P],
                                      self.coef[:, n * TILES // 2:(n + 1) * TILES // 2, :]
                                      .rearrange("p t e -> p (t e)"), self.ident[:])
        ins.then_inc(self.ct_ready, 1)

    def tensor_bias(self, pe, g):
        if g == 0:
            pe.wait_ge(self.coefT_ready, 1)
            pe.wait_ge(self.bias_loaded, TILES // 2 * 16)
        if g >= 2:
            pe.wait_ge(self.bias_used, g - 1)
        n, q = g // (GROUPS // 2), g % (GROUPS // 2)
        self.nc.tensor.matmul(self.psum[:, self.BIAS[g % 2], :], self.coefT[:, n, :],
                              self.bdiag[:, q * GW:(q + 1) * GW], start=True, stop=True).then_inc(self.bias_ready, 1)


def first_mixture(nc, name, X, ident, psum, W, A, known=False):
    with ExitStack() as ctx:
        sb = lambda n, s, dt=F32: ctx.enter_context(nc.sbuf_tensor(f"{name}_{n}", s, dt))
        sem = Semaphores(ctx, nc, name)
        ro = Router(ctx, sem, nc, name, X, ident, psum, W, W.rw[:], W.rb[:], biases=True, known=known)
        coef = ro.coef
        sh, sl = sb("staged_high", [P, 2, GW], F32R), sb("staged_low", [P, 2, GW], F32R)
        side = sb("side", [P, 4, E // 2, D])
        pairs, total = sb("pairs", [P, 2, 2, D]), sb("side_total", [P, 4, D])
        dve_chain = sem("dve_chain")
        staged, experts_ready, side_ready, pairs_ready, total_ready, x_ready, added = (
            sem("staged"), sem("experts_ready"), sem("side_ready"), sem("pairs_ready"), sem("total_ready"),
            sem("x_ready"), sem("added"))

        def weight(t, e):
            return coef[:, bass.ds(t, 1), e:e + 1].rearrange("p o d -> p (o d)")

        def out(n, e):
            return psum[:, 2 * n + e // 4, (e % 4) * D:(e % 4 + 1) * D]

        with nc.Block() as block:
            @block.vector
            def _(dve):
                chain = Chain(dve, dve_chain, W.passed)

                def combine(g, n):
                    last = {}
                    for e in range(E // 2):
                        for k in (n, n + 1):
                            if e == 0:
                                dve.wait_ge(experts_ready, g * GT + k + 1)
                            else:
                                dve.wait_ge(dve_chain, last[k])
                            x = ro.flat(X, g * GT + k)
                            ins = nc.vector.scalar_tensor_tensor(x, out(k, e), weight(g * GT + k, e), x,
                                                                 ALU.mult, ALU.add)
                            if e < E // 2 - 1:
                                last[k] = chain.mark(ins)
                            else:
                                ins.then_inc(x_ready, 1)

                def add_side(g, n):
                    for k in (n, n + 1):
                        dve.wait_ge(total_ready, g * GT + k + 1)
                        dve.wait_ge(x_ready, g * GT + k + 1)
                        x = ro.flat(X, g * GT + k)
                        nc.vector.tensor_tensor(x, x, total[:, k, :], ALU.add).then_inc(added, 1)

                ro.vector_front(dve, chain)
                ro.vector_top1(dve, chain)
                combine(0, 0)
                with dve.Fori(0, GROUPS - 1) as g:
                    chain.turn(g, 4 * (E // 2 - 1))
                    combine(g, 2)
                    add_side(g, 0)
                    combine(g + 1, 0)
                    add_side(g, 2)
                chain.leave(GROUPS - 1)
                combine(GROUPS - 1, 2)
                add_side(GROUPS - 1, 0)
                add_side(GROUPS - 1, 2)
                dve.wait_ge(added, TILES)
                for g in range(GROUPS):
                    ro.vector_bias(dve, g)

            @block.gpsimd
            def _(pool):
                def add_up(g, k, first=False):
                    t = g * GT + k
                    pool.wait_ge(side_ready, (t + 1) * (E // 2))
                    if not first or k >= 2:
                        pool.wait_ge(total_ready, t - 1)
                    nc.gpsimd.tensor_tensor(pairs[:, k % 2], side[:, k, 0:2, :], side[:, k, 2:4, :], ALU.add)\
                        .then_inc(pairs_ready, 1)
                    pool.wait_ge(pairs_ready, t + 1)
                    if not first:
                        pool.wait_ge(added, t - 3)
                    nc.gpsimd.tensor_tensor(total[:, k, :], pairs[:, k % 2, 0, :], pairs[:, k % 2, 1, :], ALU.add)\
                        .then_inc(total_ready, 1)

                ro.gpsimd_front(pool)
                for k in range(GT):
                    add_up(0, k, first=True)
                with pool.Fori(1, GROUPS) as g:
                    for k in range(GT):
                        add_up(g, k)

            @block.sync
            def _(sp):
                ro.sync_bias(sp, A["L0_ffn_expert_b"])

            @block.scalar
            def _(act):
                def stage(g, par):
                    nc.scalar.activation(sh[:, par, :], ro.flat(ro.xh, g), ACT.Copy)
                    nc.scalar.activation(sl[:, par, :], ro.flat(ro.xl, g), ACT.Copy).then_inc(staged, 1)

                def weigh_side(g, k, first=False):
                    t = g * GT + k
                    wait_alone(act, W.passed, experts_ready, t + 1)
                    if not first:
                        wait_alone(act, W.passed, pairs_ready, t - 3)
                    for e in range(E // 2, E):
                        nc.scalar.activation(side[:, k, e - E // 2, :], out(k, e), ACT.Copy, scale=weight(t, e))\
                            .then_inc(side_ready, 1)

                ro.scalar_front(act)
                act.wait_ge(ro.low_ready, 2)
                stage(0, 0)
                stage(1, 1)
                ro.scalar_exp(act)
                ro.scalar_coef_rows(act)
                for k in range(GT):
                    weigh_side(0, k, first=True)
                stage(2, 0)
                for k in range(GT):
                    weigh_side(1, k)
                with act.Fori(1, GROUPS // 2 - 1) as j:
                    for par in range(2):
                        stage(j * 2 + par + 1, 1 - par)
                        for k in range(GT):
                            weigh_side(j * 2 + par, k)
                stage(GROUPS - 1, 1)
                for k in range(GT):
                    weigh_side(GROUPS - 2, k)
                for k in range(GT):
                    weigh_side(GROUPS - 1, k)

            @block.tensor
            def _(pe):
                def experts(g, par, k, first=False):
                    tok = slice(k * P, (k + 1) * P)
                    if not first:
                        pe.wait_ge(x_ready, g * GT + k - 3)
                        pe.wait_ge(side_ready, (g * GT + k - 3) * (E // 2))
                    for half in range(2):
                        cols = slice(half * 4 * D, (half + 1) * 4 * D)
                        ins = three_products(nc, psum[:, 2 * k + half, :], (sh[:, par, tok], sl[:, par, tok]),
                                             (W.ewh[:, cols], W.ewl[:, cols]))
                    ins.then_inc(experts_ready, 1)

                ro.tensor_front(pe)
                pe.wait_ge(staged, 1)
                experts(0, 0, 0, first=True)
                experts(0, 0, 1, first=True)
                ro.tensor_coef(pe)
                pe.wait_ge(ro.coefT_ready, 1)
                experts(0, 0, 2, first=True)
                experts(0, 0, 3, first=True)
                pe.wait_ge(staged, 2)
                for k in range(GT):
                    experts(1, 1, k)
                with pe.Fori(1, GROUPS // 2) as j:
                    for par in range(2):
                        pe.wait_ge(staged, j * 2 + par + 1)
                        for k in range(GT):
                            experts(j * 2 + par, par, k)
                pe.wait_ge(x_ready, TILES)
                pe.wait_ge(side_ready, TILES * (E // 2))
                for g in range(GROUPS):
                    ro.tensor_bias(pe, g)


def attention(nc, name, X, ident, psum, W):
    SCALE = float(D) ** -0.5
    NC = S // 512
    QT = S // P
    with ExitStack() as ctx:
        sb = lambda n, s, dt=F32: ctx.enter_context(nc.sbuf_tensor(f"{name}_{n}", s, dt))
        sem = Semaphores(ctx, nc, name)
        XB, KB, QB, VB = (0, 1), (2, 3), (4, 5), (6, 7)
        TB, OB = (4, 5), (6, 7)
        fr = WholeFront(ctx, sem, nc, name, X, ident, psum, XB, W)
        xh, xl, xT = sb("xh", [P, 2, GW], F32R), sb("xl", [P, 2, GW], F32R), sb("xT", [P, 2, GW])
        kh, kl = sb("kh", [P, B * S], F32R), sb("kl", [P, B * S], F32R)
        qh, ql = sb("qh", [P, B * S], F32R), sb("ql", [P, B * S], F32R)
        v = sb("v", [P, TILES, D])
        qsh, qsl = sb("qsh", [P, 2, P], F32R), sb("qsl", [P, 2, P], F32R)
        prob, pT = sb("prob", [P, S]), sb("pT", [P, NC, 512])
        cmax, nmax, nbias = sb("chunk_max", [P, NC]), sb("neg_max", [P, 1]), sb("neg_bias", [P, 2])
        stats = sb("stats_out", [P, TILES, 6])
        rsum, rtot, rinv = sb("row_sums", [P, 2, NC]), sb("row_total", [P, 1]), sb("row_inverse", [P, 1])
        dve_chain, stats_ready = sem("dve_chain"), sem("stats_ready")
        xT_ready, high_ready, low_ready = sem("xT_ready"), sem("high_ready"), sem("low_ready")
        k_ready, q_ready, v_ready = sem("k_ready"), sem("q_ready"), sem("v_ready")
        kh_ready, qh_ready, kl_ready, ql_ready, v_done = (
            sem("kh_ready"), sem("qh_ready"), sem("kl_ready"), sem("ql_ready"), sem("v_done"))
        staged, scores_ready, nbias_ready, exp_ready = (
            sem("staged"), sem("scores_ready"), sem("nbias_ready"), sem("exp_ready"))
        pt_ready, pT_even, pT_odd, out_ready, x_done = (
            sem("pt_ready"), sem("pT_even"), sem("pT_odd"), sem("out_ready"), sem("x_done"))

        with nc.Block() as block:
            @block.vector
            def _(dve):
                chain = Chain(dve, dve_chain, W.passed)

                def low(g, par):
                    dve.wait_ge(high_ready, g + 1)
                    nc.vector.tensor_tensor(xl[:, par, :], psum[:, XB[par], :], xh[:, par, :].bitcast(F32),
                                            ALU.subtract).then_inc(low_ready, 1)

                def project(g, par):
                    dve.wait_ge(v_ready, g + 1)
                    nc.vector.tensor_tensor(v[:, bass.ts(g, GT), :],
                                            psum[:, VB[par], :].rearrange("p (t d) -> p t d", d=D),
                                            W.bvb[:].unsqueeze(1).to_broadcast([P, GT, D]), ALU.add)\
                        .then_inc(v_done, 1)
                    cols = bass.ts(g, GW)
                    for ready, high, rest, bank, bias, done in ((kh_ready, kh, kl, KB, W.bk, kl_ready),
                                                                (qh_ready, qh, ql, QB, W.bq, ql_ready)):
                        dve.wait_ge(ready, g + 1)
                        nc.vector.scalar_tensor_tensor(rest[:, cols], psum[:, bank[par], :], bias[:],
                                                       high[:, cols].bitcast(F32), ALU.add, ALU.subtract)\
                            .then_inc(done, 1)

                def vector_max(i, par):
                    for c in range(NC):
                        dve.wait_ge(scores_ready, i * NC + c + 1)
                        ins = nc.vector.tensor_reduce(cmax[:, c:c + 1], psum[:, c, :], AX.X, ALU.max)
                    chain.link(ins)
                    chain.link(nc.vector.tensor_reduce(nmax[:], cmax[:], AX.X, ALU.max))
                    nc.vector.tensor_scalar(nbias[:, par:par + 1], nmax[:], -SCALE, None, ALU.mult)\
                        .then_inc(nbias_ready, 1)

                def vector_odd(i, c):
                    dve.wait_ge(pt_ready, i * NC + c + 1)
                    nc.vector.tensor_copy(pT[:, c, :], psum[:, TB[c % 2], :]).then_inc(pT_odd, 1)

                def vector_outputs(i, par):
                    chain.link(nc.vector.tensor_reduce(rtot[:], rsum[:, par, :], AX.X, ALU.add))
                    chain.link(nc.vector.reciprocal(rinv[:], rtot[:]))
                    dve.wait_ge(out_ready, i + 1)
                    x = X[:, bass.ds(i, 1), :].rearrange("p o d -> p (o d)")
                    nc.vector.scalar_tensor_tensor(x, psum[:, OB[par], 0:D], rinv[:], x, ALU.mult, ALU.add)\
                        .then_inc(x_done, 1)

                def vector_row_stats(i):
                    wait_alone(dve, W.passed, x_done, i + 1)
                    row = lambda t: t[:, bass.ds(i, 1), :].rearrange("p o d -> p (o d)")
                    nc.vector.bn_stats(row(stats), row(X)).then_inc(stats_ready, 1)

                fr.vector_stats(dve, chain)
                fr.vector_normalize(dve, 0, 0, first=True)
                fr.vector_normalize(dve, 1, 1, first=True)
                low(0, 0)
                with dve.Fori(0, GROUPS // 2 - 1) as j:
                    for par in range(2):
                        fr.vector_normalize(dve, j * 2 + par + 2, par)
                        low(j * 2 + par + 1, 1 - par)
                        project(j * 2 + par, par)
                low(GROUPS - 1, 1)
                project(GROUPS - 2, 0)
                project(GROUPS - 1, 1)

                vector_max(0, 0)
                vector_odd(0, 1)
                def vector_step(i, par, first=False):
                    vector_max(i + 1, 1 - par)
                    vector_odd(i, 3)
                    if not first:
                        vector_row_stats(i - 1)
                    vector_outputs(i, par)
                    vector_odd(i + 1, 1)

                vector_step(0, 0, first=True)
                vector_step(1, 1)
                with dve.Fori(1, TILES // 2 - 1) as j:
                    chain.turn(j - 1, 8)
                    vector_step(j * 2, 0)
                    vector_step(j * 2 + 1, 1)
                chain.leave(TILES // 2 - 2)
                vector_step(TILES - 2, 0)
                vector_row_stats(TILES - 2)
                vector_odd(TILES - 1, 3)
                vector_outputs(TILES - 1, 1)
                vector_row_stats(TILES - 1)
                dve.wait_ge(stats_ready, TILES)
                for t in range(TILES):
                    nc.vector.bn_aggr(W.mv[:, t, :], stats[:, t, :])

            @block.gpsimd
            def _(pool):
                def stage(i, par):
                    cols = bass.ts(i, P)
                    nc.gpsimd.tensor_copy(qsh[:, par, :], qh[:, cols])
                    nc.gpsimd.tensor_copy(qsl[:, par, :], ql[:, cols]).then_inc(staged, 1)

                fr.gpsimd_rstd(pool)
                pool.wait_ge(qh_ready, 1)
                pool.wait_ge(ql_ready, 1)
                stage(0, 0)
                stage(1, 1)
                pool.wait_ge(ql_ready, GROUPS)
                with pool.Fori(1, TILES // 2) as j:
                    for par in range(2):
                        wait_alone(pool, W.passed, scores_ready, (j * 2 + par - 1) * NC)
                        stage(j * 2 + par, par)

            @block.scalar
            def _(act):
                def parts(g, par):
                    act.wait_ge(fr.xt_ready, g + 1)
                    nc.scalar.activation(xT[:, par, :], psum[:, XB[par], :], ACT.Copy).then_inc(xT_ready, 1)
                    nc.scalar.activation(xh[:, par, :], psum[:, XB[par], :], ACT.Copy).then_inc(high_ready, 1)

                def project(g, par):
                    cols = bass.ts(g, GW)
                    for ready, high, bank, bias, done in ((k_ready, kh, KB, W.bk, kh_ready),
                                                          (q_ready, qh, QB, W.bq, qh_ready)):
                        act.wait_ge(ready, g + 1)
                        nc.scalar.activation(high[:, cols], psum[:, bank[par], :], ACT.Identity, bias=bias[:])\
                            .then_inc(done, 1)

                def exps(i, par, c, first=False):
                    act.wait_ge(nbias_ready, i + 1)
                    if not first:
                        act.wait_ge(pt_ready, (i - 1) * NC + c + 1)
                    nc.scalar.activation(prob[:, c * 512:(c + 1) * 512], psum[:, c, :], ACT.Exp,
                                         bias=nbias[:, par:par + 1], scale=SCALE,
                                         accum_out=rsum[:, par, c:c + 1]).then_inc(exp_ready, 1)

                def even(i, c):
                    act.wait_ge(pt_ready, i * NC + c + 1)
                    nc.scalar.activation(pT[:, c, :], psum[:, TB[c % 2], :], ACT.Copy).then_inc(pT_even, 1)

                def step(i, par):
                    even(i, 2)
                    for c in range(NC):
                        exps(i + 1, 1 - par, c)
                    even(i + 1, 0)

                parts(0, 0)
                with act.Fori(0, GROUPS // 2 - 1) as j:
                    for par in range(2):
                        parts(j * 2 + par + 1, 1 - par)
                        project(j * 2 + par, par)
                parts(GROUPS - 1, 1)
                project(GROUPS - 2, 0)
                project(GROUPS - 1, 1)
                for c in range(NC):
                    exps(0, 0, c, first=True)
                even(0, 0)
                with act.Fori(0, TILES // 2 - 1) as j:
                    step(j * 2, 0)
                    step(j * 2 + 1, 1)
                step(TILES - 2, 0)
                even(TILES - 1, 2)

            @block.tensor
            def _(pe):
                def project(g, par, first=False):
                    pe.wait_ge(xT_ready, g + 1)
                    if not first:
                        pe.wait_ge(v_done, g - 1)
                        pe.wait_ge(kl_ready, g - 1)
                        pe.wait_ge(ql_ready, g - 1)
                    for t in range(GT):
                        tok = slice(t * P, (t + 1) * P)
                        ins = nc.tensor.matmul(psum[:, VB[par], tok], xT[:, par, tok], W.wv[:], start=True, stop=True)
                    ins.then_inc(v_ready, 1)
                    pe.wait_ge(low_ready, g + 1)
                    x = (xh[:, par, :], xl[:, par, :])
                    three_products(nc, psum[:, KB[par], :], (W.wkh[:], W.wkl[:]), x).then_inc(k_ready, 1)
                    three_products(nc, psum[:, QB[par], :], (W.wqh[:], W.wql[:]), x).then_inc(q_ready, 1)

                def scores(i, par, b, c, first=False):
                    if c == 0:
                        pe.wait_ge(staged, i + 1)
                    if not first:
                        pe.wait_ge(exp_ready, (i - 1) * NC + c + 1)
                    cols = slice(b * S + c * 512, b * S + (c + 1) * 512)
                    three_products(nc, psum[:, c, :], (qsh[:, par, :], qsl[:, par, :]),
                                   (kh[:, cols], kl[:, cols])).then_inc(scores_ready, 1)

                def turn(i, c):
                    pe.wait_ge(exp_ready, i * NC + c + 1)
                    if c >= 2:
                        pe.wait_ge(pT_odd if c % 2 else pT_even, i * 2 + 1)
                    for k in range(4):
                        cols = slice((c * 4 + k) * P, (c * 4 + k + 1) * P)
                        ins = nc.tensor.transpose(psum[:, TB[c % 2], k * P:(k + 1) * P], prob[:, cols], ident[:])
                    ins.then_inc(pt_ready, 1)

                def weigh(i, par, b, c):
                    pe.wait_ge(pT_odd if c % 2 else pT_even, i * 2 + c // 2 + 1)
                    for k in range(4):
                        ins = nc.tensor.matmul(psum[:, OB[par], 0:D], pT[:, c, k * P:(k + 1) * P],
                                               v[:, b * QT + c * 4 + k, :],
                                               start=(c == 0 and k == 0), stop=(c == NC - 1 and k == 3))
                    if c == NC - 1:
                        ins.then_inc(out_ready, 1)

                def step(i, par, b, ahead):
                    more = (lambda c: scores(i + 1, 1 - par, ahead, c)) if ahead is not None else (lambda c: None)
                    more(0)
                    turn(i, 0)
                    more(1)
                    turn(i, 1)
                    more(2)
                    weigh(i, par, b, 0)
                    more(3)
                    weigh(i, par, b, 1)
                    turn(i, 2)
                    turn(i, 3)
                    weigh(i, par, b, 2)
                    weigh(i, par, b, 3)

                fr.tensor_transpose(pe, 0, 0)
                fr.tensor_transpose(pe, 1, 1)
                project(0, 0, first=True)
                fr.tensor_transpose(pe, 2, 0)
                project(1, 1, first=True)
                fr.tensor_transpose(pe, 3, 1)
                with pe.Fori(1, GROUPS // 2 - 1) as j:
                    for par in range(2):
                        project(j * 2 + par, par)
                        fr.tensor_transpose(pe, j * 2 + par + 2, par)
                project(GROUPS - 2, 0)
                project(GROUPS - 1, 1)
                for done in (kl_ready, ql_ready, v_done):
                    pe.wait_ge(done, GROUPS)
                for c in range(NC):
                    scores(0, 0, 0, c, first=True)
                for b in range(B):
                    with pe.Fori(b * QT // 2, (b + 1) * QT // 2 - 1) as j:
                        step(j * 2, 0, b, b)
                        step(j * 2 + 1, 1, b, b)
                    step((b + 1) * QT - 2, 0, b, b)
                    step((b + 1) * QT - 1, 1, b, b + 1 if b + 1 < B else None)


def second_mixture(nc, name, X, ident, psum, W, A, out=None):
    with ExitStack() as ctx:
        sb = lambda n, s, dt=F32: ctx.enter_context(nc.sbuf_tensor(f"{name}_{n}", s, dt))
        sem = Semaphores(ctx, nc, name)
        HB, YB = (0, 1, 2, 3), (4, 5)
        ro = Router(ctx, sem, nc, name, X, ident, psum, W, W.gw[:], W.gb[:])
        flat = ro.flat
        HALF = GROUPS // 2
        w1, w2 = sb("w1", [P, E, F]), sb("w2", [P, E, FC * D])
        w1h, w1l = sb("w1h", [P, 2, F], F32R), sb("w1l", [P, 2, F], F32R)
        w2h, w2l = sb("w2h", [P, 2, FC * D], F32R), sb("w2l", [P, 2, FC * D], F32R)
        hf = sb("hf", [P, FC, GW])
        hh, hl = sb("hh", [P, 2, FC, GW], F32R), sb("hl", [P, 2, FC, GW], F32R)
        cb = sb("coef_rows", [P, 2, HALF * GW])
        weighted, total = sb("weighted", [P, GW]), sb("totals", [P, GROUPS, GW])
        last = sb("stats_out", [P, GT, 6])
        stored = sem("stored")
        total_zero = sem("total_zero")
        w1_loaded, w2_loaded, coef_stored = sem("w1_loaded"), sem("w2_loaded"), sem("coef_stored")
        cb_loaded = [sem("cb_loaded0"), sem("cb_loaded1")]
        w_high, w_low = sem("w_high"), sem("w_low")
        up_ready, hf_ready, hh_ready, hl_ready = sem("up_ready"), sem("hf_ready"), sem("hh_ready"), sem("hl_ready")
        y_ready, y_used, total_ready = sem("y_ready"), sem("y_used"), sem("total_ready")
        back_ready, x_done = sem("back_ready"), sem("x_done")
        coef_dram = A["coef_scratch"]

        with nc.Block() as block:
            @block.vector
            def _(dve):
                dve_chain = sem("dve_chain")
                chain = Chain(dve, dve_chain, W.passed)

                def low(n, par, c):
                    dve.wait_ge(hh_ready, n * FC + c + 1)
                    nc.vector.tensor_tensor(hl[:, par, c, :], hf[:, c, :], hh[:, par, c, :].bitcast(F32), ALU.subtract)\
                        .then_inc(hl_ready, 1)

                def combine(e, g, par, half, q):
                    n = e * GROUPS + g
                    dve.wait_ge(y_ready, n + 1)
                    dve.wait_ge(cb_loaded[half], (e + 1) * 16)
                    nc.vector.scalar_tensor_tensor(weighted[:], psum[:, YB[par], :], W.b2T[:, bass.ds(e, 1)],
                                                   cb[:, half, bass.ts(q, GW)], ALU.add, ALU.mult).then_inc(y_used, 1)
                    dve.wait_ge(y_used, n + 3)
                    nc.vector.tensor_tensor(flat(total, g), flat(total, g), weighted[:], ALU.add).then_inc(total_ready, 1)

                def group(e, g, par, half, q, last=False):
                    if not last:
                        for c in range(FC):
                            low(e * GROUPS + g + 1, 1 - par, c)
                    dve.wait_ge(total_ready, e * GROUPS + g + 1)
                    combine(e, g, par, half, q)

                ro.vector_front(dve, chain)
                ro.vector_top2(dve, chain)
                dve.wait_ge(total_zero, 1)
                dve.sem_inc(y_used, 2)
                dve.sem_inc(total_ready, 1)
                for c in range(FC):
                    low(0, 0, c)
                with dve.Fori(0, E - 1) as e:
                    for half in range(2):
                        with dve.Fori(0, HALF // 2) as i:
                            for par in range(2):
                                group(e, half * HALF + i * 2 + par, par, half, i * 2 + par)
                for g in range(GROUPS):
                    group(E - 1, g, g % 2, g // HALF, g % HALF, last=(g == GROUPS - 1))
                for g in range(GROUPS):
                    dve.wait_ge(back_ready, g + 1)
                    x = ro.rows(g)
                    nc.vector.tensor_tensor(x, psum[:, HB[g % 4], :].rearrange("p (t d) -> p t d", d=D), x, ALU.add)\
                        .then_inc(x_done, 1)
                    if out is None:
                        dve.wait_ge(x_done, g + 1)
                        chain.link(row_stats(nc, chain, last, W.mv[:, g * GT:(g + 1) * GT], x))

            @block.gpsimd
            def _(pool):
                def low(e, par):
                    wait_alone(pool, W.passed, w_high, e * 2 + 2)
                    nc.gpsimd.tensor_tensor(w1l[:, par, :], flat(w1, e), w1h[:, par, :].bitcast(F32), ALU.subtract)
                    nc.gpsimd.tensor_tensor(w2l[:, par, :], flat(w2, e), w2h[:, par, :].bitcast(F32), ALU.subtract)\
                        .then_inc(w_low, 1)

                ro.gpsimd_rstd(pool)
                nc.gpsimd.memset(total[:], 0.0).then_inc(total_zero, 1)
                with pool.Fori(0, E // 2) as j:
                    low(j * 2, 0)
                    low(j * 2 + 1, 1)

            @block.sync
            def _(sp):
                for half in range(2):
                    es = slice(half * E // 2, (half + 1) * E // 2)
                    sp.dma_start(w1[:, es, :], A["L1_ffn_w1"][es].rearrange("e p f -> p e f")).then_inc(w1_loaded, 16)
                for e in range(E):
                    sp.dma_start(w2[:, e, :].rearrange("p (c d) -> p c d", d=D),
                                 A["L1_ffn_w2"][e].rearrange("(c p) d -> p c d", p=P)).then_inc(w2_loaded, 16)
                sp.wait_ge(ro.coefT_ready, 1)
                sp.dma_start(coef_dram.rearrange("n te p -> te n p"), ro.coefT[:]).then_inc(coef_stored, 16)
                sp.wait_ge(coef_stored, 16)

                def rows(e, half):
                    src = coef_dram[half].rearrange("(t e) p -> e t p", e=E)[bass.ds(e, 1)]
                    sp.dma_start(cb[:, half, :].rearrange("p (o t q) -> p o t q", o=1, q=P),
                                 src.partition_broadcast(P)).then_inc(cb_loaded[half], 16)

                rows(0, 0)
                rows(0, 1)
                with sp.Fori(1, E) as e:
                    for half in range(2):
                        sp.wait_ge(y_used, (e - 1) * GROUPS + (half + 1) * HALF + 2)
                        rows(e, half)
                if out is not None:
                    rows_out = out.rearrange("b (t p) d -> p (b t) d", p=P)
                    for g in range(1, GROUPS, 2):
                        tiles = slice((g - 1) * GT, (g + 1) * GT)
                        sp.wait_ge(x_done, g + 1)
                        sp.dma_start(rows_out[:, tiles, :], X[:, tiles, :]).then_inc(stored, 16)
                    sp.wait_ge(stored, GROUPS // 2 * 16)

            @block.scalar
            def _(act):
                def high(e, par):
                    nc.scalar.activation(w1h[:, par, :], flat(w1, e), ACT.Copy).then_inc(w_high, 1)
                    nc.scalar.activation(w2h[:, par, :], flat(w2, e), ACT.Copy).then_inc(w_high, 1)

                def hidden(e, g, par):
                    n = e * GROUPS + g

                    def relu(c):
                        wait_alone(act, W.passed, up_ready, n * FC + c + 1)
                        nc.scalar.activation(hf[:, c, :], psum[:, HB[c], :], ACT.Relu,
                                             bias=W.b1T[:, bass.ds(e * FC + c, 1)]).then_inc(hf_ready, 1)

                    def part(c):
                        act.wait_ge(hf_ready, n * FC + c + 1)
                        nc.scalar.activation(hh[:, par, c, :], hf[:, c, :], ACT.Copy).then_inc(hh_ready, 1)

                    relu(0)
                    for c in range(1, FC):
                        relu(c)
                        part(c - 1)
                    part(FC - 1)

                ro.scalar_front(act)
                act.wait_ge(w1_loaded, 32)
                act.wait_ge(w2_loaded, E * 16)
                high(0, 0)
                ro.scalar_exp(act)
                high(1, 1)
                ro.scalar_coef_rows(act)
                hidden(0, 0, 0)

                def expert(e, par_e, last=False):
                    with act.Fori(0, HALF - 1) as i:
                        hidden(e, i * 2 + 1, 1)
                        hidden(e, i * 2 + 2, 0)
                    hidden(e, GROUPS - 1, 1)
                    if not last:
                        hidden(e + 1, 0, 0)

                def replace(e, par):
                    wait_alone(act, W.passed, y_ready, (e - 1) * GROUPS)
                    high(e, par)

                expert(0, 0)
                with act.Fori(1, E // 2) as j:
                    replace(j * 2, 0)
                    expert(j * 2 - 1, 1)
                    replace(j * 2 + 1, 1)
                    expert(j * 2, 0)
                expert(E - 1, 1, last=True)

            @block.tensor
            def _(pe):
                def up(e, g, c, par_e):
                    x = [flat(a, g) for a in (ro.xh, ro.xl)]
                    cols = slice(c * P, (c + 1) * P)
                    three_products(nc, psum[:, HB[c], :], (w1h[:, par_e, cols], w1l[:, par_e, cols]), x)\
                        .then_inc(up_ready, 1)

                def down(e, g, c, par_e, par):
                    if c == 0:
                        pe.wait_ge(y_used, e * GROUPS + g + 1)
                    cols = slice(c * D, (c + 1) * D)
                    ins = three_products(nc, psum[:, YB[par], :], (w2h[:, par_e, cols], w2l[:, par_e, cols]),
                                         (hh[:, par, c, :], hl[:, par, c, :]), start=(c == 0), stop=(c == FC - 1))
                    if c == FC - 1:
                        ins.then_inc(y_ready, 1)

                def group(e, g, par_e, par, ahead):
                    for c in range(FC):
                        pe.wait_ge(hl_ready, (e * GROUPS + g) * FC + c + 1)
                        if ahead:
                            up(*ahead[0:2], c, ahead[2])
                        down(e, g, c, par_e, par)

                ro.tensor_front(pe)
                pe.wait_ge(w_low, 1)
                for c in range(FC):
                    up(0, 0, c, 0)
                ro.tensor_coef(pe)

                def expert(e, par_e, last=False):
                    with pe.Fori(0, GROUPS // 2 - 1) as i:
                        group(e, i * 2, par_e, 0, (e, i * 2 + 1, par_e))
                        group(e, i * 2 + 1, par_e, 1, (e, i * 2 + 2, par_e))
                    group(e, GROUPS - 2, par_e, 0, (e, GROUPS - 1, par_e))
                    if not last:
                        pe.wait_ge(w_low, e + 2)
                    group(e, GROUPS - 1, par_e, 1, None if last else (e + 1, 0, 1 - par_e))

                with pe.Fori(0, E // 2 - 1) as j:
                    expert(j * 2, 0)
                    expert(j * 2 + 1, 1)
                expert(E - 2, 0)
                expert(E - 1, 1, last=True)
                for g in range(GROUPS):
                    pe.wait_ge(total_ready, (E - 1) * GROUPS + g + 2)
                    if g >= 4:
                        pe.wait_ge(x_done, g - 3)
                    for t in range(GT):
                        tok = slice(t * P, (t + 1) * P)
                        ins = nc.tensor.transpose(psum[:, HB[g % 4], tok], total[:, g, tok], ident[:])
                    ins.then_inc(back_ready, 1)


class Holder:
    pass


H, KD, VD = 4, 32, 64
KEY, VAL = H * KD, H * VD
CONV = 4
RMS_EPS = 1e-6
NQ = TILES * H


def row_stats(nc, chain, stats, mv, src):
    for t in range(GT):
        ins = nc.vector.bn_stats(stats[:, t, :], src[:, t, :])
    chain.link_alone(ins)
    for t in range(GT):
        ins = nc.vector.bn_aggr(mv[:, t, :], stats[:, t, :])
    return ins


def inverse_root(nc, pool, passed, sem, count, out, src, tmp, scale, eps, power):
    nc.gpsimd.tensor_scalar(tmp, src, scale, eps, ALU.mult, ALU.add).then_inc(sem, 1)
    wait_alone(pool, passed, sem, count + 1)
    nc.gpsimd.tensor_tensor(out, tmp, power, ALU.pow).then_inc(sem, 1)


def delta_inputs(nc, X, ident, psum, W, M):
    with ExitStack() as ctx:
        sb = lambda n, s, dt=F32: ctx.enter_context(nc.sbuf_tensor(f"in_{n}", s, dt))
        sem = Semaphores(ctx, nc, "in")
        ve, r2, r12, r3, power = (sb(n, [P, TILES]) for n in ("ve", "r2", "r12", "r3", "power"))
        ss, ms = sb("ss", [P, TILES]), sb("ms", [P, TILES])
        y, h = sb("y", [P, TILES, D]), sb("h", [P, GT, D])
        hT, keep = sb("hT", [P, GW]), sb("keep", [P, GROUPS])
        cv = sb("cv", [P, 2, 4, GW + CONV - 1])
        acc, th = sb("acc", [P, 2, 4, GW]), sb("th", [P, 4, GW])
        sg = sb("sg", [P, GT, VAL])
        sq = sg[:, :, 0:D]
        sq2, ss2, rq, rqt = sb("sq2", [P, 2, GW]), sb("ss2", [P, 32]), sb("rq", [P, 32]), sb("rqt", [P, 32])
        fac, nh32 = sb("fac", [P, 32]), sb("nh32", [P, 32])
        (dve_chain, consts, wloaded, pool_steps, r12_ready, y_ready, ss_ready, r3_ready,
         h_ready, ht_ready, hT_ready, proj_ready, cv_ready, halo_ready, acc0_ready, acc_ready, th_ready, s2_ready,
         gate_ready, sg_ready, gate_done, ab_ready, ab_done, nat_ready, sq2_ready, v_used, ss2_ready, rq_ready,
         nat_used) = (sem(n) for n in (
            "dve_chain consts wloaded pool_steps r12_ready y_ready ss_ready r3_ready "
            "h_ready ht_ready hT_ready proj_ready cv_ready halo_ready acc0_ready acc_ready th_ready s2_ready "
            "gate_ready sg_ready gate_done ab_ready ab_done nat_ready sq2_ready v_used ss2_ready rq_ready "
            "nat_used").split())
        PROJ, AB, TB, GATE, NAT = (0, 1), 0, 1, (2, 3), 4
        PARTS = slice(0, 2 * GT), slice(2 * GT, TILES)

        def tiles4(ap):
            return ap.unsqueeze(1).to_broadcast([P, GT, D])

        def row(ap):
            return ap.rearrange("p o d -> p (o d)")

        with nc.Block() as block:
            @block.vector
            def _(dve):
                v = nc.vector
                chain = Chain(dve, dve_chain, W.passed)

                def halo(g, par):
                    dve.wait_ge(cv_ready, g * 4)
                    v.tensor_scalar(cv[:, par, :, 0:CONV - 1], cv[:, 1 - par, :, GW:GW + CONV - 1],
                                    keep[:, bass.ds(g, 1)], None, ALU.mult).then_inc(halo_ready, 1)

                def convolve(g, par, pair):
                    last = {}
                    for i in range(1, CONV):
                        for c in pair:
                            if i == 1:
                                dve.wait_ge(acc0_ready, g * 4 + c + 1)
                            else:
                                dve.wait_ge(dve_chain, last[c])
                            ins = v.scalar_tensor_tensor(acc[:, par, c, :], cv[:, par, c, i:i + GW],
                                                         M.convw[:, c, i:i + 1], acc[:, par, c, :], ALU.mult, ALU.add)
                            if i < CONV - 1:
                                last[c] = chain.mark(ins)
                            else:
                                ins.then_inc(acc_ready, 1)

                def silu(g, par, c):
                    dve.wait_ge(th_ready, g * 4 + c + 1)
                    v.scalar_tensor_tensor(th[:, c, :], th[:, c, :], 1.0, acc[:, par, c, :], ALU.add, ALU.mult)\
                        .then_inc(s2_ready, 1)

                def gates(g):
                    for n in range(2):
                        dve.wait_ge(sg_ready, g * 2 + n + 1)
                        v.scalar_tensor_tensor(
                            M.gate[:, bass.ds(g * GT + n * 2, 2), :], sg[:, 2 * n:2 * n + 2, :], 1.0,
                            psum[:, GATE[n], :].rearrange("p (t v) -> p t v", v=VAL), ALU.add, ALU.mult)\
                            .then_inc(gate_done, 1)

                def sums(g):
                    dve.wait_ge(sq2_ready, g + 1)
                    v.tensor_reduce(ss2[:], sq2[:].rearrange("p a (n k) -> p (a n) k", k=KD), AX.X, ALU.add)\
                        .then_inc(ss2_ready, 1)

                def norm(g):
                    dve.wait_ge(rq_ready, g * 3 + 3)
                    for n, dst in enumerate((M.q, M.k)):
                        ins = v.tensor_tensor(
                            dst[:, bass.ts(g, GT), :].rearrange("p t (h k) -> p (t h) k", k=KD),
                            psum[:, NAT + n, :].rearrange("p (n k) -> p n k", k=KD),
                            rq[:, n * 16:(n + 1) * 16].unsqueeze(2).to_broadcast([P, 16, KD]), ALU.mult)
                    ins.then_inc(nat_used, 1)

                def step(g, par, prev=True, ahead=2):
                    dve.wait_ge(ab_ready, g + 1)
                    v.tensor_copy(M.ab[:, bass.ts(g, GT), :],
                                  psum[:, AB, 0:GT * 2 * H].rearrange("p (t e) -> p t e", e=2 * H)).then_inc(ab_done, 1)
                    if ahead:
                        halo(g + 1, 1 - par)
                    convolve(g, par, (0, 1))
                    if prev:
                        sums(g - 1)
                    convolve(g, par, (2, 3))
                    silu(g, par, 0)
                    silu(g, par, 1)
                    gates(g)
                    silu(g, par, 2)
                    silu(g, par, 3)
                    if prev:
                        norm(g - 1)

                chain.link(v.memset(cv[:, 0, :, 0:CONV - 1], 0.0))
                dve.sem_inc(halo_ready, 1)
                dve.wait_ge(wloaded, 16 * M.n_loads)

                def rows_of(g):
                    for t in range(GT):
                        tile = bass.ds(g * GT + t, 1)
                        ins = v.tensor_scalar(row(y[:, tile, :]), row(X[:, tile, :]), row(M.mv[:, tile, 0:1]),
                                              r12[:, tile], ALU.subtract, ALU.mult)
                    chain.link(ins)
                    rows = y[:, bass.ts(g, GT), :]
                    chain.link(v.tensor_tensor(rows, rows, tiles4(M.ln1g[:]), ALU.mult))
                    v.tensor_tensor(rows, rows, tiles4(M.ln1b[:]), ALU.add).then_inc(y_ready, 1)

                dve.wait_ge(r12_ready, 1)
                rows_of(0)
                rows_of(1)
                dve.wait_ge(r12_ready, 2)
                with dve.Fori(2, GROUPS) as g:
                    chain.turn(g - 2, 2)
                    rows_of(g)
                chain.leave(GROUPS - 2)

                PER = 8
                step(0, 0, prev=False)
                step(1, 1)
                with dve.Fori(1, GROUPS // 2 - 1) as j:
                    chain.turn(j - 1, 2 * PER)
                    step(j * 2, 0)
                    step(j * 2 + 1, 1)
                chain.leave(GROUPS // 2 - 2)
                step(GROUPS - 2, 0, ahead=1)
                step(GROUPS - 1, 1, ahead=0)
                sums(GROUPS - 1)
                norm(GROUPS - 1)

            @block.gpsimd
            def _(pool):
                g_ = nc.gpsimd
                count = [0]

                def link(ins):
                    count[0] += 1
                    ins.then_inc(pool_steps, 1)
                    pool.wait_ge(pool_steps, count[0])

                def tap0(g, par, prev=True):
                    wait_alone(pool, W.passed, halo_ready, g + 1)
                    if prev:
                        wait_alone(pool, W.passed, s2_ready, (g - 1) * 4)
                    for c in range(4):
                        wait_alone(pool, W.passed, cv_ready, g * 4 + c + 1)
                        g_.tensor_scalar(acc[:, par, c, :], cv[:, par, c, 0:GW], M.convw[:, c, 0:1], None, ALU.mult)\
                            .then_inc(acc0_ready, 1)

                def deviations(g, first=False):
                    wait_alone(pool, W.passed, ss2_ready, g + 1)
                    if not first:
                        wait_alone(pool, W.passed, nat_used, g)
                    inverse_root(nc, pool, W.passed, rq_ready, g * 3, rqt[:], ss2[:], rq[:], 0.25, RMS_EPS, nh32[:])
                    wait_alone(pool, W.passed, rq_ready, g * 3 + 2)
                    g_.tensor_tensor(rq[:], rqt[:], fac[:], ALU.mult).then_inc(rq_ready, 1)

                link(g_.memset(power[:], -0.5))
                link(g_.memset(nh32[:], -0.5))
                link(g_.memset(keep[:], 1.0))
                for b in range(B):
                    link(g_.memset(keep[:, b * GROUPS // B:b * GROUPS // B + 1], 0.0))
                g_.memset(fac[:, 0:16], 0.5 * float(KD) ** -0.5).then_inc(consts, 1)
                g_.memset(fac[:, 16:32], 0.5).then_inc(consts, 1)
                pool.wait_ge(consts, 2)
                for n, part in enumerate(PARTS):
                    link(g_.tensor_scalar(ve[:, part], M.mv[:, part, 1], LN_EPS, None, ALU.add))
                    link(g_.tensor_tensor(M.rstd[:, part], ve[:, part], power[:, part], ALU.pow))
                    link(g_.tensor_tensor(ve[:, part], M.mv[:, part, 1], M.rstd[:, part], ALU.mult))
                    link(g_.tensor_tensor(ve[:, part], ve[:, part], M.rstd[:, part], ALU.mult))
                    link(g_.tensor_scalar(ve[:, part], ve[:, part], LN_EPS, None, ALU.add))
                    link(g_.tensor_tensor(r2[:, part], ve[:, part], power[:, part], ALU.pow))
                    g_.tensor_tensor(r12[:, part], r2[:, part], M.rstd[:, part], ALU.mult).then_inc(r12_ready, 1)
                pool.wait_ge(wloaded, 16 * M.n_loads)
                for n, part in enumerate(PARTS):
                    pool.wait_ge(ss_ready, part.stop // GT)
                    link(g_.tensor_scalar(ms[:, part], ss[:, part], 1.0 / D, RMS_EPS, ALU.mult, ALU.add))
                    g_.tensor_tensor(r3[:, part], ms[:, part], power[:, part], ALU.pow).then_inc(r3_ready, 1)
                    if n == 0:
                        tap0(0, 0, prev=False)
                tap0(1, 1, prev=False)
                deviations(0, first=True)
                tap0(2, 0)
                with pool.Fori(1, GROUPS // 2 - 1) as j:
                    for par in range(2):
                        g = j * 2 + par
                        deviations(g - 1)
                        tap0(g + 1, 1 - par)
                deviations(GROUPS - 3)
                tap0(GROUPS - 1, 1)
                deviations(GROUPS - 2)
                deviations(GROUPS - 1)

            @block.sync
            def _(sp):
                for dst, src in M.loads:
                    sp.dma_start(dst, src).then_inc(wloaded, 16)

            @block.scalar
            def _(act):
                a_ = nc.scalar

                def scale_rows(g, first=False):
                    if not first:
                        act.wait_ge(ht_ready, g)
                    for t in range(GT):
                        tile = bass.ds(g * GT + t, 1)
                        ins = a_.activation(h[:, t, :], row(y[:, tile, :]), ACT.Copy, scale=r3[:, tile])
                    ins.then_inc(h_ready, 1)

                def turned(g):
                    act.wait_ge(ht_ready, g + 1)
                    a_.activation(hT[:], psum[:, TB, :], ACT.Copy, scale=M.rmsw[:]).then_inc(hT_ready, 1)

                def projected(g, par, c):
                    if c == 0:
                        act.wait_ge(halo_ready, g + 1)
                    act.wait_ge(proj_ready, g * 4 + c + 1)
                    a_.activation(cv[:, par, c, CONV - 1:], psum[:, PROJ[c % 2], :], ACT.Copy).then_inc(cv_ready, 1)

                def tanh(g, par, c, prev=True):
                    act.wait_ge(acc_ready, g * 4 + c + 1)
                    if prev:
                        act.wait_ge(nat_ready, g)
                    a_.activation(th[:, c, :], acc[:, par, c, :], ACT.Tanh, scale=0.5).then_inc(th_ready, 1)

                def gate_tanh(g, prev=True):
                    for n in range(2):
                        act.wait_ge(gate_ready, g * 2 + n + 1)
                        if prev:
                            act.wait_ge(gate_done, g * 2)
                        a_.activation(sg[:, 2 * n:2 * n + 2, :], psum[:, GATE[n], :].rearrange("p (t v) -> p t v", v=VAL),
                                      ACT.Tanh, scale=0.5).then_inc(sg_ready, 1)

                def squares(g, prev=True):
                    act.wait_ge(nat_ready, g + 1)
                    if prev:
                        act.wait_ge(ss2_ready, g)
                    a_.activation(sq2[:, 0, :], psum[:, NAT, :], ACT.Square)
                    a_.activation(sq2[:, 1, :], psum[:, NAT + 1, :], ACT.Square).then_inc(sq2_ready, 1)

                def values(g):
                    for n in range(2):
                        ins = a_.activation(M.v[:, bass.ds(g * GT + n * 2, 2), :],
                                            psum[:, NAT + 2 + n, :].rearrange("p (t v) -> p t v", v=VAL),
                                            ACT.Copy, scale=0.5)
                    ins.then_inc(v_used, 1)

                def step(g, par, prev=True, ahead=2, older=True):
                    if prev:
                        squares(g - 1, older)
                    if ahead:
                        turned(g + 1)
                        projected(g + 1, 1 - par, 0)
                        projected(g + 1, 1 - par, 1)
                    tanh(g, par, 0, prev)
                    tanh(g, par, 1, prev)
                    if ahead:
                        projected(g + 1, 1 - par, 2)
                        projected(g + 1, 1 - par, 3)
                    if prev:
                        values(g - 1)
                    tanh(g, par, 2, prev)
                    tanh(g, par, 3, prev)
                    if ahead:
                        gate_tanh(g + 1)
                    if ahead == 2:
                        scale_rows(g + 2)

                def row_squares(g, first=False):
                    wait_alone(act, W.passed, y_ready, g + 1)
                    if not first:
                        wait_alone(act, W.passed, ss_ready, g)
                    for t in range(GT):
                        tile = bass.ds(g * GT + t, 1)
                        ins = a_.activation(sq[:, t, :], row(y[:, tile, :]), ACT.Square, accum_out=ss[:, tile])
                    ins.then_inc(ss_ready, 1)

                row_squares(0, first=True)
                row_squares(1)
                act.wait_ge(r3_ready, 1)
                scale_rows(0, first=True)
                turned(0)
                scale_rows(1)
                for c in range(4):
                    projected(0, 0, c)
                with act.Fori(2, GROUPS) as g:
                    row_squares(g)
                act.wait_ge(ss_ready, GROUPS)
                gate_tanh(0, prev=False)
                act.wait_ge(r3_ready, 2)
                step(0, 0, prev=False)
                step(1, 1, older=False)
                with act.Fori(1, GROUPS // 2 - 1) as j:
                    step(j * 2, 0)
                    step(j * 2 + 1, 1)
                step(GROUPS - 2, 0, ahead=1)
                step(GROUPS - 1, 1, ahead=0)
                squares(GROUPS - 1)
                values(GROUPS - 1)

            @block.tensor
            def _(pe):
                def turn(g):
                    pe.wait_ge(h_ready, g + 1)
                    for t in range(GT):
                        ins = nc.tensor.transpose(psum[:, TB, t * P:(t + 1) * P], h[:, t, :], ident[:])
                    ins.then_inc(ht_ready, 1)

                def project(g, prev=True):
                    if prev:
                        pe.wait_ge(ab_done, g)
                    pe.wait_ge(hT_ready, g + 1)
                    for c, w in enumerate((M.wq[:], M.wk[:], M.wv[:, 0:P], M.wv[:, P:2 * P])):
                        if c >= 2:
                            pe.wait_ge(cv_ready, g * 4 + c - 1)
                        nc.tensor.matmul(psum[:, PROJ[c % 2], :], w, hT[:], start=True, stop=True).then_inc(proj_ready, 1)
                    for n in range(2):
                        if prev:
                            pe.wait_ge(gate_done, (g - 1) * 2 + n + 1)
                        for t in (2 * n, 2 * n + 1):
                            ins = nc.tensor.matmul(psum[:, GATE[n], (t % 2) * VAL:(t % 2 + 1) * VAL],
                                                   hT[:, t * P:(t + 1) * P], M.wg[:], start=True, stop=True)
                        ins.then_inc(gate_ready, 1)
                    pe.wait_ge(cv_ready, g * 4 + 3)
                    for t in range(GT):
                        ins = nc.tensor.matmul(psum[:, AB, t * 2 * H:(t + 1) * 2 * H], hT[:, t * P:(t + 1) * P],
                                               M.wab[:], start=True, stop=True)
                    ins.then_inc(ab_ready, 1)

                def naturals(g, prev=True):
                    pe.wait_ge(s2_ready, g * 4 + 4)
                    if prev:
                        pe.wait_ge(nat_used, g)
                        pe.wait_ge(v_used, g)
                    for t in range(GT):
                        tok = slice(t * P, (t + 1) * P)
                        nc.tensor.transpose(psum[:, NAT, tok], th[:, 0, tok], ident[:])
                        nc.tensor.transpose(psum[:, NAT + 1, tok], th[:, 1, tok], ident[:])
                        for n in range(2):
                            ins = nc.tensor.transpose(
                                psum[:, NAT + 2 + t // 2, (t % 2) * VAL + n * P:(t % 2) * VAL + (n + 1) * P],
                                th[:, 2 + n, tok], ident[:])
                    ins.then_inc(nat_ready, 1)

                def step(g, prev=True, ahead=True):
                    if ahead:
                        pe.wait_ge(cv_ready, g * 4 + 4)
                        turn(g + 1)
                        project(g + 1)
                    naturals(g, prev)

                turn(0)
                project(0, prev=False)
                step(0, prev=False)
                with pe.Fori(1, GROUPS - 1) as g:
                    step(g)
                step(GROUPS - 1, ahead=False)


def delta_decays(nc, psum, M):
    with ExitStack() as ctx:
        sb = lambda n, s, dt=F32: ctx.enter_context(nc.sbuf_tensor(f"dec_{n}", s, dt))
        sem = Semaphores(ctx, nc, "dec")
        z, na, u, s_, s2, po = (sb(n, [P, TILES, H]) for n in ("z", "na", "u", "s", "s2", "po"))
        expA = sb("expA", [P, H])
        tmp = sb("tmp", [P, TILES, H])
        tot = sb("tot", [P, TILES, H])
        dve_chain, act_ready, na_ready, pe_ready, g_ready, tot_ready = (
            sem(n) for n in ("dve_chain", "act_ready", "na_ready", "pe_ready", "g_ready", "tot_ready"))
        flat = lambda t: t[:].rearrange("p t h -> p (t h)")

        def bc(ap):
            return ap.unsqueeze(1).to_broadcast([P, TILES, H])

        with nc.Block() as block:
            @block.vector
            def _(dve):
                ch = Chain(dve, dve_chain, M.passed)
                v = nc.vector
                ch.link(v.tensor_tensor(z[:], M.ab[:, :, 0:H], bc(M.dtb[:]), ALU.add))
                ch.link(v.tensor_scalar(na[:], z[:], -1.0, None, ALU.mult))
                v.tensor_tensor(na[:], na[:], z[:], ALU.min).then_inc(na_ready, 1)
                dve.wait_ge(act_ready, 1)
                ch.link(v.tensor_scalar(s_[:], u[:], 2.0, None, ALU.add))
                ch.link(v.reciprocal(s_[:], s_[:]))
                ch.link(v.tensor_tensor(s_[:], s_[:], u[:], ALU.mult))
                ch.link(v.tensor_tensor(s2[:], s_[:], s_[:], ALU.mult))
                ch.link(v.tensor_scalar(po[:], s2[:], 1.0 / 17, 1.0 / 15, ALU.mult, ALU.add))
                for k in (13, 11, 9, 7, 5, 3, 1):
                    ch.link(v.tensor_tensor(po[:], po[:], s2[:], ALU.mult))
                    ch.link(v.tensor_scalar(po[:], po[:], 1.0 / k, None, ALU.add))
                ch.link(v.scalar_tensor_tensor(po[:], po[:], 2.0, s_[:], ALU.mult, ALU.mult))
                ch.link(v.scalar_tensor_tensor(po[:], z[:], 0.0, po[:], ALU.max, ALU.add))
                dve.wait_ge(act_ready, 3)
                ch.link(v.tensor_tensor(po[:], po[:], bc(expA[:]), ALU.mult))
                v.tensor_scalar(M.g[:], po[:], -1.0, -1000.0, ALU.mult, ALU.max).then_inc(g_ready, 1)
                ch.link(v.tensor_scalar(M.beta[:], tmp[:], 0.5, 0.5, ALU.mult, ALU.add))
                dve.wait_ge(tot_ready, 3)
                ch.link(v.tensor_tensor(tmp[:], tot[:], bc(M.hmask[:]), ALU.mult))
                ch.link(v.tensor_reduce(M.dec[:], tmp[:], AX.X, ALU.add))

            @block.scalar
            def _(act):
                act.wait_ge(na_ready, 1)
                nc.scalar.activation(u[:], na[:], ACT.Exp).then_inc(act_ready, 1)
                nc.scalar.activation(expA[:], M.alog[:], ACT.Exp).then_inc(act_ready, 1)
                nc.scalar.activation(tmp[:], M.ab[:, :, H:2 * H], ACT.Tanh, scale=0.5).then_inc(act_ready, 1)
                for n, dst in enumerate((M.gam, M.kap, tot)):
                    act.wait_ge(pe_ready, n + 1)
                    nc.scalar.activation(flat(dst), psum[:, n, 0:NQ], ACT.Exp).then_inc(tot_ready, 1)

            @block.tensor
            def _(pe):
                pe.wait_ge(g_ready, 1)
                for n, mask in enumerate((M.upto, M.after, M.ones)):
                    nc.tensor.matmul(psum[:, n, 0:NQ], mask[:], flat(M.g), start=True, stop=True)\
                        .then_inc(pe_ready, 1)

STEPS = TILES // B
LEVELS = 5


def delta_scan(nc, ident, psum, M):
    with ExitStack() as ctx:
        sb = lambda n, s, dt=F32: ctx.enter_context(nc.sbuf_tensor(f"sc_{n}", s, dt))
        sem = Semaphores(ctx, nc, "sc")
        ks, qs, kb, qg = (sb(n, [P, B, KEY]) for n in ("ks", "qs", "kb", "qg"))
        kt = sb("kt", [P, 2, B, KEY])
        R = sb("R", [P, B, H, VD + KD])
        gL = sb("gL", [P, B, H, P])
        km = sb("km", [P, B, H, P])
        T3 = sb("T3", [P, 2, B, 3, P])
        dec, caus = sb("decays", [P, B, H, P]), sb("causal", [P, B, H, P])
        Lt, At = sb("Lt", [P, B, H, P]), sb("At", [P, 2, B, H, P])
        T, TT, X = sb("T", [P, B, H, 32]), sb("TT", [P, B, H, 32]), sb("X", [P, B, H, 32])
        T64 = sb("T64", [64, B, H, 64])
        X2, X3 = sb("X2", [P, B, H, 32]), sb("X3", [P, B, H, 64])
        TTf = sb("TTf", [P, B, H, P])
        Us, Wn, WT = sb("Us", [P, 2, B, H, VD]), sb("Wn", [P, B, H, KD]), sb("WT", [P, 2, B, P])
        Dl = sb("delta", [P, B, VAL])
        Sd, St = sb("state", [P, B, VAL]), sb("state_new", [P, B, VAL])
        (dve_chain, staged, scaled, scaled_r, gl_ready, t4_ready, km_ready, T3_ready, seg_ready, dec_ready, caus_ready, kk_ready, qk_ready,
         lt_ready, at_ready, x_ready, X_ready, y_ready, T_ready, x2_ready, X2_ready, X2b_ready, y2_ready, diag_ready,
         T64_ready, TTa_ready, TTd_ready, x3_ready, X3_ready, y3_ready, TTf_ready, uw_ready, Us_ready, Wn_ready,
         wt_ready, WT_ready, ws_ready, delta_ready, o_ready, o_used, s_ready, S_ready, zeroed) = (sem(n) for n in (
            "dve_chain staged scaled scaled_r gl_ready t4_ready km_ready T3_ready seg_ready dec_ready caus_ready kk_ready qk_ready "
            "lt_ready at_ready x_ready X_ready y_ready T_ready x2_ready X2_ready X2b_ready y2_ready diag_ready "
            "T64_ready TTa_ready TTd_ready x3_ready X3_ready y3_ready TTf_ready uw_ready Us_ready Wn_ready "
            "wt_ready WT_ready ws_ready delta_ready o_ready o_used s_ready S_ready zeroed").split())
        BATCHES = range(B)

        def nth(i, bb):
            return i * B + bb + 1

        def tile(t, i, bb):
            return t[:, bass.ds(bb * STEPS + i, 1), :].rearrange("p o d -> p (o d)")

        def heads(ap, k):
            return ap.rearrange("p (h k) -> p h k", k=k)

        def each(t, i, bb, k):
            return tile(t, i, bb).unsqueeze(2).to_broadcast([P, H, k])

        def all_heads(ap):
            return ap.unsqueeze(1).to_broadcast([P, H, 32])

        def bank(bb, n, w, at=0):
            return psum[:, bb * 4 + n, at:at + H * w].rearrange("p (u k) -> p u k", k=w)

        def rows(n, size=32):
            return slice(size * n, size * n + size)

        def flat(ap):
            return ap.rearrange("p a b -> p (a b)")

        with nc.Block() as block:
            @block.gpsimd
            def _(pool):
                g_ = nc.gpsimd

                def prep(i, par, first=False):
                    for bb in BATCHES:
                        g_.tensor_tensor(gL[:, bb], M.upto[:].unsqueeze(1).to_broadcast([P, H, P]),
                                         each(M.g, i, bb, P), ALU.mult).then_inc(gl_ready, 1)
                        if not first:
                            wait_alone(pool, M.passed, scaled_r, nth(i, bb) - B)
                        g_.tensor_tensor(heads(kb[:, bb], KD), heads(tile(M.k, i, bb), KD), each(M.beta, i, bb, KD), ALU.mult)
                        g_.tensor_tensor(heads(qg[:, bb], KD), heads(tile(M.q, i, bb), KD), each(M.gam, i, bb, KD), ALU.mult)\
                            .then_inc(scaled, 1)
                    for bb in BATCHES:
                        if not first:
                            wait_alone(pool, M.passed, at_ready, nth(i, bb) - B)
                        wait_alone(pool, M.passed, dec_ready, nth(i, bb))
                        g_.affine_select(caus[:, bb], dec[:, bb], [[0, H], [1, P]], ALU.is_ge, 0.0,
                                         base=0, channel_multiplier=-1).then_inc(caus_ready, 1)
                    for bb in BATCHES:
                        if not first:
                            wait_alone(pool, M.passed, uw_ready, nth(i, bb) - B)
                            wait_alone(pool, M.passed, o_used, nth(i, bb) - 2)
                        g_.tensor_tensor(heads(kt[:, par, bb], KD), heads(tile(M.k, i, bb), KD), each(M.kap, i, bb, KD), ALU.mult)
                        g_.tensor_tensor(R[:, bb, :, 0:VD], heads(tile(M.v, i, bb), VD), each(M.beta, i, bb, VD), ALU.mult)
                        g_.tensor_tensor(R[:, bb, :, VD:], heads(kb[:, bb], KD), each(M.gam, i, bb, KD), ALU.mult)\
                            .then_inc(scaled_r, 1)

                g_.memset(TTf[:], 0.0).then_inc(zeroed, 1)
                g_.memset(T64[:], 0.0).then_inc(zeroed, 1)
                g_.memset(Sd[:], 0.0).then_inc(zeroed, 1)
                pool.wait_ge(zeroed, 3)
                prep(0, 0, first=True)
                with pool.Fori(0, STEPS // 2 - 1) as j:
                    prep(j * 2 + 1, 1)
                    prep(j * 2 + 2, 0)
                prep(STEPS - 1, 1)

            @block.scalar
            def _(act):
                a_ = nc.scalar

                def stage(i):
                    for bb in BATCHES:
                        a_.activation(ks[:, bb], tile(M.k, i, bb), ACT.Copy)
                        a_.activation(qs[:, bb], tile(M.q, i, bb), ACT.Copy).then_inc(staged, 1)

                def decays(i, par, bb):
                    act.wait_ge(seg_ready, nth(i, bb))
                    a_.activation(flat(dec[:, bb]), psum[:, bb * 4 + 3, :], ACT.Exp).then_inc(dec_ready, 1)
                    act.wait_ge(km_ready, nth(i, bb))
                    a_.activation(flat(T3[:, par, bb]), psum[:, bb * 4 + 2, P:], ACT.Copy).then_inc(T3_ready, 1)

                def prep(i, par, ahead, before):
                    if ahead:
                        stage(i + 1)
                    if before:
                        outputs(i - 1)
                    for bb in BATCHES:
                        act.wait_ge(T_ready, (i * LEVELS + LEVELS - 1) * B + bb + 1)
                        for n in range(4):
                            a_.activation(TTf[rows(n), bb, :, rows(n)], TT[rows(n), bb], ACT.Copy)
                        for n in range(2):
                            ins = a_.activation(T64[rows(n), bb, :, rows(n)], T[rows(n), bb], ACT.Copy)
                        ins.then_inc(diag_ready, 1)
                        act.wait_ge(x2_ready, nth(i, bb))
                        a_.activation(X2[96:128, bb], bank(bb, 0, 32)[96:128], ACT.Copy).then_inc(X2b_ready, 1)
                    for bb in BATCHES:
                        act.wait_ge(y2_ready, nth(i, bb))
                        a_.activation(T64[32:64, bb, :, 0:32], bank(bb, 1, 32)[32:64], ACT.Copy, scale=-1.0)\
                            .then_inc(T64_ready, 1)
                        a_.activation(TTf[64:96, bb, :, 96:128], bank(bb, 1, 32, 256)[64:96], ACT.Copy, scale=-1.0)\
                            .then_inc(TTa_ready, 1)
                    for bb in BATCHES:
                        if ahead:
                            decays(i + 1, 1 - par, bb)
                        act.wait_ge(y3_ready, nth(i, bb))
                        a_.activation(TTf[0:64, bb, :, 64:128], bank(bb, 1, 64)[0:64], ACT.Copy, scale=-1.0)\
                            .then_inc(TTf_ready, 1)
                    for bb in BATCHES:
                        act.wait_ge(uw_ready, nth(i, bb))
                        a_.activation(Wn[:, bb], bank(bb, 0, VD + KD)[:, :, VD:], ACT.Copy).then_inc(Wn_ready, 1)
                    for bb in BATCHES:
                        act.wait_ge(wt_ready, nth(i, bb))
                        a_.activation(WT[:, par, bb], psum[:, bb * 4 + 1, 0:P], ACT.Copy).then_inc(WT_ready, 1)

                def outputs(i):
                    for bb in BATCHES:
                        act.wait_ge(o_ready, nth(i, bb))
                        a_.activation(tile(M.v, i, bb), psum[:, bb * 4 + 3, 0:VAL], ACT.Copy).then_inc(o_used, 1)

                stage(0)
                for bb in BATCHES:
                    decays(0, 0, bb)
                prep(0, 0, ahead=True, before=False)
                with act.Fori(0, STEPS // 2 - 1) as j:
                    prep(j * 2 + 1, 1, ahead=True, before=True)
                    prep(j * 2 + 2, 0, ahead=True, before=True)
                prep(STEPS - 1, 1, ahead=False, before=True)
                outputs(STEPS - 1)

            @block.vector
            def _(dve):
                v = nc.vector
                ch = Chain(dve, dve_chain, M.passed)

                def inverse(i, l, bb):
                    dve.wait_ge(x_ready, (i * (LEVELS - 1) + l - 1) * B + bb + 1)
                    v.tensor_tensor(X[:, bb], bank(bb, 0, 32), all_heads(M.level[:, l, :]), ALU.mult).then_inc(X_ready, 1)

                def update(i, l, bb):
                    dve.wait_ge(y_ready, (i * (LEVELS - 1) + l - 1) * B + bb + 1)
                    ch.link(v.tensor_tensor(T[:, bb], T[:, bb], bank(bb, 1, 32), ALU.subtract))
                    v.transpose(TT[:, bb], T[:, bb]).then_inc(T_ready, 1)

                def delta(i, par):
                    for bb in BATCHES:
                        dve.wait_ge(ws_ready, nth(i, bb))
                        v.tensor_tensor(Dl[:, bb], flat(Us[:, par, bb]), psum[:, bb * 4 + 2, 0:VAL], ALU.subtract)\
                            .then_inc(delta_ready, 1)

                def state(i):
                    for bb in BATCHES:
                        dve.wait_ge(s_ready, nth(i, bb))
                        ins = v.tensor_tensor(St[:, bb], psum[:, bb * 4 + 2, VAL:2 * VAL], M.bmask[:], ALU.mult)
                        ch.mark(ins)
                    dve.wait_ge(ch.sem, ch.base + ch.n)
                    for bb in BATCHES:
                        v.scalar_tensor_tensor(Sd[:, bb], Sd[:, bb], M.dec[:, bass.ds(bb * STEPS + i, 1)], St[:, bb],
                                               ALU.mult, ALU.add).then_inc(S_ready, 1)

                def mask_keys(i):
                    for bb in BATCHES:
                        dve.wait_ge(t4_ready, nth(i, bb))
                        v.tensor_tensor(km[:, bb], psum[:, bb * 4 + 2, 0:P].unsqueeze(1).to_broadcast([P, H, P]),
                                        M.hmask[:].unsqueeze(2).to_broadcast([P, H, P]), ALU.mult).then_inc(km_ready, 1)

                def prep(i, par, first=False, ahead=True):
                    for bb in BATCHES:
                        dve.wait_ge(kk_ready, nth(i, bb))
                        v.tensor_tensor(flat(Lt[:, bb]), psum[:, bb * 4, :], flat(dec[:, bb]), ALU.mult).then_inc(lt_ready, 1)
                    dve.wait_ge(lt_ready, nth(i, B - 1))
                    for bb in BATCHES:
                        for n in range(4):
                            ins = v.tensor_tensor(X[rows(n), bb], Lt[rows(n), bb, :, rows(n)],
                                                  M.pairs[rows(n)].unsqueeze(1).to_broadcast([32, H, 32]), ALU.mult)
                        ch.mark(ins)
                    dve.wait_ge(ch.sem, ch.base + ch.n)
                    for bb in BATCHES:
                        ins = v.tensor_tensor(TT[:, bb], all_heads(M.eye32[:]), X[:, bb], ALU.subtract)
                        ch.mark(ins)
                    dve.wait_ge(ch.sem, ch.base + ch.n)
                    for bb in BATCHES:
                        v.transpose(T[:, bb], TT[:, bb]).then_inc(T_ready, 1)
                    if not first:
                        delta(i - 1, 1 - par)
                    for bb in BATCHES:
                        dve.wait_ge(qk_ready, nth(i, bb))
                        dve.wait_ge(caus_ready, nth(i, bb))
                        if not first:
                            dve.wait_ge(o_used, nth(i, bb) - 2)
                        v.tensor_tensor(flat(At[:, par, bb]), psum[:, bb * 4 + 1, :], flat(caus[:, bb]), ALU.mult)\
                            .then_inc(at_ready, 1)
                    for l in range(1, LEVELS):
                        for bb in BATCHES:
                            inverse(i, l, bb)
                        for bb in BATCHES:
                            update(i, l, bb)
                        if l == 1 and not first:
                            state(i - 1)
                    for bb in BATCHES:
                        dve.wait_ge(x2_ready, nth(i, bb))
                        v.tensor_copy(X2[32:64, bb], bank(bb, 0, 32)[32:64]).then_inc(X2_ready, 1)
                    for bb in BATCHES:
                        dve.wait_ge(y2_ready, nth(i, bb))
                        v.tensor_scalar(TTf[0:32, bb, :, 32:64], bank(bb, 1, 32, 256)[0:32], -1.0, None, ALU.mult)\
                            .then_inc(TTd_ready, 1)
                    for bb in BATCHES:
                        dve.wait_ge(x3_ready, nth(i, bb))
                        v.tensor_copy(X3[64:128, bb], bank(bb, 0, 64)[64:128]).then_inc(X3_ready, 1)
                    if ahead:
                        mask_keys(i + 1)
                    for bb in BATCHES:
                        dve.wait_ge(Wn_ready, nth(i, bb))
                        v.tensor_copy(Us[:, par, bb], bank(bb, 0, VD + KD)[:, :, 0:VD]).then_inc(Us_ready, 1)
                    dve.wait_ge(Us_ready, nth(i, B - 1))

                PER = 2 * B + (LEVELS - 1) * B
                dve.wait_ge(zeroed, 3)
                dve.sem_inc(S_ready, B)
                dve.sem_inc(o_used, B)
                mask_keys(0)
                prep(0, 0, first=True)
                with dve.Fori(0, STEPS // 2 - 1) as j:
                    ch.turn(j, 2 * (PER + B))
                    prep(j * 2 + 1, 1)
                    prep(j * 2 + 2, 0)
                ch.leave(STEPS // 2 - 1)
                prep(STEPS - 1, 1, ahead=False)
                delta(STEPS - 1, 1)
                state(STEPS - 1)

            @block.tensor
            def _(pe):
                mm = nc.tensor.matmul
                alone = lambda s, n: wait_alone(pe, M.passed, s, n)

                def blocks(bb, out_bank, left, right):
                    for u in range(H):
                        for n in range(4):
                            ins = mm(bank(bb, out_bank, 32)[rows(n), u, :], left(u, rows(n)), right(u, rows(n)),
                                     start=True, stop=True)
                    return ins

                def recur_a(i, par):
                    for bb in BATCHES:
                        pe.wait_ge(WT_ready, nth(i, bb))
                        pe.wait_ge(S_ready, nth(i, bb))
                        mm(psum[:, bb * 4 + 2, 0:VAL], WT[:, par, bb, :], Sd[:, bb, :], start=True, stop=True)\
                            .then_inc(ws_ready, 1)
                        pe.wait_ge(o_used, nth(i, bb))
                        mm(psum[:, bb * 4 + 3, 0:VAL], T3[:, par, bb, 2, :], Sd[:, bb, :], start=True, stop=False,
                           skip_group_check=True)

                def recur_b(i, par):
                    for bb in BATCHES:
                        pe.wait_ge(delta_ready, nth(i, bb))
                        mm(psum[:, bb * 4 + 2, VAL:2 * VAL], kt[:, par, bb, :], Dl[:, bb, :], start=True, stop=True)\
                            .then_inc(s_ready, 1)
                        for h in range(H):
                            ins = mm(psum[:, bb * 4 + 3, h * VD:(h + 1) * VD], At[:, par, bb, h, :],
                                     Dl[:, bb, h * VD:(h + 1) * VD], start=False, stop=True, skip_group_check=True)
                        ins.then_inc(o_ready, 1)

                def turn(i, first=False):
                    for bb in BATCHES:
                        pe.wait_ge(staged, nth(i, bb))
                        pe.wait_ge(scaled, nth(i, bb))
                        if not first:
                            pe.wait_ge(S_ready, nth(i, bb) - B)
                            pe.wait_ge(o_used, nth(i, bb) - B)
                        for n, t in enumerate((ks, kb, qs, qg)):
                            ins = nc.tensor.transpose(psum[:, bb * 4 + 2, n * P:(n + 1) * P], t[:, bb, :], ident[:])
                        ins.then_inc(t4_ready, 1)
                        pe.wait_ge(gl_ready, nth(i, bb))
                        mm(psum[:, bb * 4 + 3, :], M.after[:], flat(gL[:, bb]), start=True, stop=True).then_inc(seg_ready, 1)

                def prep(i, par, first=False, ahead=True):
                    for bb in BATCHES:
                        if not first:
                            pe.wait_ge(Us_ready, nth(i, bb) - B)
                            pe.wait_ge(WT_ready, nth(i, bb) - B)
                        pe.wait_ge(T3_ready, nth(i, bb))
                        pe.wait_ge(dec_ready, nth(i, bb))
                        for h in range(H):
                            ins = mm(psum[:, bb * 4, h * P:(h + 1) * P], km[:, bb, h, :], T3[:, par, bb, 0, :],
                                     start=True, stop=True)
                        ins.then_inc(kk_ready, 1)
                    for bb in BATCHES:
                        for h in range(H):
                            ins = mm(psum[:, bb * 4 + 1, h * P:(h + 1) * P], km[:, bb, h, :], T3[:, par, bb, 1, :],
                                     start=True, stop=True)
                        ins.then_inc(qk_ready, 1)
                    if not first:
                        recur_a(i - 1, 1 - par)
                    for l in range(1, LEVELS):
                        for bb in BATCHES:
                            if l == 1:
                                alone(lt_ready, nth(i, bb))
                            alone(T_ready, (i * LEVELS + l - 1) * B + bb + 1)
                            blocks(bb, 0, lambda u, r: Lt[r, bb, u, r], lambda u, r: T[r, bb, u, :]).then_inc(x_ready, 1)
                        if l == 1 and not first:
                            recur_b(i - 1, 1 - par)
                        for bb in BATCHES:
                            if l == 1:
                                alone(at_ready, nth(i, bb))
                            alone(X_ready, (i * (LEVELS - 1) + l - 1) * B + bb + 1)
                            blocks(bb, 1, lambda u, r: TT[r, bb, u, :], lambda u, r: X[r, bb, u, :]).then_inc(y_ready, 1)
                    for bb in BATCHES:
                        alone(T_ready, (i * LEVELS + LEVELS - 1) * B + bb + 1)
                        for u in range(H):
                            for n in (0, 2):
                                ins = mm(bank(bb, 0, 32)[rows(n + 1), u, :], Lt[rows(n), bb, u, rows(n + 1)], T[rows(n), bb, u, :],
                                         start=True, stop=True)
                        ins.then_inc(x2_ready, 1)
                    for bb in BATCHES:
                        alone(X2_ready, nth(i, bb))
                        alone(X2b_ready, nth(i, bb))
                        for u in range(H):
                            mm(bank(bb, 1, 32)[32:64, u, :], TT[32:64, bb, u, :], X2[32:64, bb, u, :], start=True, stop=True)
                        for u in range(H):
                            for n in (0, 2):
                                ins = mm(bank(bb, 1, 32, 256)[rows(n), u, :], X2[rows(n + 1), bb, u, :],
                                         TT[rows(n + 1), bb, u, :], start=True, stop=True)
                        ins.then_inc(y2_ready, 1)
                    for bb in BATCHES:
                        for s in (T64_ready, diag_ready, TTa_ready, TTd_ready):
                            alone(s, nth(i, bb))
                        for u in range(H):
                            ins = mm(bank(bb, 0, 64)[64:128, u, :], Lt[0:64, bb, u, 64:128], T64[0:64, bb, u, :],
                                     start=True, stop=True)
                        ins.then_inc(x3_ready, 1)
                    if ahead:
                        turn(i + 1)
                    for bb in BATCHES:
                        alone(X3_ready, nth(i, bb))
                        for u in range(H):
                            ins = mm(bank(bb, 1, 64)[0:64, u, :], X3[64:128, bb, u, :], TTf[64:128, bb, u, 64:128],
                                     start=True, stop=True)
                        ins.then_inc(y3_ready, 1)
                    for bb in BATCHES:
                        pe.wait_ge(TTf_ready, nth(i, bb))
                        pe.wait_ge(scaled_r, nth(i, bb))
                        for u in range(H):
                            ins = mm(bank(bb, 0, VD + KD)[:, u, :], TTf[:, bb, u, :], R[:, bb, u, :], start=True, stop=True)
                        ins.then_inc(uw_ready, 1)
                    for bb in BATCHES:
                        pe.wait_ge(Wn_ready, nth(i, bb))
                        nc.tensor.transpose(psum[:, bb * 4 + 1, 0:P], flat(Wn[:, bb]), ident[:]).then_inc(wt_ready, 1)

                pe.wait_ge(zeroed, 3)
                turn(0, first=True)
                prep(0, 0, first=True)
                with pe.Fori(0, STEPS // 2 - 1) as j:
                    prep(j * 2 + 1, 1)
                    prep(j * 2 + 2, 0)
                prep(STEPS - 1, 1, ahead=False)
                recur_a(STEPS - 1, 1)
                recur_b(STEPS - 1, 1)


def delta_outputs(nc, X, ident, neg_half, psum, W, M):
    with ExitStack() as ctx:
        sb = lambda n, s, dt=F32: ctx.enter_context(nc.sbuf_tensor(f"out_{n}", s, dt))
        sem = Semaphores(ctx, nc, "out")
        sq, o1, gain = sb("sq", [P, GT, VAL]), sb("o1", [P, GT, VAL]), sb("gain", [P, 2, GT, VAL])
        ss, r, rt = sb("ss", [P, GT * H]), sb("r", [P, 2, GT * H]), sb("rt", [P, GT * H])
        nh, half = sb("nh", [P, GT * H]), sb("half", [P, GT * H])
        oT, hT = sb("oT", [P, 2, GW]), sb("hT", [P, GW])
        x1, y, z = sb("x1", [P, 2, GT, D]), sb("y", [P, GT, D]), sb("z", [P, GT, D])
        stats, mv = sb("stats", [P, GT, 6]), sb("mv", [P, GT, 2])
        r2, r2t = sb("r2", [P, GT]), sb("r2t", [P, GT])
        dve_chain, consts = sem("dve_chain"), sem("consts")
        (sq_ready, ss_ready, r_ready, gain_ready, o1_ready, ot_ready, oT_ready, enc_ready, mv_ready, r2_ready, yg_ready,
         y_ready, x_ready, ht_ready, hT_ready, z_ready, zb_ready, gelu_ready, x_done) = (sem(n) for n in (
            "sq_ready ss_ready r_ready gain_ready o1_ready ot_ready oT_ready enc_ready mv_ready r2_ready yg_ready "
            "y_ready x_ready ht_ready hT_ready z_ready zb_ready gelu_ready x_done").split())
        OT, ENC, HT, Z = (0, 1), (2, 3), 4, (5, 6)

        def tiles4(ap):
            return ap.unsqueeze(1).to_broadcast([P, GT, D])

        def by_head(ap):
            return ap.rearrange("p t (h v) -> p (t h) v", v=VD)

        def by_tile(ap):
            return ap.rearrange("p (t d) -> p t d", d=D)

        with nc.Block() as block:
            @block.vector
            def _(dve):
                v = nc.vector
                ch = Chain(dve, dve_chain, W.passed)

                def sums(g):
                    dve.wait_ge(sq_ready, g + 1)
                    v.tensor_reduce(ss[:], by_head(sq[:]), AX.X, ALU.add).then_inc(ss_ready, 1)

                def weigh(g, par, first=False):
                    dve.wait_ge(r_ready, g * 3 + 3)
                    if not first:
                        dve.wait_ge(ot_ready, g)
                    ch.link(v.tensor_tensor(by_head(o1[:]), by_head(M.v[:, bass.ts(g, GT), :]),
                                            r[:, par, :].unsqueeze(2).to_broadcast([P, GT * H, VD]), ALU.mult))
                    dve.wait_ge(gain_ready, g * 2 + 2)
                    v.tensor_tensor(o1[:], o1[:], gain[:, par], ALU.mult).then_inc(o1_ready, 1)

                def residual(g, par):
                    for t in range(GT):
                        tile = bass.ds(g * GT + t, 1)
                        ins = v.tensor_scalar(x1[:, par, t, :], X[:, tile, :].rearrange("p o d -> p (o d)"),
                                              M.mv[:, tile, 0:1].rearrange("p o d -> p (o d)"), M.rstd[:, tile],
                                              ALU.subtract, ALU.mult)
                    ch.link(ins)
                    dve.wait_ge(enc_ready, g + 1)
                    ch.link(v.tensor_tensor(x1[:, par], by_tile(psum[:, ENC[par], :]), x1[:, par], ALU.add))
                    row_stats(nc, ch, stats, mv, x1[:, par]).then_inc(mv_ready, 1)

                def normalize(g, par, first=False):
                    dve.wait_ge(r2_ready, g * 2 + 2)
                    if not first:
                        dve.wait_ge(ht_ready, g)
                    for t in range(GT):
                        ins = v.tensor_scalar(y[:, t, :], x1[:, par, t, :], mv[:, t, 0:1], r2[:, t:t + 1], ALU.subtract, ALU.mult)
                    ch.link(ins)
                    v.tensor_tensor(y[:], y[:], tiles4(M.ln2g[:]), ALU.mult).then_inc(yg_ready, 1)

                def bias(g, par):
                    dve.wait_ge(z_ready, g + 1)
                    v.tensor_tensor(z[:], by_tile(psum[:, Z[par], :]), tiles4(M.b2[:]), ALU.add).then_inc(zb_ready, 1)

                def final(g, par):
                    dve.wait_ge(x_ready, g + 1)
                    dve.wait_ge(gelu_ready, g + 1)
                    v.tensor_tensor(X[:, bass.ts(g, GT), :], x1[:, par], z[:], ALU.add).then_inc(x_done, 1)

                def step(g, par, first=False, ahead=2):
                    residual(g, par)
                    if not first:
                        bias(g - 1, 1 - par)
                    if ahead >= 1:
                        weigh(g + 1, 1 - par)
                    normalize(g, par, first)
                    if ahead >= 2:
                        sums(g + 2)
                    if not first:
                        final(g - 1, 1 - par)
                        dve.wait_ge(x_done, g)

                sums(0)
                dve.wait_ge(r_ready, 1)
                sums(1)
                weigh(0, 0, first=True)
                LINKS = 5
                step(0, 0, first=True)
                step(1, 1)
                with dve.Fori(1, GROUPS // 2 - 1) as j:
                    ch.turn(j - 1, 2 * LINKS)
                    step(j * 2, 0)
                    step(j * 2 + 1, 1)
                ch.leave(GROUPS // 2 - 2)
                step(GROUPS - 2, 0, ahead=1)
                step(GROUPS - 1, 1, ahead=0)
                bias(GROUPS - 1, 1)
                final(GROUPS - 1, 1)

            @block.gpsimd
            def _(pool):
                g_ = nc.gpsimd

                def deviation(g, par, first=False):
                    wait_alone(pool, W.passed, ss_ready, g + 1)
                    g_.tensor_scalar(rt[:], ss[:], 1.0 / VD, RMS_EPS, ALU.mult, ALU.add).then_inc(r_ready, 1)
                    wait_alone(pool, W.passed, r_ready, g * 3 + 1)
                    if not first:
                        wait_alone(pool, W.passed, o1_ready, g - 1)
                    g_.tensor_tensor(r[:, par, :], rt[:], nh[:], ALU.pow).then_inc(r_ready, 1)
                    wait_alone(pool, W.passed, r_ready, g * 3 + 2)
                    g_.tensor_tensor(r[:, par, :], r[:, par, :], half[:], ALU.mult).then_inc(r_ready, 1)

                def gains(g, par, first=False):
                    if not first:
                        wait_alone(pool, W.passed, o1_ready, g - 1)
                    for n in range(2):
                        tiles = bass.ds(g * GT + n * 2, 2)
                        g_.tensor_tensor(by_head(gain[:, par, 2 * n:2 * n + 2]), by_head(M.gate[:, tiles, :]),
                                         M.onw[:].unsqueeze(1).to_broadcast([P, GT * H // 2, VD]), ALU.mult)\
                            .then_inc(gain_ready, 1)

                def step(g, par, first=False, ahead=True):
                    wait_alone(pool, W.passed, mv_ready, g + 1)
                    if not first:
                        wait_alone(pool, W.passed, yg_ready, g)
                    inverse_root(nc, pool, W.passed, r2_ready, g * 2, r2[:], mv[:, :, 1], r2t[:], 1.0, LN_EPS, neg_half[:])
                    wait_alone(pool, W.passed, yg_ready, g + 1)
                    g_.tensor_tensor(y[:], y[:], tiles4(M.ln2b[:]), ALU.add).then_inc(y_ready, 1)
                    g_.tensor_tensor(x1[:, par], x1[:, par], X[:, bass.ts(g, GT), :], ALU.add).then_inc(x_ready, 1)
                    if ahead:
                        deviation(g + 2, par)
                        gains(g + 2, par)

                g_.memset(nh[:], -0.5).then_inc(consts, 1)
                g_.memset(half[:], 0.5).then_inc(consts, 1)
                pool.wait_ge(consts, 2)
                deviation(0, 0, first=True)
                gains(0, 0, first=True)
                deviation(1, 1, first=True)
                gains(1, 1, first=True)
                step(0, 0, first=True)
                step(1, 1)
                with pool.Fori(1, GROUPS // 2 - 1) as j:
                    step(j * 2, 0)
                    step(j * 2 + 1, 1)
                step(GROUPS - 2, 0, ahead=False)
                step(GROUPS - 1, 1, ahead=False)

            @block.scalar
            def _(act):
                def squares(g, first=False):
                    if not first:
                        act.wait_ge(ss_ready, g)
                    nc.scalar.activation(sq[:], M.v[:, bass.ts(g, GT), :], ACT.Square).then_inc(sq_ready, 1)

                def turned(g):
                    act.wait_ge(ot_ready, g + 1)
                    nc.scalar.activation(oT[:], psum[:, OT[0]:OT[1] + 1, :], ACT.Copy).then_inc(oT_ready, 1)

                def gelu(g):
                    act.wait_ge(zb_ready, g + 1)
                    nc.scalar.activation(z[:], z[:], ACT.Gelu).then_inc(gelu_ready, 1)

                def step(g, first=False, ahead=2):
                    if ahead >= 2:
                        squares(g + 2)
                    if ahead >= 1:
                        turned(g + 1)
                    if not first:
                        gelu(g - 1)
                    act.wait_ge(ht_ready, g + 1)
                    nc.scalar.activation(hT[:], psum[:, HT, :], ACT.Copy).then_inc(hT_ready, 1)

                squares(0, first=True)
                squares(1)
                turned(0)
                step(0, first=True)
                with act.Fori(1, GROUPS - 2) as g:
                    step(g)
                step(GROUPS - 2, ahead=1)
                step(GROUPS - 1, ahead=0)
                gelu(GROUPS - 1)

            @block.tensor
            def _(pe):
                def turn(g):
                    pe.wait_ge(o1_ready, g + 1)
                    for n in range(2):
                        for t in range(GT):
                            ins = nc.tensor.transpose(psum[:, OT[n], t * P:(t + 1) * P], o1[:, t, n * P:(n + 1) * P], ident[:])
                    ins.then_inc(ot_ready, 1)

                def encode(g, par, first=False):
                    pe.wait_ge(oT_ready, g + 1)
                    if not first:
                        pe.wait_ge(mv_ready, g - 1)
                    for t in range(GT):
                        for n in range(2):
                            ins = nc.tensor.matmul(psum[:, ENC[par], t * D:(t + 1) * D], oT[:, n, t * P:(t + 1) * P],
                                                   M.wo[:, n, :], start=(n == 0), stop=(n == 1))
                    ins.then_inc(enc_ready, 1)

                def step(g, par, ahead=True, first=False, second=False):
                    if ahead:
                        turn(g + 1)
                    pe.wait_ge(y_ready, g + 1)
                    for t in range(GT):
                        ins = nc.tensor.transpose(psum[:, HT, t * P:(t + 1) * P], y[:, t, :], ident[:])
                    ins.then_inc(ht_ready, 1)
                    if ahead:
                        encode(g + 1, 1 - par, first=first)
                    pe.wait_ge(hT_ready, g + 1)
                    if not (first or second):
                        pe.wait_ge(zb_ready, g - 1)
                    for t in range(GT):
                        ins = nc.tensor.matmul(psum[:, Z[par], t * D:(t + 1) * D], hT[:, t * P:(t + 1) * P], M.w2[:],
                                               start=True, stop=True)
                    ins.then_inc(z_ready, 1)

                turn(0)
                encode(0, 0, first=True)
                step(0, 0, first=True)
                step(1, 1, second=True)
                with pe.Fori(1, GROUPS // 2 - 1) as j:
                    step(j * 2, 0)
                    step(j * 2 + 1, 1)
                step(GROUPS - 2, 0)
                step(GROUPS - 1, 1, ahead=False)


def gated_delta(nc, X, ident, neg_half, psum, W, A):
    with ExitStack() as ctx:
        sb = lambda n, s, dt=F32: ctx.enter_context(nc.sbuf_tensor(f"gd_{n}", s, dt))
        M = Holder()
        M.passed = W.passed
        M.mv, M.rstd = W.mv, sb("rstd", [P, TILES])
        M.q, M.k = sb("q", [P, TILES, KEY]), sb("k", [P, TILES, KEY])
        M.v, M.gate = sb("v", [P, TILES, VAL]), sb("gate", [P, TILES, VAL])
        M.ab = sb("ab", [P, TILES, 2 * H])
        M.g, M.beta, M.gam, M.kap = (sb(n, [P, TILES, H]) for n in ("g", "beta", "gam", "kap"))
        M.dec = sb("dec", [P, TILES])
        M.wq, M.wk, M.wv, M.wg = sb("wq", [P, KEY]), sb("wk", [P, KEY]), sb("wv", [P, VAL]), sb("wg", [P, VAL])
        M.wab, M.wo, M.w2 = sb("wab", [P, 2 * H]), sb("wo", [P, 2, D]), sb("w2", [P, D])
        M.ln1g, M.ln1b, M.ln2g, M.ln2b, M.b2 = (sb(n, [P, D]) for n in ("ln1g", "ln1b", "ln2g", "ln2b", "b2"))
        M.rmsw, M.convw, M.onw = sb("rmsw", [P, 1]), sb("convw", [P, 4, CONV]), sb("onw", [P, VD])
        M.dtb, M.alog = sb("dtb", [P, H]), sb("alog", [P, H])
        consts = sb("masks", [P, MASK_COLS])
        M.upto, M.after, M.ones = (consts[:, n * P:(n + 1) * P] for n in range(3))
        M.bmask, M.hmask = consts[:, 384:640], consts[:, 640:644]
        M.eye32, M.level = consts[:, 644:676], consts[:, 676:836].rearrange("p (l k) -> p l k", k=32)
        M.pairs = consts[:, 836:868]
        a = lambda n: A[f"L1_attn_{n}"]
        row = lambda n: a(n).partition_broadcast(P)
        M.loads = [
            (M.wq[:], a("Wq")), (M.wk[:], a("Wk")), (M.wv[:], a("Wv")), (M.wg[:], a("Wg")),
            (M.wab[:, 0:H], a("Wa")), (M.wab[:, H:], a("Wb")), (M.wo[:], a("Wo").rearrange("(n p) d -> p n d", p=P)),
            (M.w2[:], a("W2")), (M.ln1g[:], row("ln1_g")), (M.ln1b[:], row("ln1_b")), (M.ln2g[:], row("ln2_g")),
            (M.ln2b[:], row("ln2_b")), (M.b2[:], row("b2")), (M.rmsw[:], a("rms_in_w").unsqueeze(1)),
            (M.convw[:, 0, :], a("conv_q_w")), (M.convw[:, 1, :], a("conv_k_w")),
            (M.convw[:, 2:4, :], a("conv_v_w").rearrange("(n p) i -> p n i", p=P)), (M.onw[:], row("o_norm_w")),
            (M.dtb[:], row("dt_bias")), (M.alog[:], row("A_log")), (consts[:], A["masks"]),
        ]
        M.n_loads = len(M.loads)
        delta_inputs(nc, X, ident, psum, W, M)
        delta_decays(nc, psum, M)
        delta_scan(nc, ident, psum, M)
        delta_outputs(nc, X, ident, neg_half, psum, W, M)


MASK_COLS = 3 * P + VAL + H + 7 * 32


def masks():
    import numpy as np
    r, c = np.arange(P)[:, None], np.arange(P)[None, :]
    upto, after, ones = r <= c, r > c, np.ones((P, P))
    bmask = (r // KD) == (np.arange(VAL)[None, :] // VD)
    hmask = (r // KD) == np.arange(H)[None, :]
    c32 = np.arange(32)[None, :]
    eye = (r % 32) == c32
    level = [(((r % 32) // n) % 2 == 1) & (c32 // n == (r % 32) // n - 1) for n in (1, 2, 4, 8, 16)]
    pairs = (c32 % 2 == 1) & ((r % 32) == c32 - 1)
    return np.concatenate([upto, after, ones, bmask, hmask, eye] + level + [pairs], axis=1).astype(np.float32)


WEIGHT_LOADS = 13


def build(nc, A, out):
    ctx = ExitStack()
    with ctx:
        sb = lambda n, s, dt=F32: ctx.enter_context(nc.sbuf_tensor(n, s, dt))
        sem = lambda n: ctx.enter_context(nc.semaphore(n))
        X = sb("X", [P, TILES, D])
        ident = sb("ident", [P, P])
        neg_half = sb("neg_half", [P, GT])
        psum = ctx.enter_context(nc.psum_tensor("psum", [P, 8, 512], F32))
        W = Holder()
        W.passed = sem("passed")
        W.mv = sb("mean_var", [P, TILES, 2])
        rw = sb("rw", [P, E])
        W.rb, W.rank = sb("rb", [P, E]), sb("rank", [P, E])
        gw = sb("gw", [P, E])
        W.gw, W.rw = gw, rw
        W.gb, W.b1T, W.b2T = sb("gb", [P, E]), sb("b1T", [P, E * FC]), sb("b2T", [P, E])
        b1T_ready = sem("b1T_ready")
        W.wqh, W.wkh, W.wql, W.wkl = (sb(n, [P, D], F32R) for n in ("wqh", "wkh", "wql", "wkl"))
        W.wv = sb("wv", [P, D])
        W.bq, W.bk, W.bvb = sb("bq", [P, 1]), sb("bk", [P, 1]), sb("bvb", [P, D])
        qkvT_ready = sem("qkvT_ready")
        x_loaded, w_loaded = sem("x_loaded"), sem("w_loaded")
        consts_ready, ident_zero = sem("consts_ready"), sem("ident_zero")
        w_high, w_low = sem("w_high"), sem("w_low")

        experts = ExitStack()
        W.ewh, W.ewl = (experts.enter_context(nc.sbuf_tensor(n, [P, E * D], F32R)) for n in ("ewh", "ewl"))

        A["coef_scratch"] = nc.dram_tensor("coef_scratch", (2, P, P), F32, kind="Internal").ap()
        x_dram = A["L0_attn_x"].rearrange("b (t p) d -> p (b t) d", p=P)
        with (nc.sbuf_tensor("ew", [P, E * D], F32) as ew, nc.sbuf_tensor("wraw", [P, 3, D], F32) as wraw,
              nc.sbuf_tensor("b1raw", [E * FC, P], F32) as b1raw, nc.sbuf_tensor("b2raw", [E, D], F32) as b2raw, nc.Block() as block):
            @block.sync
            def _(sp):
                for b in range(B):
                    tiles = slice(b * TILES // B, (b + 1) * TILES // B)
                    sp.dma_start(X[:, tiles, :], x_dram[:, tiles, :]).then_inc(x_loaded, 16)

            @block.gpsimd
            def _(pool):
                nc.gpsimd.memset(ident[:], 0.0).then_inc(ident_zero, 1)
                pool.wait_ge(ident_zero, 1)
                nc.gpsimd.affine_select(ident[:], ident[:], [[-1, P]], ALU.not_equal, 1.0, base=0,
                                        channel_multiplier=1).then_inc(consts_ready, 1)
                nc.gpsimd.memset(neg_half[:], -0.5).then_inc(consts_ready, 1)
                for e in range(E):
                    nc.gpsimd.memset(W.rank[:, e:e + 1], float(E - e)).then_inc(consts_ready, 1)
                pool.wait_ge(x_loaded, 16 * B)

            @block.scalar
            def _(act):
                act.dma_start(ew[:].rearrange("p (e d) -> p e d", d=D),
                             A["L0_ffn_expert_w"].rearrange("e h d -> h e d")).then_inc(w_loaded, 16)
                act.dma_start(rw[:], A["L0_ffn_router_w"]).then_inc(w_loaded, 16)
                act.dma_start(W.rb[:], A["L0_ffn_router_b"].partition_broadcast(P)).then_inc(w_loaded, 16)
                for n, w in enumerate(("wq", "wk", "wv")):
                    act.dma_start(wraw[:, n, :], A[f"L0_attn_{w}"]).then_inc(w_loaded, 16)
                act.dma_start(W.bq[:], A["L0_attn_bq"].unsqueeze(1)).then_inc(w_loaded, 16)
                act.dma_start(W.bk[:], A["L0_attn_bk"].unsqueeze(1)).then_inc(w_loaded, 16)
                act.dma_start(W.bvb[:], A["L0_attn_bv"].partition_broadcast(P)).then_inc(w_loaded, 16)
                act.dma_start(gw[:], A["L1_ffn_gate_w"]).then_inc(w_loaded, 16)
                act.dma_start(W.gb[:], A["L1_ffn_gate_b"].partition_broadcast(P)).then_inc(w_loaded, 16)
                act.dma_start(b1raw[:], A["L1_ffn_b1"].rearrange("e (c p) -> (e c) p", p=P)).then_inc(w_loaded, 16)
                act.dma_start(b2raw[:], A["L1_ffn_b2"]).then_inc(w_loaded, 16)
                act.wait_ge(w_loaded, 16 * WEIGHT_LOADS)
                nc.scalar.activation(W.ewh[:], ew[:], ACT.Copy).then_inc(w_high, 1)
                act.wait_ge(b1T_ready, 1)
                nc.scalar.activation(W.b1T[:], psum[:, 1, 0:E * FC], ACT.Copy)
                nc.scalar.activation(W.b2T[:], psum[:, 1, E * FC:E * FC + E], ACT.Copy)
                act.wait_ge(qkvT_ready, 1)
                for n, h in enumerate((W.wqh, W.wkh, W.wv)):
                    nc.scalar.activation(h[:], psum[:, 0, n * D:(n + 1) * D], ACT.Copy).then_inc(w_high, 1)

            @block.tensor
            def _(pe):
                pe.wait_ge(w_loaded, 16 * WEIGHT_LOADS)
                pe.wait_ge(consts_ready, 1)
                nc.tensor.transpose(psum[:, 1, 0:E * FC], b1raw[:], ident[0:E * FC, 0:E * FC])
                nc.tensor.transpose(psum[:, 1, E * FC:E * FC + E], b2raw[:], ident[0:E, 0:E]).then_inc(b1T_ready, 1)
                for n in range(3):
                    ins = nc.tensor.transpose(psum[:, 0, n * D:(n + 1) * D], wraw[:, n, :], ident[:])
                ins.then_inc(qkvT_ready, 1)

            @block.vector
            def _(dve):
                dve.wait_ge(w_high, 1)
                nc.vector.tensor_tensor(W.ewl[:], ew[:], W.ewh[:].bitcast(F32), ALU.subtract).then_inc(w_low, 1)
                dve.wait_ge(w_high, 4)
                for n, (h, l) in enumerate(((W.wqh, W.wql), (W.wkh, W.wkl))):
                    nc.vector.tensor_tensor(l[:], psum[:, 0, n * D:(n + 1) * D], h[:].bitcast(F32),
                                            ALU.subtract).then_inc(w_low, 1)

        first_mixture(nc, "mix1", X, ident, psum, W, A)
        attention(nc, "attn", X, ident, psum, W)
        first_mixture(nc, "mix2", X, ident, psum, W, A, known=True)
        experts.close()
        second_mixture(nc, "ffn3", X, ident, psum, W, A, None)
        gated_delta(nc, X, ident, neg_half, psum, W, A)
        second_mixture(nc, "ffn5", X, ident, psum, W, A, out)


_L1_ATTN = ["ln1_g", "ln1_b", "ln2_g", "ln2_b", "rms_in_w", "Wq", "Wk", "Wv", "conv_q_w", "conv_k_w", "conv_v_w",
            "Wa", "dt_bias", "A_log", "Wb", "Wg", "o_norm_w", "Wo", "W2", "b2"]
_INS = (["L0_attn_" + n for n in ("x", "wq", "bq", "wk", "bk", "wv", "bv")]
        + ["L0_ffn_" + n for n in ("router_w", "router_b", "expert_w", "expert_b")]
        + ["L1_attn_" + n for n in _L1_ATTN]
        + ["L1_ffn_" + n for n in ("gate_w", "gate_b", "w1", "b1", "w2", "b2")])


def kernel(**inputs):
    import numpy as _np
    import concourse.bacc as _bacc
    from concourse import mybir as _mybir
    from concourse.bass_utils import run_bass_kernel_spmd as _run

    nc = _bacc.Bacc("TRN2", target_bir_lowering=False, num_devices=1)
    arrays, access = {}, {}
    for name in _INS + ["masks"]:
        a = masks() if name == "masks" else _np.ascontiguousarray(inputs[name])
        arrays[f"in_{name}_dram"] = a
        access[name] = nc.dram_tensor(f"in_{name}_dram", a.shape, _mybir.dt.from_np(a.dtype),
                                      kind="ExternalInput").ap()
    out = nc.dram_tensor("out_0_dram", (B, S, D), _mybir.dt.float32, kind="ExternalOutput").ap()
    build(nc, access, out)
    r = _run(nc, [arrays], core_ids=[0])
    return r.results[0]["out_0_dram"]
```
